# Optimizing a Trainium2 kernel written in Bass

```python
import numpy as np
import jax
import jax.numpy as jnp

def _softmax(x, axis=-1):
    return jax.nn.softmax(x, axis=axis)

def _gelu(x):
    return jax.nn.gelu(x, approximate=True)

def _silu(x):
    return jax.nn.silu(x)

def _sigmoid(x):
    return jax.nn.sigmoid(x)

def _layernorm(x, axis=-1, eps=1e-05):
    m = jnp.mean(x, axis=axis, keepdims=True)
    v = jnp.var(x, axis=axis, keepdims=True)
    return (x - m) / jnp.sqrt(v + eps)

def _scatter_add(tgt, idx, src, axis=0):
    return tgt.at[idx].add(src)

def _segment_sum(src, seg, n):
    return jax.ops.segment_sum(src, seg, n)
kernel_name = 'mk_vit_tower_postln_d1_tok_img1024_r4_1adfb1'

def setup_inputs(seed: int=0):
    np.random.seed(seed)
    _w = jnp.asarray

    def _rec_inputs():
        import jax
        import jax.numpy as jnp
        _rk = jax.random.key(seed)
        x = -0.00016672 + 0.999947 * jax.random.normal(jax.random.fold_in(_rk, 1), (64, 3, 96, 96), jnp.float32)
        return x
    x = _rec_inputs()

    def _L0_tok_setup():
        import jax, jax.numpy as jnp
        import numpy as np
        B, C, H, W = (64, 3, 96, 96)
        P = 16
        NP = H // P * (W // P)
        PD = C * P * P
        ED = 256
        NCLS = 1

        def _layernorm(x, g, b, eps=1e-05):
            mu = jnp.mean(x, axis=-1, keepdims=True)
            var = jnp.mean(jnp.square(x - mu), axis=-1, keepdims=True)
            return (x - mu) * jax.lax.rsqrt(var + eps) * g + b
        key = jax.random.key(seed)
        ks = jax.random.split(key, 8)
        x = jax.random.normal(ks[0], (B, C, H, W), dtype=jnp.float32)
        ln1_g = jnp.ones((PD,), jnp.float32)
        ln1_b = jnp.zeros((PD,), jnp.float32)
        W_proj = jax.random.normal(ks[1], (PD, ED), jnp.float32) / np.sqrt(PD)
        b_proj = jnp.zeros((ED,), jnp.float32)
        ln2_g = jnp.ones((ED,), jnp.float32)
        ln2_b = jnp.zeros((ED,), jnp.float32)
        cls_token = jax.random.normal(ks[2], (1, NCLS, ED), jnp.float32)
        pos_emb = jax.random.normal(ks[3], (1, NP + NCLS, ED), jnp.float32)
        return {'x': x, 'ln1_g': ln1_g, 'ln1_b': ln1_b, 'W_proj': W_proj, 'b_proj': b_proj, 'ln2_g': ln2_g, 'ln2_b': ln2_b, 'cls_token': cls_token, 'pos_emb': pos_emb}
    _L0_tok_all = _L0_tok_setup()
    _L0_tok_in = {k: v for k, v in _L0_tok_all.items() if k in ('ln1_g', 'ln1_b', 'W_proj', 'b_proj', 'ln2_g', 'ln2_b', 'cls_token', 'pos_emb')}
    del _L0_tok_all

    def _L0_attn_setup():
        import jax, jax.numpy as jnp
        import numpy as np
        HIDDEN = 256
        HEADS = 16
        HEAD_DIM = HIDDEN // HEADS
        SCALE = HEAD_DIM ** (-0.5)
        key = jax.random.key(seed)
        ks = jax.random.split(key, 9)
        init = 1.0 / np.sqrt(HIDDEN)
        hidden_states = jax.random.normal(ks[0], (8, 256, HIDDEN), dtype=jnp.float32)

        def lin(k):
            kw, kb = jax.random.split(k)
            W = jax.random.uniform(kw, (HIDDEN, HIDDEN), jnp.float32, -init, init)
            b = jax.random.uniform(kb, (HIDDEN,), jnp.float32, -init, init)
            return (W, b)
        Wq, bq = lin(ks[1])
        Wk, bk = lin(ks[2])
        Wv, bv = lin(ks[3])
        Wo, bo = lin(ks[4])
        return {'hidden_states': hidden_states, 'Wq': Wq, 'bq': bq, 'Wk': Wk, 'bk': bk, 'Wv': Wv, 'bv': bv, 'Wo': Wo, 'bo': bo}
    _L0_attn_all = _L0_attn_setup()
    _L0_attn_in = {k: v for k, v in _L0_attn_all.items() if k in ('Wq', 'bq', 'Wk', 'bk', 'Wv', 'bv', 'Wo', 'bo')}
    del _L0_attn_all

    def _L0_ffn_setup():
        import jax, jax.numpy as jnp
        import numpy as np
        NUM_HEADS = 16
        TOP_K = 2
        key = jax.random.key(seed)
        ks = jax.random.split(key, 5)
        B, S, D, E = (4, 512, 256, 8)
        scale = 0.02
        return {'x': jax.random.normal(ks[0], (B, S, D), dtype=jnp.float32), 'W_qkv': jax.random.normal(ks[1], (D, 3 * D), dtype=jnp.float32) * scale, 'b_qkv': jnp.zeros((3 * D,), dtype=jnp.float32), 'W_gate': jax.random.normal(ks[2], (D, E), dtype=jnp.float32) * scale, 'b_gate': jnp.zeros((E,), dtype=jnp.float32), 'W_experts': jax.random.normal(ks[3], (E, D, D), dtype=jnp.float32) * scale, 'b_experts': jnp.zeros((E, D), dtype=jnp.float32)}
    _L0_ffn_all = _L0_ffn_setup()
    _L0_ffn_in = {k: v for k, v in _L0_ffn_all.items() if k in ('W_qkv', 'b_qkv', 'W_gate', 'b_gate', 'W_experts', 'b_experts')}
    del _L0_ffn_all
    return {'x': x, 'L0_tok_ln1_g': _L0_tok_in['ln1_g'], 'L0_tok_ln1_b': _L0_tok_in['ln1_b'], 'L0_tok_W_proj': _L0_tok_in['W_proj'], 'L0_tok_b_proj': _L0_tok_in['b_proj'], 'L0_tok_ln2_g': _L0_tok_in['ln2_g'], 'L0_tok_ln2_b': _L0_tok_in['ln2_b'], 'L0_tok_cls_token': _L0_tok_in['cls_token'], 'L0_tok_pos_emb': _L0_tok_in['pos_emb'], 'L0_attn_Wq': _L0_attn_in['Wq'], 'L0_attn_bq': _L0_attn_in['bq'], 'L0_attn_Wk': _L0_attn_in['Wk'], 'L0_attn_bk': _L0_attn_in['bk'], 'L0_attn_Wv': _L0_attn_in['Wv'], 'L0_attn_bv': _L0_attn_in['bv'], 'L0_attn_Wo': _L0_attn_in['Wo'], 'L0_attn_bo': _L0_attn_in['bo'], 'L0_ffn_W_qkv': _L0_ffn_in['W_qkv'], 'L0_ffn_b_qkv': _L0_ffn_in['b_qkv'], 'L0_ffn_W_gate': _L0_ffn_in['W_gate'], 'L0_ffn_b_gate': _L0_ffn_in['b_gate'], 'L0_ffn_W_experts': _L0_ffn_in['W_experts'], 'L0_ffn_b_experts': _L0_ffn_in['b_experts']}

def reference(x, L0_tok_ln1_g, L0_tok_ln1_b, L0_tok_W_proj, L0_tok_b_proj, L0_tok_ln2_g, L0_tok_ln2_b, L0_tok_cls_token, L0_tok_pos_emb, L0_attn_Wq, L0_attn_bq, L0_attn_Wk, L0_attn_bk, L0_attn_Wv, L0_attn_bv, L0_attn_Wo, L0_attn_bo, L0_ffn_W_qkv, L0_ffn_b_qkv, L0_ffn_W_gate, L0_ffn_b_gate, L0_ffn_W_experts, L0_ffn_b_experts):
    import jax
    import jax.numpy as jnp

    def _L0_tok_ref(x, ln1_g, ln1_b, W_proj, b_proj, ln2_g, ln2_b, cls_token, pos_emb):
        import jax, jax.numpy as jnp
        import numpy as np
        B, C, H, W = (64, 3, 96, 96)
        P = 16
        NP = H // P * (W // P)
        PD = C * P * P
        ED = 256
        NCLS = 1

        def _layernorm(x, g, b, eps=1e-05):
            mu = jnp.mean(x, axis=-1, keepdims=True)
            var = jnp.mean(jnp.square(x - mu), axis=-1, keepdims=True)
            return (x - mu) * jax.lax.rsqrt(var + eps) * g + b
        b = x.shape[0]
        h, w = (H // P, W // P)
        patches = x.reshape(b, C, h, P, w, P)
        patches = patches.transpose(0, 2, 4, 3, 5, 1).reshape(b, h * w, P * P * C)
        z = _layernorm(patches, ln1_g, ln1_b)
        z = jnp.einsum('bnp,pe->bne', z, W_proj) + b_proj
        z = _layernorm(z, ln2_g, ln2_b)
        cls = jnp.broadcast_to(cls_token, (b, NCLS, ED))
        z = jnp.concatenate([cls, z], axis=1)
        z = z + pos_emb
        return z

    def _L0_attn_ref(hidden_states, Wq, bq, Wk, bk, Wv, bv, Wo, bo):
        import jax, jax.numpy as jnp
        import numpy as np
        HIDDEN = 256
        HEADS = 16
        HEAD_DIM = HIDDEN // HEADS
        SCALE = HEAD_DIM ** (-0.5)
        b, s, d = hidden_states.shape
        q = (hidden_states @ Wq.T + bq).reshape(b, s, HEADS, HEAD_DIM)
        k = (hidden_states @ Wk.T + bk).reshape(b, s, HEADS, HEAD_DIM)
        v = (hidden_states @ Wv.T + bv).reshape(b, s, HEADS, HEAD_DIM)
        q = q * SCALE
        scores = jnp.einsum('bqhd,bkhd->bhqk', q, k)
        probs = jax.nn.softmax(scores.astype(jnp.float32), axis=-1).astype(scores.dtype)
        out = jnp.einsum('bhqk,bkhd->bqhd', probs, v).reshape(b, s, d)
        return out @ Wo.T + bo

    def _L0_ffn_ref(x, W_qkv, b_qkv, W_gate, b_gate, W_experts, b_experts):
        import jax, jax.numpy as jnp
        import numpy as np
        NUM_HEADS = 16
        TOP_K = 2
        B, S, D = x.shape
        H = NUM_HEADS
        hd = D // H
        E = W_gate.shape[-1]
        qkv = (x @ W_qkv + b_qkv).reshape(B, S, 3, H, hd)
        q, k, v = (qkv[:, :, 0], qkv[:, :, 1], qkv[:, :, 2])
        attn = jnp.einsum('bqhd,bkhd->bhqk', q, k) / jnp.sqrt(jnp.asarray(hd, x.dtype))
        attn = jax.nn.softmax(attn, axis=-1)
        attn_out = jnp.einsum('bhqk,bkhd->bqhd', attn, v).reshape(B, S, D)
        gate = jax.nn.softmax(x @ W_gate + b_gate, axis=-1)
        top_g, top_i = jax.lax.top_k(gate, TOP_K)
        combine = jnp.sum(jax.nn.one_hot(top_i, E, dtype=x.dtype) * top_g[..., None], axis=2)
        expert_out = jnp.einsum('bsd,edf->bsef', x, W_experts) + b_experts
        moe_out = jnp.einsum('bsef,bse->bsf', expert_out, combine)
        return attn_out + moe_out
    h = _L0_tok_ref(x, L0_tok_ln1_g, L0_tok_ln1_b, L0_tok_W_proj, L0_tok_b_proj, L0_tok_ln2_g, L0_tok_ln2_b, L0_tok_cls_token, L0_tok_pos_emb)
    h = _layernorm(h + _L0_attn_ref(h, L0_attn_Wq, L0_attn_bq, L0_attn_Wk, L0_attn_bk, L0_attn_Wv, L0_attn_bv, L0_attn_Wo, L0_attn_bo), axis=-1)
    h = _layernorm(h + _L0_ffn_ref(h, L0_ffn_W_qkv, L0_ffn_b_qkv, L0_ffn_W_gate, L0_ffn_b_gate, L0_ffn_W_experts, L0_ffn_b_experts), axis=-1)
    return h

_drawn_inputs = setup_inputs


def setup_inputs(seed=0):
    import zlib

    import numpy as np

    out = dict(_drawn_inputs(seed))
    spreads = {'L0_tok_ln1_g': (1.0, 0.2),
     'L0_tok_ln1_b': (0.0, 0.1),
     'L0_tok_b_proj': (0.0, 0.1),
     'L0_tok_ln2_g': (1.0, 0.2),
     'L0_tok_ln2_b': (0.0, 0.1),
     'L0_ffn_b_qkv': (0.0, 0.1),
     'L0_ffn_b_gate': (0.0, 0.1),
     'L0_ffn_b_experts': (0.0, 0.332)}
    factors = {'L0_attn_bq': 23.068, 'L0_attn_bk': 64.0, 'L0_attn_bv': 3.222}
    for name, (base, spread) in spreads.items():
        noise = np.random.default_rng([zlib.crc32(name.encode()), seed]).standard_normal(out[name].shape)
        drawn = base * np.exp(spread * noise) if base else spread * noise
        out[name] = jnp.asarray(drawn.astype(out[name].dtype))
    for name, factor in factors.items():
        out[name] = (out[name] * factor).astype(out[name].dtype)
    return out
```

```python
from contextlib import ExitStack, contextmanager

import concourse.bass as bass
from concourse import mybir

F32 = mybir.dt.float32
F32R = mybir.dt.float32r
U32 = mybir.dt.uint32
ALU = mybir.AluOpType
ACT = mybir.ActivationFunctionType
AX = mybir.AxisListType

P = 128
B, CH, IMG = 64, 3, 96
PATCH = 16
GRID = IMG // PATCH
D = 256
DC = D // P
HEADS, HD = 16, 16
E = 8
EPS = 1e-5
NPOS = GRID * GRID + 1
NPT = GRID * GRID // 2
NT = NPT + 1
NTOK = NPOS * B
HP = GRID // 2
ROWPIX = PATCH * IMG
FC = CH * PATCH * PATCH // P

IG = 8
GC = IG * NPOS
HC = HEADS // DC
UNITS = B // 2 * DC
KEYROWS = 3 * NPOS
VW = HD + 1
QPAD = 64


@contextmanager
def phase(nc):
    taken = []
    with ExitStack() as ctx:
        yield ctx, taken
    nc.clear_and_free_semaphores(taken)
    nc.all_engine_barrier()


def ds(start, size):
    return bass.ds(start, size)


def wait(eng, sem, value):
    if not isinstance(value, int) or value > 0:
        eng.wait_ge(sem, value)


def alone(eng, sem):
    eng.sem_inc(sem, 1)


def live(i, per, l, total):
    return 0 <= i * per + l < total if isinstance(i, int) else True


def rounds(eng, trips, per, tail, step):
    for l in range(per):
        step(0, l)
    with eng.Fori(1, trips) as i:
        for l in range(per):
            step(i, l)
    for l in range(tail):
        step(trips, l)


def rows_of(i, l, per=GRID):
    return B if isinstance(i, int) and i * per + l == NT - 1 else P


def patch_tokens(nc, a, keep):
    h, hT_hi, hT_lo, ps = keep["h"], keep["hT_hi"], keep["hT_lo"], keep["ps"]
    wqkv_hi, wqkv_lo, wo_hi, wo_lo = keep["wqkv_hi"], keep["wqkv_lo"], keep["wo_hi"], keep["wo_lo"]
    ident, bias_col = keep["ident"], keep["bias_col"]
    with phase(nc) as (ctx, taken):
        def sb(name, shape, dt=F32):
            return ctx.enter_context(nc.sbuf_tensor(name, shape, dt))

        def sem(name):
            taken.append(nc.alloc_semaphore(name))
            return taken[-1]

        xs = sb("xs", [P, HP, CH, ROWPIX])
        xn = sb("xn", [P, 2, CH * PATCH * PATCH])
        xT = sb("xT", [P, 2, FC * P])
        zs = sb("zs", [P, 2, D])
        t1 = sb("t1", [P, 2, D])
        hn = sb("hn", [P, 2, D])
        hraw = sb("hraw", [P, 2, D])
        hcls = sb("hcls", [B, 2, D])
        hcls_sum = sb("hcls_sum", [B, D])
        w_raw = sb("w_raw", [P, 4, DC, D])
        wp = sb("wp", [P, 2, CH, D])
        wpg = sb("wpg", [P, 2, CH, D])
        rows12 = sb("rows12", [12, P])
        rows4 = sb("rows4", [4, FC * P // 2])
        gcol = sb("gcol", [P, CH, 4])
        bmat = sb("bmat", [P, FC, P])
        bp_row = sb("bp_row", [P, D])
        zbias = sb("zbias", [P, D])
        g2_row = sb("g2_row", [P, D])
        b2_row = sb("b2_row", [P, D])
        bo_row = sb("bo_row", [P, D])
        stat = sb("stat", [P, 2, CH * 6])
        mv = sb("mv", [P, 2, 2])
        ve = sb("ve", [P, 2])
        sd = sb("sd", [P, 2])
        rstd = sb("rstd", [P, 2])
        nmu = sb("nmu", [P, 2])
        stat2 = sb("stat2", [P, 2, 6])
        mv2 = sb("mv2", [P, 2, 2])
        ve2 = sb("ve2", [P, 2])
        sd2 = sb("sd2", [P, 2])
        rstd2 = sb("rstd2", [P, 2])

        in_x = [sem(f"in_x{r}") for r in range(HP)]
        in_pos, in_cls, in_rows, in_b, in_w, in_wp = map(sem, ("in_pos", "in_cls", "in_rows", "in_b", "in_w", "in_wp"))
        ident_zero, ident_made, cols_ps, cols_sb = map(sem, ("ident_zero", "ident_made", "cols_ps", "cols_sb"))
        wT_ps, wT_hi, wT_lo, bmat_made, zb_ps, zb_made, gain_made = map(
            sem, ("wT_ps", "wT_hi", "wT_lo", "bmat_made", "zb_ps", "zb_made", "gain_made"))
        table_made, cls_made, cls_ps, cls_raw, cls_hi, cls_out = map(
            sem, ("table_made", "cls_made", "cls_ps", "cls_raw", "cls_hi", "cls_out"))
        carried = sem("carried")
        statd, aggr, vard, sdev, rsd, nmud, xnd, xT_ps, xTd = map(
            sem, ("statd", "aggr", "vard", "sdev", "rsd", "nmud", "xnd", "xT_ps", "xTd"))
        z_ps, zsd, stat2d, aggr2, var2, sdev2, rsd2, t1d, hnd, h_ps, hrawd, hhi, hlo, hres = map(
            sem, ("z_ps", "zsd", "stat2d", "aggr2", "var2", "sdev2", "rsd2", "t1d", "hnd", "h_ps", "hrawd",
                  "hhi", "hlo", "hres"))

        def xT_bank(r):
            return ps[:, 1024 * r:1024 * r + FC * P]

        def z_bank(r):
            return ps[:, 2048 + 512 * r:2048 + 512 * r + D]

        def h_bank(r):
            return ps[:, 3072 + 512 * r:3072 + 512 * r + D]

        block = ctx.enter_context(nc.Block())

        @block.sync
        def _(sp):
            for hp in range(HP):
                for c in range(CH):
                    for h2 in range(2):
                        r0 = PATCH * (2 * hp + h2)
                        sp.dma_start(xs[B * h2:B * h2 + B, hp, c, :],
                                     a["x"][:, c, r0:r0 + PATCH, :].rearrange("b r q -> b (r q)")).then_inc(in_x[hp], 16)

        @block.gpsimd
        def _(pool):
            pool.memset(ident[:, :], 0.0).then_inc(ident_zero, 1)
            pool.wait_ge(ident_zero, 1)
            pool.affine_select(out=ident[:, :], in_=ident[:, :], compare_op=ALU.not_equal, fill=1.0,
                               base=0, pattern=[[-1, P]], channel_multiplier=1).then_inc(ident_made, 1)
            pool.wait_ge(cols_sb, 2)
            pool.wait_ge(in_wp, 16)
            for half in range(2):
                for c in range(CH):
                    pool.tensor_scalar(wpg[:, half, c, :], wp[:, half, c, :], gcol[:, c, half:half + 1], 1.0,
                                       ALU.mult, ALU.mult).then_inc(gain_made, 1)
            pool.wait_ge(in_rows, 64)
            pool.wait_ge(in_pos, 96)
            for hp in range(HP):
                part = h[:, hp * GRID * D:(hp + 1) * GRID * D].rearrange("p (w d) -> p w d", d=D)
                pool.tensor_tensor(part, part, b2_row[:, :].unsqueeze(1).to_broadcast([P, GRID, D]),
                                   ALU.add).then_inc(table_made, 1)
            pool.wait_ge(cls_made, 1)
            pool.tensor_tensor(h[0:B, NPT * D:NT * D], hcls_sum[:, :], bo_row[0:B, :], ALU.add).then_inc(cls_out, 1)
            pool.wait_ge(cls_raw, 1)
            pool.wait_ge(cls_hi, 1)
            pool.tensor_tensor(hT_lo[:, :, NPT * P:NTOK],
                               hraw[:, 0, 0:DC * B].rearrange("p (c b) -> p c b", c=DC),
                               hT_hi[:, :, NPT * P:NTOK].bitcast(F32), ALU.subtract).then_inc(cls_out, 1)

            def step(i, l):
                if live(i, GRID, l - 4, NPT):
                    r, n = (l - 4) % 2, i * GRID + (l - 4)
                    wait(pool, hnd, n + 1)
                    pool.tensor_tensor(h[:, ds(n * D, D)], hn[:, r, :], bo_row[:, :], ALU.add).then_inc(hres, 1)
                if live(i, GRID, l - 5, NPT):
                    r, n = (l - 5) % 2, i * GRID + (l - 5)
                    wait(pool, hrawd, n + 1)
                    wait(pool, hhi, n + 1)
                    pool.tensor_tensor(hT_lo[:, :, ds(n * P, P)], hraw[:, r, :].rearrange("p (c t) -> p c t", c=DC),
                                       hT_hi[:, :, ds(n * P, P)].bitcast(F32), ALU.subtract).then_inc(hlo, 1)

            rounds(pool, HP, GRID, 5, step)

        @block.scalar
        def _(act):
            act.dma_start(rows12[0:2, :], a["bq"].rearrange("(c p) -> c p", p=P)).then_inc(in_b, 16)
            act.dma_start(rows12[2:4, :], a["bk"].rearrange("(c p) -> c p", p=P)).then_inc(in_b, 16)
            act.dma_start(rows12[4:6, :], a["bv"].rearrange("(c p) -> c p", p=P)).then_inc(in_b, 16)
            act.dma_start(rows12[6:12, :], a["b_qkv"].rearrange("(c p) -> c p", p=P)).then_inc(in_b, 16)
            act.dma_start(rows4[0:2, :], a["ln1_g"].rearrange("(h f) -> h f", h=2)).then_inc(in_b, 16)
            act.dma_start(rows4[2:4, :], a["ln1_b"].rearrange("(h f) -> h f", h=2)).then_inc(in_b, 16)
            for j, name in enumerate(("wq", "wk", "wv", "wo")):
                act.dma_start(w_raw[:, j, :, :], a[name].rearrange("(c p) n -> p c n", p=P)).then_inc(in_w, 16)
            act.dma_start(wp[:, :, :, :],
                          a["w_proj"].rearrange("(h p c) n -> p h (c n)", h=2, c=CH).rearrange(
                              "p h (c n) -> p h c n", c=CH)).then_inc(in_wp, 16)
            for row, name in ((bp_row, "b_proj"), (g2_row, "ln2_g"), (b2_row, "ln2_b"), (bo_row, "bo")):
                act.dma_start(row[:, :], a[name].partition_broadcast(P)).then_inc(in_rows, 16)
            for hp in range(HP):
                for h2 in range(2):
                    s = 1 + 2 * GRID * hp + GRID * h2
                    act.dma_start(h[B * h2:B * h2 + B, hp * GRID * D:(hp + 1) * GRID * D],
                                  a["pos"][0, s:s + GRID, :].rearrange("s d -> (s d)").partition_broadcast(B)
                                  ).then_inc(in_pos, 16)
            act.dma_start(hcls[:, 0, :], a["pos"][0, 0, :].partition_broadcast(B)).then_inc(in_cls, 16)
            act.dma_start(hcls[:, 1, :], a["cls"][0, 0, :].partition_broadcast(B)).then_inc(in_cls, 16)
            for j in range(4):
                for ic in range(DC):
                    n = DC * j + ic
                    act.wait_ge(wT_ps, n + 1)
                    dst = wo_hi[:, ic, :] if j == 3 else wqkv_hi[:, ic, j * D:(j + 1) * D]
                    act.activation(dst, ps[:, 2048 + 512 * (n % 4):2048 + 512 * (n % 4) + D], ACT.Copy).then_inc(wT_hi, 1)
            act.wait_ge(cls_ps, 1)
            act.activation(hraw[:, 0, 0:DC * B], h_bank(0)[:, 0:DC * B], ACT.Copy).then_inc(cls_raw, 1)
            act.activation(hT_hi[:, :, NPT * P:NTOK], h_bank(0)[:, 0:DC * B].rearrange("p (c b) -> p c b", c=DC),
                           ACT.Copy).then_inc(cls_hi, 1)

            def step(i, l):
                if live(i, GRID, l - 2, NPT):
                    r, n = (l - 2) % 2, i * GRID + (l - 2)
                    wait(act, xT_ps, n + 1)
                    wait(act, z_ps, n - 1)
                    act.activation(xT[:, r, :], xT_bank(r), ACT.Copy).then_inc(xTd, 1)
                if live(i, GRID, l - 1, NPT):
                    r, n = (l - 1) % 2, i * GRID + (l - 1)
                    hp, w = i + (l - 1) // GRID, (l - 1) % GRID
                    wait(act, rsd, n + 1)
                    wait(act, nmud, n + 1)
                    wait(act, xT_ps, n - 1)
                    src = xs[:, ds(hp, 1), :, :].rearrange("p o c (y w q) -> p (o c) y w q", w=GRID, q=PATCH)
                    act.activation(xn[:, r, :].rearrange("p (c y q) -> p c y q", c=CH, q=PATCH), src[:, :, :, w, :],
                                   ACT.Identity, bias=nmu[:, r:r + 1], scale=rstd[:, r:r + 1]).then_inc(xnd, 1)
                if live(i, GRID, l, NPT):
                    r, n = l % 2, i * GRID + l
                    wait(act, vard, n + 1)
                    wait(act, rsd, n - 1)
                    act.activation(sd[:, r:r + 1], ve[:, r:r + 1], ACT.Sqrt).then_inc(sdev, 1)
                if live(i, GRID, l - 3, NPT):
                    r, n = (l - 3) % 2, i * GRID + (l - 3)
                    wait(act, var2, n + 1)
                    wait(act, rsd2, n - 1)
                    act.activation(sd2[:, r:r + 1], ve2[:, r:r + 1], ACT.Sqrt).then_inc(sdev2, 1)
                if live(i, GRID, l - 5, NPT):
                    r, n = (l - 5) % 2, i * GRID + (l - 5)
                    wait(act, h_ps, n + 1)
                    wait(act, hlo, n - 1)
                    wait(act, cls_out, 2)
                    act.activation(hraw[:, r, :], h_bank(r), ACT.Copy).then_inc(hrawd, 1)
                    act.activation(hT_hi[:, :, ds(n * P, P)], h_bank(r).rearrange("p (c t) -> p c t", c=DC),
                                   ACT.Copy).then_inc(hhi, 1)

            rounds(act, HP, GRID, 5, step)

        @block.tensor
        def _(pe):
            pe.wait_ge(ident_made, 1)
            pe.wait_ge(in_b, 96)
            pe.transpose(ps[:, 3584:3596], rows12[:, :], ident[0:12, 0:12])
            for c in range(CH):
                last = pe.transpose(ps[:, 3600 + 4 * c:3604 + 4 * c], rows4[:, c:FC * P // 2:CH], ident[0:4, 0:4])
            last.then_inc(cols_ps, 1)
            pe.wait_ge(in_w, 64)
            for j in range(4):
                for ic in range(DC):
                    n = DC * j + ic
                    if n == 3:
                        pe.wait_ge(cols_sb, 2)
                    wait(pe, wT_hi, n - 3)
                    wait(pe, wT_lo, n - 3)
                    for oc in range(DC):
                        o = 2048 + 512 * (n % 4) + P * oc
                        last = pe.transpose(ps[:, o:o + P], w_raw[:, j, oc, ic * P:(ic + 1) * P], ident[:, :])
                    last.then_inc(wT_ps, 1)
            pe.wait_ge(bmat_made, FC)
            pe.wait_ge(in_wp, 16)
            for f in range(FC):
                last = pe.matmul(ps[:, 0:D], bmat[:, f, :], wp[:, f // CH, f % CH, :], start=(f == 0), stop=(f == FC - 1))
            last.then_inc(zb_ps, 1)
            pe.wait_ge(cls_made, 1)
            pe.wait_ge(wT_lo, 8)
            pe.wait_ge(wT_hi, 8)
            for c in range(DC):
                last = pe.transpose(h_bank(0)[:, c * B:(c + 1) * B], hcls_sum[:, c * P:(c + 1) * P], ident[0:B, 0:B])
            last.then_inc(cls_ps, 1)
            pe.wait_ge(gain_made, FC)
            pe.wait_ge(zb_made, 1)

            def step(i, l):
                if live(i, GRID, l - 1, NPT):
                    r, n = (l - 1) % 2, i * GRID + (l - 1)
                    wait(pe, xnd, n + 1)
                    wait(pe, xTd, n - 1)
                    for f in range(FC):
                        last = pe.transpose(xT_bank(r)[:, f * P:(f + 1) * P], xn[:, r, f * P:(f + 1) * P], ident[:, :])
                    last.then_inc(xT_ps, 1)
                if live(i, GRID, l - 2, NPT):
                    r, n = (l - 2) % 2, i * GRID + (l - 2)
                    wait(pe, xTd, n + 1)
                    wait(pe, zsd, n - 1)
                    for f in range(FC):
                        last = pe.matmul(z_bank(r), xT[:, r, f * P:(f + 1) * P], wpg[:, f % 2, f // 2, :],
                                         start=(f == 0), stop=(f == FC - 1))
                    last.then_inc(z_ps, 1)
                if live(i, GRID, l - 4, NPT):
                    r, n = (l - 4) % 2, i * GRID + (l - 4)
                    wait(pe, hnd, n + 1)
                    wait(pe, hhi, n - 1)
                    wait(pe, cls_hi, 1)
                    for c in range(DC):
                        last = pe.transpose(h_bank(r)[:, c * P:(c + 1) * P], hn[:, r, c * P:(c + 1) * P], ident[:, :])
                    last.then_inc(h_ps, 1)

            rounds(pe, HP, GRID, 5, step)

        @block.vector
        def _(dve):
            dve.wait_ge(cols_ps, 1)
            dve.tensor_copy(bias_col[:, :], ps[:, 3584:3596]).then_inc(cols_sb, 1)
            dve.tensor_copy(gcol[:, :, :], ps[:, 3600:3612].rearrange("p (c f) -> p c f", f=4)).then_inc(cols_sb, 1)
            dve.wait_ge(cols_sb, 2)
            for f in range(FC):
                dve.tensor_copy(bmat[:, f, :], gcol[:, f % CH, 2 + f // CH:3 + f // CH].to_broadcast([P, P])
                                ).then_inc(bmat_made, 1)
            dve.wait_ge(in_cls, 32)
            dve.tensor_tensor(hcls_sum[:, :], hcls[:, 0, :], hcls[:, 1, :], ALU.add).then_inc(cls_made, 1)
            for j in range(4):
                for ic in range(DC):
                    n = DC * j + ic
                    hi, lo = ((wo_hi[:, ic, :], wo_lo[:, ic, :]) if j == 3 else
                              (wqkv_hi[:, ic, j * D:(j + 1) * D], wqkv_lo[:, ic, j * D:(j + 1) * D]))
                    dve.wait_ge(wT_hi, n + 1)
                    dve.tensor_tensor(lo, ps[:, 2048 + 512 * (n % 4):2048 + 512 * (n % 4) + D], hi.bitcast(F32),
                                      ALU.subtract).then_inc(wT_lo, 1)
            dve.wait_ge(zb_ps, 1)
            dve.wait_ge(in_rows, 64)
            dve.tensor_tensor(zbias[:, :], ps[:, 0:D], bp_row[:, :], ALU.add).then_inc(zb_made, 1)
            dve.wait_ge(zb_made, 1)
            dve.wait_ge(table_made, HP)

            def step(i, l):
                if live(i, GRID, l, NPT):
                    r, n = l % 2, i * GRID + l
                    if isinstance(i, int):
                        dve.wait_ge(in_x[i], 16 * 2 * CH)
                    elif l == 0:
                        for hp in range(1, HP):
                            dve.wait_ge(in_x[hp], 16 * 2 * CH)
                    wait(dve, aggr, n - 1)
                    src = xs[:, ds(i, 1), :, :].rearrange("p o c (y w q) -> p (o c) y w q", w=GRID, q=PATCH)
                    alone(dve, carried)
                    for c in range(CH):
                        dve.bn_stats(stat[:, r, 6 * c:6 * c + 6], src[:, c, :, l, :]).then_inc(statd, 1)
                    wait(dve, statd, CH * n + CH)
                    wait(dve, nmud, n - 1)
                    alone(dve, carried)
                    dve.bn_aggr(mv[:, r, :], stat[:, r, :]).then_inc(aggr, 1)
                    wait(dve, aggr, n + 1)
                    wait(dve, sdev, n - 1)
                    dve.tensor_scalar(ve[:, r:r + 1], mv[:, r, 1:2], EPS, None, ALU.add).then_inc(vard, 1)
                if live(i, GRID, l - 1, NPT):
                    r, n = (l - 1) % 2, i * GRID + (l - 1)
                    wait(dve, sdev, n + 1)
                    wait(dve, xnd, n - 1)
                    dve.reciprocal(rstd[:, r:r + 1], sd[:, r:r + 1]).then_inc(rsd, 1)
                    wait(dve, rsd, n + 1)
                    dve.tensor_scalar(nmu[:, r:r + 1], mv[:, r, 0:1], rstd[:, r:r + 1], -1.0, ALU.mult,
                                      ALU.mult).then_inc(nmud, 1)
                if live(i, GRID, l - 3, NPT):
                    r, n = (l - 3) % 2, i * GRID + (l - 3)
                    wait(dve, z_ps, n + 1)
                    wait(dve, t1d, n - 1)
                    dve.tensor_tensor(zs[:, r, :], z_bank(r), zbias[:, :], ALU.add).then_inc(zsd, 1)
                    wait(dve, zsd, n + 1)
                    wait(dve, aggr2, n - 1)
                    dve.bn_stats(stat2[:, r, :], zs[:, r, :]).then_inc(stat2d, 1)
                    wait(dve, stat2d, n + 1)
                    alone(dve, carried)
                    dve.bn_aggr(mv2[:, r, :], stat2[:, r, :]).then_inc(aggr2, 1)
                    wait(dve, aggr2, n + 1)
                    wait(dve, sdev2, n - 1)
                    dve.tensor_scalar(ve2[:, r:r + 1], mv2[:, r, 1:2], EPS, None, ALU.add).then_inc(var2, 1)
                if live(i, GRID, l - 4, NPT):
                    r, n = (l - 4) % 2, i * GRID + (l - 4)
                    wait(dve, sdev2, n + 1)
                    wait(dve, hnd, n - 1)
                    dve.reciprocal(rstd2[:, r:r + 1], sd2[:, r:r + 1]).then_inc(rsd2, 1)
                    dve.scalar_tensor_tensor(out=t1[:, r, :], in0=zs[:, r, :], scalar=mv2[:, r, 0:1], in1=g2_row[:, :],
                                             op0=ALU.subtract, op1=ALU.mult).then_inc(t1d, 1)
                    wait(dve, t1d, n + 1)
                    wait(dve, rsd2, n + 1)
                    wait(dve, h_ps, n - 1)
                    wait(dve, hres, n - 1)
                    dve.scalar_tensor_tensor(out=hn[:, r, :], in0=t1[:, r, :], scalar=rstd2[:, r:r + 1],
                                             in1=h[:, ds(n * D, D)], op0=ALU.mult, op1=ALU.add).then_inc(hnd, 1)

            rounds(dve, HP, GRID, 5, step)


def attention(nc, a, keep, first):
    hT_hi, hT_lo, ps = keep["hT_hi"], keep["hT_lo"], keep["ps"]
    wqkv_hi, wqkv_lo, ident, bias_col, attn = (keep[x] for x in ("wqkv_hi", "wqkv_lo", "ident", "bias_col", "attn"))
    tag = "a" if first else "b"
    bcol = 0 if first else 6
    PER = 2 * IG
    AHEAD = IG
    ROUNDS = UNITS // PER
    with phase(nc) as (ctx, taken):
        def sb(name, shape, dt=F32):
            return ctx.enter_context(nc.sbuf_tensor(name + tag, shape, dt))

        def sem(name):
            taken.append(nc.alloc_semaphore(name + tag))
            return taken[-1]

        qT = sb("qT", [P, 2, DC * GC + P])
        kT = sb("kT", [P, 2, DC * GC])
        vT = sb("vT", [P, 2, DC * 3 * GC])
        kbd = sb("kbd", [P, 2, DC, HC, GC])
        PW = HC * NPOS + NPOS
        prob = sb("prob", [P, 2, PW])
        pT = sb("pT", [KEYROWS, 2, 3 * P])
        vbd = sb("vbd", [KEYROWS, 2, 2 * HEADS * VW])
        osb = sb("osb", [P, 2, D])
        mx = sb("mx", [P, 2, HC])
        rsum = sb("rsum", [P, 2, HEADS])
        kmask = sb("kmask", [P, HC])
        vmask3 = sb("vmask3", [KEYROWS, 3])
        vmask = sb("vmask", [KEYROWS, 2 * HEADS])
        raw = sb("raw", [P, 2, 2 * D]) if first else None

        kmask_steps, vmask_steps, vmask_made, zeros_made, ones_made = map(
            sem, ("kmask_steps", "vmask_steps", "vmask_made", "zeros_made", "ones_made"))
        qkv_ps, qkv_sb, kbd_made, s_ps, max_made, sub_made, exp_made = map(
            sem, ("qkv_ps", "qkv_sb", "kbd_made", "s_ps", "max_made", "sub_made", "exp_made"))
        pT_ps, pT_sb, v_ps, vbd_made, o_ps, rsum_made, o_made, oT_ps, oT_sb = map(
            sem, ("pT_ps", "pT_sb", "v_ps", "vbd_made", "o_ps", "rsum_made", "o_made", "oT_ps", "oT_sb"))
        o_moved = [sem(f"o_moved{r}") for r in range(2)]
        o_back, carried = sem("o_back"), sem("carried")
        in_exp = [sem(f"in_exp{r}") for r in range(2)]
        exp_hi, exp_lo = map(sem, ("exp_hi", "exp_lo"))

        def s_bank(r):
            return ps[:, 512 * r:512 * r + HC * NPOS]

        def pT_bank(r):
            return ps[0:KEYROWS, 1024 + 512 * r:1024 + 512 * r + 3 * P]

        qkv_bank = ps[:, 2048:2048 + GC]
        v_bank = ps[0:KEYROWS, 2560:3072]
        o_bank = ps[:, 3072:3072 + HEADS * VW]
        oT_bank = ps[:, 3584:3584 + DC * P]

        block = ctx.enter_context(nc.Block())

        @block.gpsimd
        def _(pool):
            pool.memset(kmask[:, :], 1.0).then_inc(kmask_steps, 1)
            pool.wait_ge(kmask_steps, 1)
            pool.affine_select(out=kmask[:, :], in_=kmask[:, :], compare_op=ALU.is_ge, fill=0.0,
                               base=0, pattern=[[-HD, HC]], channel_multiplier=1).then_inc(kmask_steps, 1)
            pool.wait_ge(kmask_steps, 2)
            pool.affine_select(out=kmask[:, :], in_=kmask[:, :], compare_op=ALU.is_ge, fill=0.0,
                               base=HD - 1, pattern=[[HD, HC]], channel_multiplier=-1).then_inc(kmask_steps, 1)
            pool.memset(vmask3[:, :], 1.0).then_inc(vmask_steps, 1)
            pool.wait_ge(vmask_steps, 1)
            pool.affine_select(out=vmask3[:, :], in_=vmask3[:, :], compare_op=ALU.is_ge, fill=0.0,
                               base=0, pattern=[[-NPOS, 3]], channel_multiplier=1).then_inc(vmask_steps, 1)
            pool.wait_ge(vmask_steps, 2)
            pool.affine_select(out=vmask3[:, :], in_=vmask3[:, :], compare_op=ALU.is_ge, fill=0.0,
                               base=NPOS - 1, pattern=[[NPOS, 3]], channel_multiplier=-1).then_inc(vmask_steps, 1)
            pool.wait_ge(kmask_steps, 3)

            def step(i, l):
                for c in range(DC):
                    if l % IG == 3 + c and live(i, 2, l // IG, IG):
                        g, r = 2 * i + l // IG, l // IG
                        wait(pool, qkv_sb, 6 * g + 3 + c)
                        wait(pool, s_ps, IG * (g - 1))
                        alone(pool, carried)
                        for hh in range(HC):
                            pool.tensor_scalar(kbd[:, r, c, hh, :], kT[:, r, c * GC:(c + 1) * GC],
                                               kmask[:, hh:hh + 1], 1.0, ALU.mult, ALU.mult).then_inc(kbd_made, 1)
                if first and isinstance(i, int) and i == 0 and l < E:
                    pool.wait_ge(exp_hi, l + 1)
                    pool.tensor_tensor(keep["we_lo"][:, :, l * D:(l + 1) * D],
                                       raw[:, l % 2, :].rearrange("p (c n) -> p c n", c=DC),
                                       keep["we_hi"][:, :, l * D:(l + 1) * D].bitcast(F32), ALU.subtract
                                       ).then_inc(exp_lo, 1)

            rounds(pool, ROUNDS, PER, 0, step)

        @block.sync
        def _(sp):
            if first:
                for e in range(E):
                    if e >= 2:
                        sp.wait_ge(exp_lo, e - 1)
                    sp.dma_start(raw[:, e % 2, :].rearrange("p (c n) -> p c n", c=DC),
                                 a["w_exp"][e].rearrange("(c p) n -> p c n", p=P)).then_inc(in_exp[e % 2], 16)
            else:
                def move(i, l):
                    if l % 2 == 1:
                        return
                    if live(i, PER // 2, (l - AHEAD) // 2, B // 2):
                        r, p = (l // 2) % 2, i * (PER // 2) + (l - AHEAD) // 2
                        wait(sp, o_made, p + 1)
                        for im in range(2):
                            sp.dma_start(a["o_dram"][ds(2 * p + im, 1), :, :].rearrange("o s d -> (o s) d"),
                                         osb[QPAD * im:QPAD * im + NPOS, r, :]).then_inc(o_moved[r], 16)

                rounds(sp, ROUNDS, PER, AHEAD, move)
                for r in range(2):
                    sp.wait_ge(o_moved[r], 16 * B // 2)
                for h2 in range(2):
                    cnt = (NPOS + 1 - h2) // 2
                    sp.dma_start(attn[B * h2:B * h2 + B, 0:cnt * D].rearrange("b (t d) -> b t d", d=D),
                                 a["o_dram"][:, h2:NPOS:2, :]).then_inc(o_back, 16)
                sp.wait_ge(o_back, 32)

        @block.scalar
        def _(act):
            act.wait_ge(zeros_made, 5)

            def step(i, l):
                if l % IG < 6 and live(i, 2, l // IG, IG):
                    g, r, j = 2 * i + l // IG, l // IG, l % IG
                    src = qkv_bank.rearrange("p (k b) -> p b k", b=IG)
                    if j < 2 * DC:
                        dst = (qT, kT)[j // DC][:, r, (j % DC) * GC:(j % DC + 1) * GC].rearrange("p (b k) -> p b k", k=NPOS)
                    else:
                        dst = vT[:, r, (j % DC) * 3 * GC:(j % DC + 1) * 3 * GC].rearrange(
                            "p (b t k) -> p b t k", t=3, k=NPOS)
                        src = src.unsqueeze(2).to_broadcast([P, IG, 3, NPOS])
                    wait(act, qkv_ps, 6 * g + j + 1)
                    if j == 0:
                        wait(act, s_ps, IG * (g - 1))
                    if j == DC:
                        wait(act, kbd_made, 2 * HC * (g - 1))
                    if j == 2 * DC:
                        wait(act, v_ps, 4 * (g - 1))
                    act.activation(dst, src, ACT.Identity,
                                   bias=bias_col[:, bcol + j:bcol + j + 1]).then_inc(qkv_sb, 1)
                if first and isinstance(i, int) and i == 0 and l < E:
                    act.wait_ge(in_exp[l % 2], 16 * (l // 2 + 1))
                    act.activation(keep["we_hi"][:, :, l * D:(l + 1) * D],
                                   raw[:, l % 2, :].rearrange("p (c n) -> p c n", c=DC), ACT.Copy).then_inc(exp_hi, 1)
                if live(i, PER, l - AHEAD, UNITS):
                    n, r = i * PER + (l - AHEAD), l % 2
                    wait(act, sub_made, n + 1)
                    p8 = prob[:, r, 0:HC * NPOS]
                    act.activation(p8, p8, ACT.Exp, scale=float(HD) ** -0.5).then_inc(exp_made, 1)
                if live(i, PER, l - AHEAD - 1, UNITS):
                    n, r = i * PER + (l - AHEAD - 1), (l - 1) % 2
                    wait(act, pT_ps, n + 1)
                    wait(act, o_ps, n - 1)
                    act.activation(pT[:, r, :], pT_bank(r), ACT.Copy).then_inc(pT_sb, 1)
                if first and l % 2 == 0 and live(i, PER // 2, (l - AHEAD - 4) // 2, B // 2):
                    p = i * (PER // 2) + (l - AHEAD - 4) // 2
                    wait(act, oT_ps, p + 1)
                    src = oT_bank.rearrange("p (c m k) -> p c m k", c=DC, m=2)
                    dst = attn[:, 0:DC * NTOK].rearrange("p (c k b) -> p c k b", c=DC, b=B)
                    for im in range(2):
                        act.activation(dst[:, :, :, ds(2 * p + im, 1)].rearrange("p c k o -> p c (k o)"),
                                       src[:, :, im, 0:NPOS], ACT.Copy).then_inc(oT_sb, 1)

            rounds(act, ROUNDS, PER, AHEAD + 5, step)

        @block.tensor
        def _(pe):
            def step(i, l):
                if live(i, PER, l - AHEAD, UNITS):
                    n, r = i * PER + (l - AHEAD), l % 2
                    g, st, c = 2 * i + (l - AHEAD) // IG, ((l - AHEAD) // IG) % 2, l % 2
                    if l % IG < 2:
                        wait(pe, kbd_made, 2 * HC * g + HC * (c + 1))
                    wait(pe, sub_made, n - 1)
                    for im in range(2):
                        b = ((l % IG) // 2) * 2 + im
                        q0 = c * GC + b * NPOS
                        last = pe.matmul(s_bank(r)[QPAD * im:QPAD * im + QPAD, :], qT[:, st, q0:q0 + QPAD],
                                         kbd[:, st, c, :, b * NPOS:(b + 1) * NPOS], start=True, stop=True)
                    last.then_inc(s_ps, 1)
                if l % IG < 6 and live(i, 2, l // IG, IG):
                    g, j = 2 * i + l // IG, l % IG
                    wait(pe, qkv_sb, 6 * g + j)
                    terms = [(w, x, c) for w, x in ((wqkv_hi, hT_hi), (wqkv_lo, hT_hi), (wqkv_hi, hT_lo)) for c in range(DC)]
                    for m, (w, x, c) in enumerate(terms):
                        rhs = x[:, c, :].rearrange("p (k b) -> p k b", b=B)[:, :, ds(IG * g, IG)]
                        last = pe.matmul(qkv_bank.rearrange("p (k b) -> p k b", b=IG), w[:, c, j * P:(j + 1) * P], rhs,
                                         start=(m == 0), stop=(m == len(terms) - 1))
                    last.then_inc(qkv_ps, 1)
                if l % 2 == 0 and live(i, PER // 2, (l - AHEAD) // 2, B // 2):
                    p, st = i * (PER // 2) + (l - AHEAD) // 2, ((l - AHEAD) // IG) % 2
                    wait(pe, vbd_made, p)
                    if l % IG == 0:
                        wait(pe, qkv_sb, 6 * (2 * i + (l - AHEAD) // IG) + 6)
                    for im in range(2):
                        b = ((l % IG) // 2) * 2 + im
                        for c in range(DC):
                            v0 = (c * IG + b) * KEYROWS
                            last = pe.transpose(v_bank[:, im * D + c * P:im * D + (c + 1) * P],
                                                vT[:, st, v0:v0 + KEYROWS], ident[:, :])
                    last.then_inc(v_ps, 1)
                if live(i, PER, l - AHEAD - 1, UNITS):
                    n, r = i * PER + (l - AHEAD - 1), (l - 1) % 2
                    wait(pe, exp_made, n + 1)
                    wait(pe, pT_sb, n - 1)
                    for t in range(3):
                        last = pe.transpose(pT_bank(r)[:, t * P:(t + 1) * P],
                                            prob[:, r, t * KEYROWS:(t + 1) * KEYROWS], ident[:, :])
                    last.then_inc(pT_ps, 1)
                if live(i, PER, l - AHEAD - 2, UNITS):
                    n, r, c = i * PER + (l - AHEAD - 2), l % 2, l % 2
                    p, pr = i * (PER // 2) + (l - AHEAD - 2 - c) // 2, ((l - AHEAD - 2) // 2) % 2
                    wait(pe, pT_sb, n + 1)
                    wait(pe, vbd_made, p + 1)
                    if c == 0:
                        wait(pe, o_made, p)
                    for t in range(3):
                        hn_ = min(3, HC - 3 * t)
                        h0 = HC * c + 3 * t
                        for im in range(2):
                            v0 = (HEADS * im + h0) * VW
                            last = pe.matmul(o_bank[QPAD * im:QPAD * im + QPAD, h0 * VW:(h0 + hn_) * VW],
                                             pT[:, r, t * P + QPAD * im:t * P + QPAD * im + QPAD],
                                             vbd[:, pr, v0:v0 + hn_ * VW], start=True, stop=True)
                    last.then_inc(o_ps, 1)
                if first and l % 2 == 0 and live(i, PER // 2, (l - AHEAD - 4) // 2, B // 2):
                    p, r = i * (PER // 2) + (l - AHEAD - 4) // 2, ((l - AHEAD - 4) // 2) % 2
                    wait(pe, o_made, p + 1)
                    wait(pe, oT_sb, 2 * p)
                    for c in range(DC):
                        last = pe.transpose(oT_bank[:, c * P:(c + 1) * P], osb[:, r, c * P:(c + 1) * P], ident[:, :])
                    last.then_inc(oT_ps, 1)

            pe.wait_ge(zeros_made, 5)
            rounds(pe, ROUNDS, PER, AHEAD + 5, step)

        @block.vector
        def _(dve):
            for r in range(2):
                dve.memset(qT[:, r, DC * GC:DC * GC + P], 0.0).then_inc(zeros_made, 1)
                dve.memset(prob[:, r, HC * NPOS:PW], 0.0).then_inc(zeros_made, 1)
            dve.memset(ps[:, 0:8 * 512], 0.0).then_inc(zeros_made, 1)
            dve.wait_ge(vmask_steps, 3)
            for hh in range(2 * HEADS):
                j = (hh % HC) % 3
                dve.tensor_copy(vmask[:, hh:hh + 1], vmask3[:, j:j + 1]).then_inc(vmask_made, 1)
            dve.wait_ge(vmask_made, 2 * HEADS)
            for r in range(2):
                ones = vbd[:, r, :].rearrange("p (h v) -> p h v", v=VW)[:, :, HD:VW]
                dve.tensor_copy(ones, vmask[:, :].unsqueeze(2)).then_inc(ones_made, 1)
            dve.wait_ge(ones_made, 2)

            def step(i, l):
                if live(i, PER, l - AHEAD, UNITS):
                    n, r = i * PER + (l - AHEAD), l % 2
                    wait(dve, s_ps, n + 1)
                    wait(dve, sub_made, n - 1)
                    s8 = s_bank(r).rearrange("p (h k) -> p h k", k=NPOS)
                    dve.tensor_reduce(mx[:, r, :], s8, AX.X, ALU.max).then_inc(max_made, 1)
                    wait(dve, max_made, n + 1)
                    wait(dve, pT_ps, n - 1)
                    dve.tensor_tensor(prob[:, r, 0:HC * NPOS].rearrange("p (h k) -> p h k", k=NPOS), s8,
                                      mx[:, r, :].unsqueeze(2).to_broadcast([P, HC, NPOS]), ALU.subtract
                                      ).then_inc(sub_made, 1)
                if l % 2 == 1 and live(i, PER // 2, (l - AHEAD - 1) // 2, B // 2):
                    p, r = i * (PER // 2) + (l - AHEAD - 1) // 2, ((l - AHEAD - 1) // 2) % 2
                    wait(dve, v_ps, p + 1)
                    wait(dve, o_ps, 2 * (p - 1))
                    dve.tensor_tensor(vbd[:, r, :].rearrange("p (h v) -> p h v", v=VW)[:, :, 0:HD],
                                      v_bank.rearrange("p (h v) -> p h v", v=HD),
                                      vmask[:, :].unsqueeze(2).to_broadcast([KEYROWS, 2 * HEADS, HD]), ALU.mult
                                      ).then_inc(vbd_made, 1)
                if l % 2 == 0 and live(i, PER // 2, (l - AHEAD - 4) // 2, B // 2):
                    p, r = i * (PER // 2) + (l - AHEAD - 4) // 2, ((l - AHEAD - 4) // 2) % 2
                    wait(dve, o_ps, 2 * p + 2)
                    wait(dve, o_made, p - 1)
                    o16 = o_bank.rearrange("p (h v) -> p h v", v=VW)
                    dve.reciprocal(rsum[:, r, :].unsqueeze(2), o16[:, :, HD:VW]).then_inc(rsum_made, 1)
                    wait(dve, rsum_made, p + 1)
                    if first:
                        wait(dve, oT_ps, p - 1)
                    else:
                        wait(dve, o_moved[r], 32 * (i * (PER // 4) + (l - AHEAD - 4) // 4))
                    dve.tensor_tensor(osb[:, r, :].rearrange("p (h v) -> p h v", v=HD), o16[:, :, 0:HD],
                                      rsum[:, r, :].unsqueeze(2).to_broadcast([P, HEADS, HD]), ALU.mult
                                      ).then_inc(o_made, 1)

            rounds(dve, ROUNDS, PER, AHEAD + 5, step)


def norm_and_experts(nc, a, keep):
    h, hT_hi, hT_lo, ps, attn = (keep[x] for x in ("h", "hT_hi", "hT_lo", "ps", "attn"))
    wqkv_hi, wqkv_lo, wo_hi, wo_lo = (keep[x] for x in ("wqkv_hi", "wqkv_lo", "wo_hi", "wo_lo"))
    we_hi, we_lo, ident = keep["we_hi"], keep["we_lo"], keep["ident"]
    with phase(nc) as (ctx, taken):
        def sb(name, shape, dt=F32):
            return ctx.enter_context(nc.sbuf_tensor(name, shape, dt))

        def sem(name):
            taken.append(nc.alloc_semaphore(name))
            return taken[-1]

        w2_raw = sb("w2_raw", [P, DC, 3 * D])
        aT_hi = sb("aT_hi", [P, 2, DC, P], F32R)
        aT_lo = sb("aT_lo", [P, 2, DC, P], F32R)
        stat = sb("stat3", [P, 2, 6])
        mv = sb("mv3", [P, 2, 2])
        mean = sb("mean3", [P, NT])
        ve = sb("ve3", [P, NT])
        sd = sb("sd3", [P, NT])
        rstd = sb("rstd3", [P, NT])
        nmr = sb("nmr3", [P, NT])
        hn = sb("hn3", [P, 2, D])
        tT_hi = sb("tT_hi", [P, 2, DC, P], F32R)
        tT_lo = sb("tT_lo", [P, 2, DC, P], F32R)
        wg_raw = sb("wg_raw", [P, DC, E])
        wg_hi = sb("wg_hi", [P, DC, E], F32R)
        wg_lo = sb("wg_lo", [P, DC, E], F32R)
        bg_row = sb("bg_row", [P, E])
        be = sb("be", [E, D])
        iota8 = sb("iota8", [P, E])
        lg = sb("lg", [P, 2, E])
        lmax = sb("lmax", [P, 2])
        lsub = sb("lsub", [P, 2, E])
        ge = sb("ge", [P, 2, E])
        gsum = sb("gsum", [P, 2])
        grs = sb("grs", [P, 2])
        gate = sb("gate", [P, 2, E])
        top = sb("top", [P, 2, E])
        topi = sb("topi", [P, 2, E], U32)
        topf = sb("topf", [P, 2, 2])
        pick = sb("pick", [P, 2, 2, E])
        comb = sb("comb", [P, 2, E])
        combT = sb("combT", [E, 2, P])

        in_w2, in_g, in_be, w2_hi, w2_lo, wg_h, wg_l, iota_made, mv_set = map(
            sem, ("in_w2", "in_g", "in_be", "w2_hi", "w2_lo", "wg_h", "wg_l", "iota_made", "mv_set"))
        carried, meand = sem("carried3"), sem("meand")
        ahi, alo, wo_ps, zadd, statd, aggrd, vard, sdev, rsd, nmrd = map(
            sem, ("ahi", "alo", "wo_ps", "zadd", "statd3", "aggrd", "vard3", "sdev3", "rsd3", "nmrd"))
        hnd, hback, t_ps, thi, tlo, tcopy, g_ps, lgd, lmaxd, lsubd, ged, grsd, gated, topd, topid, topfd, pickd, combd = map(
            sem, ("hnd3", "hback", "t_ps", "thi", "tlo", "tcopy", "g_ps", "lgd", "lmaxd", "lsubd", "ged", "grsd",
                  "gated", "topd", "topid", "topfd", "pickd", "combd"))
        cT_ps, cT_sb, be_ps, ex_ps, acc = map(sem, ("cT_ps", "cT_sb", "be_ps", "ex_ps", "acc"))

        def wo_bank(r):
            return ps[:, 3072 + 512 * r:3072 + 512 * r + D]

        t_bank = ps[:, 2048:2048 + D]
        g_bank = ps[:, 2560:2560 + E]
        cT_bank = ps[0:E, 2560 + 64:2560 + 64 + P]
        be_bank = ps[:, 3072:3072 + D]

        block = ctx.enter_context(nc.Block())

        @block.sync
        def _(sp):
            sp.dma_start(wg_raw[:, :, :], a["w_gate"].rearrange("(c p) e -> p c e", p=P)).then_inc(in_g, 16)
            sp.dma_start(bg_row[:, :], a["b_gate"].partition_broadcast(P)).then_inc(in_g, 16)
            sp.dma_start(be[:, :], a["b_exp"]).then_inc(in_be, 16)
            sp.dma_start(w2_raw[:, :, :], a["w_qkv"].rearrange("(c p) n -> p c n", p=P)).then_inc(in_w2, 16)

        @block.gpsimd
        def _(pool):
            pool.memset(mean[:, :], 0.0).then_inc(mv_set, 1)
            pool.memset(ve[:, :], 1.0).then_inc(mv_set, 1)
            pool.iota(iota8[:, :], pattern=[[1, E]], base=0, channel_multiplier=0,
                      allow_small_or_imprecise_dtypes=True).then_inc(iota_made, 1)

            def split(i, l):
                if live(i, GRID, l, NT):
                    r, n, m = l % 2, i * GRID + l, rows_of(i, l)
                    wait(pool, ahi, n + 1)
                    wait(pool, wo_ps, n - 1)
                    src = attn[:, 0:DC * NTOK].rearrange("p (c t) -> p c t", c=DC)[:, :, ds(n * P, m)]
                    pool.tensor_tensor(aT_lo[:, r, :, 0:m], src, aT_hi[:, r, :, 0:m].bitcast(F32),
                                       ALU.subtract).then_inc(alo, 1)

            rounds(pool, HP, GRID, 1, split)
            pool.wait_ge(in_w2, 16)
            pool.wait_ge(w2_hi, 1)
            pool.tensor_tensor(wqkv_lo[:, :, :], w2_raw[:, :, :], wqkv_hi[:, :, :].bitcast(F32),
                               ALU.subtract).then_inc(w2_lo, 1)

            def step(i, l):
                if live(i, GRID, l, NT):
                    r, n, m = l % 2, i * GRID + l, rows_of(i, l)
                    wait(pool, hnd, n + 1)
                    pool.tensor_copy(h[0:m, ds(n * D, D)], hn[0:m, r, :]).then_inc(hback, 1)
                if live(i, GRID, l - 1, NT):
                    r, n, m = (l - 1) % 2, i * GRID + (l - 1), rows_of(i, l - 1)
                    wait(pool, thi, n + 1)
                    wait(pool, tlo, n + 1)
                    for src, dst in ((tT_hi, hT_hi), (tT_lo, hT_lo)):
                        pool.tensor_copy(dst[:, :, ds(n * P, m)], src[:, r, :, 0:m]).then_inc(tcopy, 1)

            rounds(pool, HP, GRID, 2, step)

        @block.scalar
        def _(act):
            act.wait_ge(in_w2, 16)
            act.activation(wqkv_hi[:, :, :], w2_raw[:, :, :], ACT.Copy).then_inc(w2_hi, 1)
            act.wait_ge(in_g, 32)
            act.activation(wg_hi[:, :, :], wg_raw[:, :, :], ACT.Copy).then_inc(wg_h, 1)

            def split(i, l):
                if live(i, GRID, l, NT):
                    r, n, m = l % 2, i * GRID + l, rows_of(i, l)
                    wait(act, alo, n - 1)
                    wait(act, wo_ps, n - 1)
                    src = attn[:, 0:DC * NTOK].rearrange("p (c t) -> p c t", c=DC)[:, :, ds(n * P, m)]
                    act.activation(aT_hi[:, r, :, 0:m], src, ACT.Copy).then_inc(ahi, 1)

            rounds(act, HP, GRID, 1, split)
            act.wait_ge(vard, NT)
            act.activation(sd[:, :], ve[:, :], ACT.Sqrt).then_inc(sdev, 1)
            act.wait_ge(nmrd, 1)

            def step(i, l):
                if live(i, GRID, l, NT):
                    r, n, m = l % 2, i * GRID + l, rows_of(i, l)
                    wait(act, hback, n - 1)
                    wait(act, t_ps, n - 1)
                    act.activation(hn[0:m, r, :], h[0:m, ds(n * D, D)], ACT.Identity, bias=nmr[0:m, ds(n, 1)],
                                   scale=rstd[0:m, ds(n, 1)]).then_inc(hnd, 1)
                    wait(act, t_ps, n + 1)
                    wait(act, ex_ps, 4 * (n - 1))
                    wait(act, tcopy, 2 * (n - 1))
                    act.activation(tT_hi[:, r, :, 0:m], t_bank.rearrange("p (c t) -> p c t", c=DC)[:, :, 0:m],
                                   ACT.Copy).then_inc(thi, 1)
                    wait(act, lsubd, n + 1)
                    wait(act, gated, n - 1)
                    act.activation(ge[0:m, r, :], lsub[0:m, r, :], ACT.Exp, accum_out=gsum[0:m, r:r + 1]).then_inc(ged, 1)
                if live(i, GRID, l - 1, NT):
                    r, n, m = (l - 1) % 2, i * GRID + (l - 1), rows_of(i, l - 1)
                    wait(act, cT_ps, n + 1)
                    wait(act, be_ps, n - 1)
                    act.activation(combT[:, r, 0:m], cT_bank[:, 0:m], ACT.Copy).then_inc(cT_sb, 1)

            rounds(act, HP, GRID, 2, step)

        @block.tensor
        def _(pe):
            def project(i, l):
                if live(i, GRID, l, NT):
                    r, n, m = l % 2, i * GRID + l, rows_of(i, l)
                    wait(pe, alo, n + 1)
                    wait(pe, zadd, n - 1)
                    terms = [(x, w, c) for x, w in ((aT_hi, wo_hi), (aT_hi, wo_lo), (aT_lo, wo_hi)) for c in range(DC)]
                    for k, (x, w, c) in enumerate(terms):
                        last = pe.matmul(wo_bank(r)[0:m, :], x[:, r, c, 0:m], w[:, c, :], start=(k == 0),
                                         stop=(k == len(terms) - 1))
                    last.then_inc(wo_ps, 1)

            rounds(pe, HP, GRID, 1, project)
            pe.wait_ge(wg_h, 1)
            pe.wait_ge(wg_l, 1)
            pe.wait_ge(in_be, 16)
            pe.wait_ge(zadd, NT)

            def experts(i, l, r, n, m, q):
                wait(pe, acc, 9 * (n - 1) + 2 * q + 2)
                terms = [(x, w, c) for x, w in ((tT_hi, we_hi), (tT_hi, we_lo), (tT_lo, we_hi)) for c in range(DC)]
                for k, (x, w, c) in enumerate(terms):
                    last = pe.matmul(ps[0:m, 512 * q:512 * q + 2 * D], x[:, r, c, 0:m], w[:, c, 2 * D * q:2 * D * (q + 1)],
                                     start=(k == 0), stop=(k == len(terms) - 1))
                last.then_inc(ex_ps, 1)

            def step(i, l):
                cur, prev = live(i, GRID, l, NT), live(i, GRID, l - 1, NT)
                r, n, m = l % 2, i * GRID + l, rows_of(i, l)
                rp, np_, mp = (l - 1) % 2, i * GRID + (l - 1), rows_of(i, l - 1)
                if cur:
                    wait(pe, hnd, n + 1)
                    wait(pe, thi, n)
                    wait(pe, tlo, n)
                    for c in range(DC):
                        last = pe.transpose(t_bank[:, c * P:c * P + m], hn[0:m, r, c * P:(c + 1) * P], ident[0:m, 0:m])
                    last.then_inc(t_ps, 1)
                if prev:
                    experts(i, l, rp, np_, mp, 0)
                if cur:
                    wait(pe, thi, n + 1)
                    wait(pe, tlo, n + 1)
                    wait(pe, lgd, n)
                    wait(pe, cT_sb, n - 1)
                    terms = [(x, w, c) for x, w in ((tT_hi, wg_hi), (tT_hi, wg_lo), (tT_lo, wg_hi)) for c in range(DC)]
                    for k, (x, w, c) in enumerate(terms):
                        last = pe.matmul(g_bank[0:m, :], x[:, r, c, 0:m], w[:, c, :], start=(k == 0),
                                         stop=(k == len(terms) - 1))
                    last.then_inc(g_ps, 1)
                if prev:
                    experts(i, l, rp, np_, mp, 1)
                    experts(i, l, rp, np_, mp, 2)
                    wait(pe, combd, np_ + 1)
                    if cur:
                        wait(pe, lgd, n + 1)
                    pe.transpose(cT_bank[:, 0:mp], comb[0:mp, rp, :], ident[0:mp, 0:mp]).then_inc(cT_ps, 1)
                    experts(i, l, rp, np_, mp, 3)
                    wait(pe, cT_sb, np_ + 1)
                    wait(pe, acc, 9 * np_)
                    pe.matmul(be_bank[0:mp, :], combT[:, rp, 0:mp], be[:, :], start=True, stop=True).then_inc(be_ps, 1)

            rounds(pe, HP, GRID, 2, step)

        @block.vector
        def _(dve):
            dve.wait_ge(wg_h, 1)
            dve.tensor_tensor(wg_lo[:, :, :], wg_raw[:, :, :], wg_hi[:, :, :].bitcast(F32), ALU.subtract).then_inc(wg_l, 1)
            dve.wait_ge(mv_set, 2)

            def add(i, l):
                if live(i, GRID, l, NT):
                    r, n, m = l % 2, i * GRID + l, rows_of(i, l)
                    hh = h[0:m, ds(n * D, D)]
                    wait(dve, wo_ps, n + 1)
                    dve.tensor_tensor(hh, wo_bank(r)[0:m, :], hh, ALU.add).then_inc(zadd, 1)
                    wait(dve, zadd, n + 1)
                    wait(dve, aggrd, n - 1)
                    alone(dve, carried)
                    dve.bn_stats(stat[0:m, r, :], hh).then_inc(statd, 1)
                    wait(dve, statd, n + 1)
                    wait(dve, meand, n - 1)
                    alone(dve, carried)
                    dve.bn_aggr(mv[0:m, r, :], stat[0:m, r, :]).then_inc(aggrd, 1)
                    wait(dve, aggrd, n + 1)
                    dve.tensor_scalar(ve[0:m, ds(n, 1)], mv[0:m, r, 1:2], EPS, None, ALU.add).then_inc(vard, 1)
                    dve.tensor_copy(mean[0:m, ds(n, 1)], mv[0:m, r, 0:1]).then_inc(meand, 1)

            rounds(dve, HP, GRID, 1, add)
            dve.wait_ge(meand, NT)
            dve.wait_ge(sdev, 1)
            dve.reciprocal(rstd[:, :], sd[:, :]).then_inc(rsd, 1)
            dve.wait_ge(rsd, 1)
            dve.scalar_tensor_tensor(out=nmr[:, :], in0=mean[:, :], scalar=-1.0, in1=rstd[:, :],
                                     op0=ALU.mult, op1=ALU.mult).then_inc(nmrd, 1)
            dve.wait_ge(iota_made, 1)
            dve.wait_ge(in_g, 32)

            def combine(i, l, js):
                r, n, m = (l - 1) % 2, i * GRID + (l - 1), rows_of(i, l - 1)
                hh = h[0:m, ds(n * D, D)]
                for j in js:
                    if j == 0:
                        wait(dve, hback, n + 1)
                        wait(dve, combd, n + 1)
                    else:
                        wait(dve, acc, 9 * n + j)
                    if j == E:
                        wait(dve, be_ps, n + 1)
                        dve.tensor_tensor(hh, be_bank[0:m, :], hh, ALU.add).then_inc(acc, 1)
                    else:
                        if j % 2 == 0:
                            wait(dve, ex_ps, 4 * n + j // 2 + 1)
                        dve.scalar_tensor_tensor(out=hh, in0=ps[0:m, D * j:D * (j + 1)], scalar=comb[0:m, r, j:j + 1],
                                                 in1=hh, op0=ALU.mult, op1=ALU.add).then_inc(acc, 1)

            def step(i, l):
                cur, prev = live(i, GRID, l, NT), live(i, GRID, l - 1, NT)
                r, n, m = l % 2, i * GRID + l, rows_of(i, l)
                if cur:
                    wait(dve, thi, n + 1)
                    wait(dve, ex_ps, 4 * (n - 1))
                    dve.tensor_tensor(tT_lo[:, r, :, 0:m], t_bank.rearrange("p (c t) -> p c t", c=DC)[:, :, 0:m],
                                      tT_hi[:, r, :, 0:m].bitcast(F32), ALU.subtract).then_inc(tlo, 1)
                if prev:
                    combine(i, l, [0, 1])
                if cur:
                    wait(dve, g_ps, n + 1)
                    dve.tensor_tensor(lg[0:m, r, :], g_bank[0:m, :], bg_row[0:m, :], ALU.add).then_inc(lgd, 1)
                    wait(dve, lgd, n + 1)
                    dve.tensor_reduce(lmax[0:m, r:r + 1], lg[0:m, r, :], AX.X, ALU.max).then_inc(lmaxd, 1)
                    wait(dve, lmaxd, n + 1)
                    wait(dve, ged, n - 1)
                    dve.tensor_scalar(lsub[0:m, r, :], lg[0:m, r, :], lmax[0:m, r:r + 1], None,
                                      ALU.subtract).then_inc(lsubd, 1)
                if prev:
                    combine(i, l, [2, 3])
                if cur:
                    wait(dve, ged, n + 1)
                    dve.reciprocal(grs[0:m, r:r + 1], gsum[0:m, r:r + 1]).then_inc(grsd, 1)
                    wait(dve, grsd, n + 1)
                    dve.tensor_scalar(gate[0:m, r, :], ge[0:m, r, :], grs[0:m, r:r + 1], None, ALU.mult).then_inc(gated, 1)
                    wait(dve, gated, n + 1)
                    alone(dve, carried)
                    dve.max(top[0:m, r, :], gate[0:m, r, :]).then_inc(topd, 1)
                    wait(dve, topd, n + 1)
                    alone(dve, carried)
                    dve.max_index(topi[0:m, r, :], top[0:m, r, :], gate[0:m, r, :]).then_inc(topid, 1)
                    wait(dve, topid, n + 1)
                    dve.tensor_copy(topf[0:m, r, :], topi[0:m, r, 0:2]).then_inc(topfd, 1)
                    wait(dve, topfd, n + 1)
                    for t in range(2):
                        dve.tensor_scalar(pick[0:m, r, t, :], iota8[0:m, :], topf[0:m, r, t:t + 1],
                                          top[0:m, r, t:t + 1], ALU.is_equal, ALU.mult).then_inc(pickd, 1)
                    wait(dve, pickd, 2 * n + 2)
                    wait(dve, cT_ps, n - 1)
                    dve.tensor_tensor(comb[0:m, r, :], pick[0:m, r, 0, :], pick[0:m, r, 1, :], ALU.add).then_inc(combd, 1)
                if prev:
                    combine(i, l, [4, 5, 6, 7, 8])

            rounds(dve, HP, GRID, 2, step)


def last_norm(nc, a, keep):
    h, attn = keep["h"], keep["attn"]
    with phase(nc) as (ctx, taken):
        def sb(name, shape, dt=F32):
            return ctx.enter_context(nc.sbuf_tensor(name, shape, dt))

        def sem(name):
            taken.append(nc.alloc_semaphore(name))
            return taken[-1]

        stat = sb("stat4", [P, NT, 6])
        mv = sb("mv4", [P, NT, 2])
        ve = sb("ve4", [P, NT])
        sd = sb("sd4", [P, NT])
        rstd = sb("rstd4", [P, NT])
        nmr = sb("nmr4", [P, NT])
        y = sb("y4", [P, NT * D])
        added, statd, aggrd, vard, sdev, rsd, nmrd, yd, stored = map(
            sem, ("added", "statd4", "aggrd4", "vard4", "sdev4", "rsd4", "nmrd4", "yd", "stored"))
        block = ctx.enter_context(nc.Block())

        ROUND = [(hp * GRID, GRID, P) for hp in range(HP)] + [(NPT, 1, B)]

        @block.vector
        def _(dve):
            for k, (t0, cnt, m) in enumerate(ROUND):
                for n in range(t0, t0 + cnt):
                    hh = h[0:m, n * D:(n + 1) * D]
                    dve.tensor_tensor(hh, hh, attn[0:m, n * D:(n + 1) * D], ALU.add).then_inc(added, 1)
                    dve.wait_ge(added, n + 1)
                    dve.bn_stats(stat[0:m, n, :], hh).then_inc(statd, 1)
                    dve.wait_ge(statd, n + 1)
                    dve.bn_aggr(mv[0:m, n, :], stat[0:m, n, :]).then_inc(aggrd, 1)
                dve.wait_ge(aggrd, t0 + cnt)
                dve.tensor_scalar(ve[0:m, t0:t0 + cnt], mv[0:m, t0:t0 + cnt, 1], EPS, None, ALU.add).then_inc(vard, 1)
                dve.wait_ge(sdev, k + 1)
                dve.reciprocal(rstd[0:m, t0:t0 + cnt], sd[0:m, t0:t0 + cnt]).then_inc(rsd, 1)
                dve.wait_ge(rsd, k + 1)
                dve.scalar_tensor_tensor(out=nmr[0:m, t0:t0 + cnt], in0=mv[0:m, t0:t0 + cnt, 0], scalar=-1.0,
                                         in1=rstd[0:m, t0:t0 + cnt], op0=ALU.mult, op1=ALU.mult).then_inc(nmrd, 1)

        @block.scalar
        def _(act):
            for k, (t0, cnt, m) in enumerate(ROUND):
                act.wait_ge(vard, k + 1)
                act.activation(sd[0:m, t0:t0 + cnt], ve[0:m, t0:t0 + cnt], ACT.Sqrt).then_inc(sdev, 1)
                act.wait_ge(nmrd, k + 1)
                for n in range(t0, t0 + cnt):
                    act.activation(y[0:m, n * D:(n + 1) * D], h[0:m, n * D:(n + 1) * D], ACT.Identity,
                                   bias=nmr[0:m, n:n + 1], scale=rstd[0:m, n:n + 1]).then_inc(yd, 1)

        @block.sync
        def _(sp):
            for hp in range(HP):
                sp.wait_ge(yd, (hp + 1) * GRID)
                for h2 in range(2):
                    s = 1 + 2 * GRID * hp + GRID * h2
                    sp.dma_start(a["out"][:, s:s + GRID, :].rearrange("b s d -> b (s d)"),
                                 y[B * h2:B * h2 + B, hp * GRID * D:(hp + 1) * GRID * D]).then_inc(stored, 16)
            sp.wait_ge(yd, NT)
            sp.dma_start(a["out"][:, 0, :], y[0:B, NPT * D:NT * D]).then_inc(stored, 16)
            sp.wait_ge(stored, 16 * (2 * HP + 1))


def vit_layer(nc, a):
    with ExitStack() as ctx:
        def sb(name, shape, dt=F32):
            return ctx.enter_context(nc.sbuf_tensor(name, shape, dt))

        keep = {
            "h": sb("h", [P, NT * D]),
            "hT_hi": sb("hT_hi", [P, DC, NTOK], F32R),
            "hT_lo": sb("hT_lo", [P, DC, NTOK], F32R),
            "wqkv_hi": sb("wqkv_hi", [P, DC, 3 * D], F32R),
            "wqkv_lo": sb("wqkv_lo", [P, DC, 3 * D], F32R),
            "wo_hi": sb("wo_hi", [P, DC, D], F32R),
            "wo_lo": sb("wo_lo", [P, DC, D], F32R),
            "ident": sb("ident", [P, P]),
            "bias_col": sb("bias_col", [P, 12]),
            "ps": ctx.enter_context(nc.psum_tensor("ps", [P, 8 * 512], F32)),
        }
        patch_tokens(nc, a, keep)
        keep["attn"] = sb("attn", [P, NT * D])
        with ExitStack() as inner:
            keep["we_hi"] = inner.enter_context(nc.sbuf_tensor("we_hi", [P, DC, E * D], F32R))
            keep["we_lo"] = inner.enter_context(nc.sbuf_tensor("we_lo", [P, DC, E * D], F32R))
            attention(nc, a, keep, True)
            norm_and_experts(nc, a, keep)
        attention(nc, a, keep, False)
        last_norm(nc, a, keep)


_INS = {"x": "x", "L0_tok_ln1_g": "ln1_g", "L0_tok_ln1_b": "ln1_b", "L0_tok_W_proj": "w_proj",
        "L0_tok_b_proj": "b_proj", "L0_tok_ln2_g": "ln2_g", "L0_tok_ln2_b": "ln2_b", "L0_tok_cls_token": "cls",
        "L0_tok_pos_emb": "pos", "L0_attn_Wq": "wq", "L0_attn_bq": "bq", "L0_attn_Wk": "wk", "L0_attn_bk": "bk",
        "L0_attn_Wv": "wv", "L0_attn_bv": "bv", "L0_attn_Wo": "wo", "L0_attn_bo": "bo", "L0_ffn_W_qkv": "w_qkv",
        "L0_ffn_b_qkv": "b_qkv", "L0_ffn_W_gate": "w_gate", "L0_ffn_b_gate": "b_gate",
        "L0_ffn_W_experts": "w_exp", "L0_ffn_b_experts": "b_exp"}


def kernel(**inputs):
    import numpy as _np
    import concourse.bacc as _bacc
    from concourse import mybir as _mybir
    from concourse.bass_utils import run_bass_kernel_spmd as _run

    nc = _bacc.Bacc("TRN2", target_bir_lowering=False, num_devices=1)
    arrays, args = {}, {}
    for name, short in _INS.items():
        arr = _np.ascontiguousarray(inputs[name])
        arrays[f"in_{name}_dram"] = arr
        args[short] = nc.dram_tensor(f"in_{name}_dram", arr.shape, _mybir.dt.from_np(arr.dtype),
                                     kind="ExternalInput").ap()
    args["out"] = nc.dram_tensor("out_0_dram", (B, NPOS, D), _mybir.dt.float32, kind="ExternalOutput").ap()
    args["o_dram"] = nc.dram_tensor("o_dram", (B, NPOS, D), _mybir.dt.float32, kind="Internal").ap()
    vit_layer(nc, args)
    r = _run(nc, [arrays], core_ids=[0])
    return r.results[0]["out_0_dram"]
```

```python
from contextlib import ExitStack, contextmanager

import concourse.bass as bass
from concourse import mybir

F32 = mybir.dt.float32
F32R = mybir.dt.float32r
U32 = mybir.dt.uint32
ALU = mybir.AluOpType
ACT = mybir.ActivationFunctionType
AX = mybir.AxisListType

P = 128
B, CH, IMG = 64, 3, 96
PATCH = 16
GRID = IMG // PATCH
D = 256
DC = D // P
HEADS, HD = 16, 16
E = 8
EPS = 1e-5
NPOS = GRID * GRID + 1
NPT = GRID * GRID // 2
NT = NPT + 1
NTOK = NPOS * B
HP = GRID // 2
ROWPIX = PATCH * IMG
FC = CH * PATCH * PATCH // P

IG = 8
GC = IG * NPOS
HC = HEADS // DC
UNITS = B // 2 * DC
KEYROWS = 3 * NPOS
VW = HD + 1
QPAD = 64


@contextmanager
def phase(nc):
    taken = []
    with ExitStack() as ctx:
        yield ctx, taken
    nc.clear_and_free_semaphores(taken)
    nc.all_engine_barrier()


def ds(start, size):
    return bass.ds(start, size)


def wait(eng, sem, value):
    if not isinstance(value, int):
        assert bass.sinput_min_value(value) > 0
    if not isinstance(value, int) or value > 0:
        eng.wait_ge(sem, value)


def alone(eng, sem):
    eng.sem_inc(sem, 1)


def live(i, per, l, total):
    return 0 <= i * per + l < total if isinstance(i, int) else True


def rounds(eng, trips, per, tail, step):
    for l in range(per):
        step(0, l)
    with eng.Fori(1, trips) as i:
        for l in range(per):
            step(i, l)
    for l in range(tail):
        step(trips, l)


def tile_cols(buf, i, l):
    v = buf[:, 0:DC * NTOK].rearrange("p (c s b) -> p c s b", c=DC, b=B)
    if isinstance(i, int) and i * GRID + l == NPT:
        return v[:, :, 0:1, :]
    v = v[:, :, 1:NPOS, :].rearrange("p c (y h w) b -> p c y h w b", h=2, w=GRID)
    return v[:, :, ds(i + l // GRID, 1), :, l % GRID, :].rearrange("p c y h b -> p c (y h) b")


def by_tile(ap):
    return ap.rearrange("p (c h b) -> p c h b", c=DC, b=B)


def rows_of(i, l, per=GRID):
    return B if isinstance(i, int) and i * per + l == NT - 1 else P


def patch_tokens(nc, a, keep):
    h, hT_hi, hT_lo, ps = keep["h"], keep["hT_hi"], keep["hT_lo"], keep["ps"]
    wqkv_hi, wqkv_lo, wo_hi, wo_lo = keep["wqkv_hi"], keep["wqkv_lo"], keep["wo_hi"], keep["wo_lo"]
    ident, bias_col = keep["ident"], keep["bias_col"]
    with phase(nc) as (ctx, taken):
        def sb(name, shape, dt=F32):
            return ctx.enter_context(nc.sbuf_tensor(name, shape, dt))

        def sem(name):
            taken.append(nc.alloc_semaphore(name))
            return taken[-1]

        xs = sb("xs", [P, HP, CH, ROWPIX])
        xn = sb("xn", [P, 2, CH * PATCH * PATCH])
        xT = sb("xT", [P, 2, FC * P])
        zs = sb("zs", [P, 2, D])
        t1 = sb("t1", [P, 2, D])
        hn = sb("hn", [P, 2, D])
        hraw = sb("hraw", [P, 2, D])
        hcls = sb("hcls", [B, 2, D])
        hcls_sum = sb("hcls_sum", [B, D])
        w_raw = sb("w_raw", [P, 4, DC, D])
        wp = sb("wp", [P, 2, CH, D])
        wpg = sb("wpg", [P, 2, CH, D])
        rows12 = sb("rows12", [12, P])
        rows4 = sb("rows4", [4, FC * P // 2])
        gcol = sb("gcol", [P, CH, 4])
        bmat = sb("bmat", [P, FC, P])
        bp_row = sb("bp_row", [P, D])
        zbias = sb("zbias", [P, D])
        g2_row = sb("g2_row", [P, D])
        b2_row = sb("b2_row", [P, D])
        bo_row = sb("bo_row", [P, D])
        stat = sb("stat", [P, 2, CH * 6])
        mv = sb("mv", [P, 2, 2])
        ve = sb("ve", [P, 2])
        sd = sb("sd", [P, 2])
        rstd = sb("rstd", [P, 2])
        nmu = sb("nmu", [P, 2])
        stat2 = sb("stat2", [P, 2, 6])
        mv2 = sb("mv2", [P, 2, 2])
        ve2 = sb("ve2", [P, 2])
        sd2 = sb("sd2", [P, 2])
        rstd2 = sb("rstd2", [P, 2])

        in_x = [sem(f"in_x{r}") for r in range(HP)]
        in_pos = [sem(f"in_pos{r}") for r in range(HP)]
        in_cls, in_rows, in_b, in_w, in_wp = map(sem, ("in_cls", "in_rows", "in_b", "in_w", "in_wp"))
        ident_zero, ident_made, cols_ps, cols_sb = map(sem, ("ident_zero", "ident_made", "cols_ps", "cols_sb"))
        wT_ps, wT_hi, wT_lo, bmat_made, zb_ps, zb_made, gain_made = map(
            sem, ("wT_ps", "wT_hi", "wT_lo", "bmat_made", "zb_ps", "zb_made", "gain_made"))
        table_made, cls_made, cls_ps, cls_raw, cls_hi, cls_out = map(
            sem, ("table_made", "cls_made", "cls_ps", "cls_raw", "cls_hi", "cls_out"))
        carried, carried_pool = sem("carried"), sem("carried_pool")
        statd, aggr, vard, sdev, rsd, nmud, xnd, xT_ps, xTd = map(
            sem, ("statd", "aggr", "vard", "sdev", "rsd", "nmud", "xnd", "xT_ps", "xTd"))
        z_ps, zsd, stat2d, aggr2, var2, sdev2, rsd2, t1d, hnd, h_ps, hrawd, hhi, hlo, hres = map(
            sem, ("z_ps", "zsd", "stat2d", "aggr2", "var2", "sdev2", "rsd2", "t1d", "hnd", "h_ps", "hrawd",
                  "hhi", "hlo", "hres"))

        def xT_bank(r):
            return ps[:, 1024 * r:1024 * r + FC * P]

        def z_bank(r):
            return ps[:, 2048 + 512 * r:2048 + 512 * r + D]

        def h_bank(r):
            return ps[:, 3072 + 512 * r:3072 + 512 * r + D]

        block = ctx.enter_context(nc.Block())

        @block.sync
        def _(sp):
            for hp in range(HP):
                for c in range(CH):
                    for h2 in range(2):
                        r0 = PATCH * (2 * hp + h2)
                        sp.dma_start(xs[B * h2:B * h2 + B, hp, c, :],
                                     a["x"][:, c, r0:r0 + PATCH, :].rearrange("b r q -> b (r q)")).then_inc(in_x[hp], 16)
                if hp == 0:
                    for j, name in enumerate(("wq", "wk", "wv", "wo")):
                        sp.dma_start(w_raw[:, j, :, :], a[name].rearrange("(c p) n -> p c n", p=P)).then_inc(in_w, 16)

        @block.gpsimd
        def _(pool):
            pool.memset(ident[:, :], 0.0).then_inc(ident_zero, 1)
            pool.wait_ge(ident_zero, 1)
            pool.affine_select(out=ident[:, :], in_=ident[:, :], compare_op=ALU.not_equal, fill=1.0,
                               base=0, pattern=[[-1, P]], channel_multiplier=1).then_inc(ident_made, 1)
            pool.wait_ge(cols_sb, 2)
            pool.wait_ge(in_wp, 16)
            for half in range(2):
                for c in range(CH):
                    pool.tensor_scalar(wpg[:, half, c, :], wp[:, half, c, :], gcol[:, c, half:half + 1], 1.0,
                                       ALU.mult, ALU.mult).then_inc(gain_made, 1)
            pool.wait_ge(in_rows, 64)
            pool.wait_ge(cls_made, 1)
            pool.tensor_tensor(h[0:B, NPT * D:NT * D], hcls_sum[:, :], bo_row[0:B, :], ALU.add).then_inc(cls_out, 1)
            pool.wait_ge(cls_raw, 1)
            pool.wait_ge(cls_hi, 1)
            pool.tensor_tensor(tile_cols(hT_lo, HP, 0), by_tile(hraw[:, 0, 0:DC * B]),
                               tile_cols(hT_hi, HP, 0).bitcast(F32), ALU.subtract).then_inc(cls_out, 1)

            def step(i, l):
                if l < HP and live(i, GRID, 2 * l, NPT):
                    for hp in (range(i, i + 1) if isinstance(i, int) else range(1, HP)):
                        pool.wait_ge(in_pos[hp], 32)
                    part = h[:, ds((i * GRID + 2 * l) * D, 2 * D)].rearrange("p (w d) -> p w d", d=D)
                    pool.tensor_tensor(part, part, b2_row[:, :].unsqueeze(1).to_broadcast([P, 2, D]),
                                       ALU.add).then_inc(table_made, 1)
                if live(i, GRID, l - 4, NPT):
                    r, n = (l - 4) % 2, i * GRID + (l - 4)
                    wait(pool, hnd, n + 1)
                    alone(pool, carried_pool)
                    pool.tensor_tensor(h[:, ds(n * D, D)], hn[:, r, :], bo_row[:, :], ALU.add).then_inc(hres, 1)
                if live(i, GRID, l - 5, NPT):
                    r, n = (l - 5) % 2, i * GRID + (l - 5)
                    wait(pool, hrawd, n + 1)
                    wait(pool, hhi, n + 1)
                    pool.tensor_tensor(tile_cols(hT_lo, i, l - 5), by_tile(hraw[:, r, :]),
                                       tile_cols(hT_hi, i, l - 5).bitcast(F32), ALU.subtract).then_inc(hlo, 1)

            rounds(pool, HP, GRID, 5, step)

        @block.scalar
        def _(act):
            act.dma_start(rows12[0:2, :], a["bq"].rearrange("(c p) -> c p", p=P)).then_inc(in_b, 16)
            act.dma_start(rows12[2:4, :], a["bk"].rearrange("(c p) -> c p", p=P)).then_inc(in_b, 16)
            act.dma_start(rows12[4:6, :], a["bv"].rearrange("(c p) -> c p", p=P)).then_inc(in_b, 16)
            act.dma_start(rows12[6:12, :], a["b_qkv"].rearrange("(c p) -> c p", p=P)).then_inc(in_b, 16)
            act.dma_start(rows4[0:2, :], a["ln1_g"].rearrange("(h f) -> h f", h=2)).then_inc(in_b, 16)
            act.dma_start(rows4[2:4, :], a["ln1_b"].rearrange("(h f) -> h f", h=2)).then_inc(in_b, 16)
            act.dma_start(wp[:, :, :, :],
                          a["w_proj"].rearrange("(h p c) n -> p h (c n)", h=2, c=CH).rearrange(
                              "p h (c n) -> p h c n", c=CH)).then_inc(in_wp, 16)
            for row, name in ((bp_row, "b_proj"), (g2_row, "ln2_g"), (b2_row, "ln2_b"), (bo_row, "bo")):
                act.dma_start(row[:, :], a[name].partition_broadcast(P)).then_inc(in_rows, 16)
            act.dma_start(hcls[:, 0, :], a["pos"][0, 0, :].partition_broadcast(B)).then_inc(in_cls, 16)
            act.dma_start(hcls[:, 1, :], a["cls"][0, 0, :].partition_broadcast(B)).then_inc(in_cls, 16)
            for hp in range(HP):
                for h2 in range(2):
                    s = 1 + 2 * GRID * hp + GRID * h2
                    act.dma_start(h[B * h2:B * h2 + B, hp * GRID * D:(hp + 1) * GRID * D],
                                  a["pos"][0, s:s + GRID, :].rearrange("s d -> (s d)").partition_broadcast(B)
                                  ).then_inc(in_pos[hp], 16)
            for j in range(4):
                for ic in range(DC):
                    n = DC * j + ic
                    act.wait_ge(wT_ps, n + 1)
                    dst = wo_hi[:, ic, :] if j == 3 else wqkv_hi[:, ic, j * D:(j + 1) * D]
                    act.activation(dst, ps[:, 2048 + 512 * (n % 4):2048 + 512 * (n % 4) + D], ACT.Copy).then_inc(wT_hi, 1)
            act.wait_ge(cls_ps, 1)
            act.activation(hraw[:, 0, 0:DC * B], h_bank(0)[:, 0:DC * B], ACT.Copy).then_inc(cls_raw, 1)
            act.activation(tile_cols(hT_hi, HP, 0), by_tile(h_bank(0)[:, 0:DC * B]), ACT.Copy).then_inc(cls_hi, 1)

            def step(i, l):
                if live(i, GRID, l - 1, NPT):
                    r, n = (l - 1) % 2, i * GRID + (l - 1)
                    hp, w = i + (l - 1) // GRID, (l - 1) % GRID
                    wait(act, nmud, n + 1)
                    wait(act, xT_ps, n - 1)
                    src = xs[:, ds(hp, 1), :, :].rearrange("p o c (y w q) -> p (o c) y w q", w=GRID, q=PATCH)
                    act.activation(xn[:, r, :].rearrange("p (c y q) -> p c y q", c=CH, q=PATCH), src[:, :, :, w, :],
                                   ACT.Identity, bias=nmu[:, r:r + 1], scale=rstd[:, r:r + 1]).then_inc(xnd, 1)
                if live(i, GRID, l - 2, NPT):
                    r, n = (l - 2) % 2, i * GRID + (l - 2)
                    wait(act, xT_ps, n + 1)
                    wait(act, z_ps, n - 1)
                    act.activation(xT[:, r, :], xT_bank(r), ACT.Copy).then_inc(xTd, 1)
                if live(i, GRID, l - 5, NPT):
                    r, n = (l - 5) % 2, i * GRID + (l - 5)
                    wait(act, h_ps, n + 1)
                    wait(act, hlo, n)
                    wait(act, cls_out, 2)
                    act.activation(hraw[:, r, :], h_bank(r), ACT.Copy).then_inc(hrawd, 1)
                    act.activation(tile_cols(hT_hi, i, l - 5), by_tile(h_bank(r)), ACT.Copy).then_inc(hhi, 1)
                if live(i, GRID, l - 3, NPT):
                    r, n = (l - 3) % 2, i * GRID + (l - 3)
                    wait(act, var2, n + 1)
                    wait(act, rsd2, n - 1)
                    act.activation(sd2[:, r:r + 1], ve2[:, r:r + 1], ACT.Sqrt).then_inc(sdev2, 1)
                if live(i, GRID, l, NPT):
                    r, n = l % 2, i * GRID + l
                    wait(act, vard, n + 1)
                    wait(act, rsd, n - 1)
                    act.activation(sd[:, r:r + 1], ve[:, r:r + 1], ACT.Sqrt).then_inc(sdev, 1)

            rounds(act, HP, GRID, 5, step)

        @block.tensor
        def _(pe):
            pe.wait_ge(ident_made, 1)
            pe.wait_ge(in_b, 96)
            pe.transpose(ps[:, 3584:3596], rows12[:, :], ident[0:12, 0:12])
            for c in range(CH):
                last = pe.transpose(ps[:, 3600 + 4 * c:3604 + 4 * c], rows4[:, c:FC * P // 2:CH], ident[0:4, 0:4])
            last.then_inc(cols_ps, 1)
            pe.wait_ge(in_w, 64)
            for j in range(4):
                for ic in range(DC):
                    n = DC * j + ic
                    if n == 3:
                        pe.wait_ge(cols_sb, 2)
                    wait(pe, wT_hi, n - 3)
                    wait(pe, wT_lo, n - 3)
                    for oc in range(DC):
                        o = 2048 + 512 * (n % 4) + P * oc
                        last = pe.transpose(ps[:, o:o + P], w_raw[:, j, oc, ic * P:(ic + 1) * P], ident[:, :])
                    last.then_inc(wT_ps, 1)
            pe.wait_ge(bmat_made, FC)
            pe.wait_ge(in_wp, 16)
            for f in range(FC):
                last = pe.matmul(ps[:, 0:D], bmat[:, f, :], wp[:, f // CH, f % CH, :], start=(f == 0), stop=(f == FC - 1))
            last.then_inc(zb_ps, 1)
            pe.wait_ge(cls_made, 1)
            pe.wait_ge(wT_lo, 8)
            pe.wait_ge(wT_hi, 8)
            for c in range(DC):
                last = pe.transpose(h_bank(0)[:, c * B:(c + 1) * B], hcls_sum[:, c * P:(c + 1) * P], ident[0:B, 0:B])
            last.then_inc(cls_ps, 1)
            pe.wait_ge(gain_made, FC)
            pe.wait_ge(zb_made, 1)

            def step(i, l):
                if live(i, GRID, l - 2, NPT):
                    r, n = (l - 2) % 2, i * GRID + (l - 2)
                    wait(pe, xTd, n + 1)
                    wait(pe, zsd, n - 1)
                    for f in range(FC):
                        last = pe.matmul(z_bank(r), xT[:, r, f * P:(f + 1) * P], wpg[:, f % 2, f // 2, :],
                                         start=(f == 0), stop=(f == FC - 1))
                    last.then_inc(z_ps, 1)
                if live(i, GRID, l - 1, NPT):
                    r, n = (l - 1) % 2, i * GRID + (l - 1)
                    wait(pe, xnd, n + 1)
                    wait(pe, xTd, n - 1)
                    for f in range(FC):
                        last = pe.transpose(xT_bank(r)[:, f * P:(f + 1) * P], xn[:, r, f * P:(f + 1) * P], ident[:, :])
                    last.then_inc(xT_ps, 1)
                if live(i, GRID, l - 4, NPT):
                    r, n = (l - 4) % 2, i * GRID + (l - 4)
                    wait(pe, hnd, n + 1)
                    wait(pe, hhi, n - 1)
                    wait(pe, cls_hi, 1)
                    for c in range(DC):
                        last = pe.transpose(h_bank(r)[:, c * P:(c + 1) * P], hn[:, r, c * P:(c + 1) * P], ident[:, :])
                    last.then_inc(h_ps, 1)

            rounds(pe, HP, GRID, 5, step)

        @block.vector
        def _(dve):
            dve.wait_ge(cols_ps, 1)
            dve.tensor_copy(bias_col[:, :], ps[:, 3584:3596]).then_inc(cols_sb, 1)
            dve.tensor_copy(gcol[:, :, :], ps[:, 3600:3612].rearrange("p (c f) -> p c f", f=4)).then_inc(cols_sb, 1)
            dve.wait_ge(cols_sb, 2)
            for f in range(FC):
                dve.tensor_copy(bmat[:, f, :], gcol[:, f % CH, 2 + f // CH:3 + f // CH].to_broadcast([P, P])
                                ).then_inc(bmat_made, 1)
            dve.wait_ge(in_cls, 32)
            dve.tensor_tensor(hcls_sum[:, :], hcls[:, 0, :], hcls[:, 1, :], ALU.add).then_inc(cls_made, 1)
            for j in range(4):
                for ic in range(DC):
                    n = DC * j + ic
                    hi, lo = ((wo_hi[:, ic, :], wo_lo[:, ic, :]) if j == 3 else
                              (wqkv_hi[:, ic, j * D:(j + 1) * D], wqkv_lo[:, ic, j * D:(j + 1) * D]))
                    dve.wait_ge(wT_hi, n + 1)
                    dve.tensor_tensor(lo, ps[:, 2048 + 512 * (n % 4):2048 + 512 * (n % 4) + D], hi.bitcast(F32),
                                      ALU.subtract).then_inc(wT_lo, 1)
            dve.wait_ge(zb_ps, 1)
            dve.wait_ge(in_rows, 64)
            dve.tensor_tensor(zbias[:, :], ps[:, 0:D], bp_row[:, :], ALU.add).then_inc(zb_made, 1)
            dve.wait_ge(zb_made, 1)

            def step(i, l):
                now, nrm, z, fin = (live(i, GRID, l - lag, NPT) for lag in (0, 1, 3, 4))
                n, r = i * GRID + l, l % 2
                n1, r1 = i * GRID + (l - 1), (l - 1) % 2
                n3, r3 = i * GRID + (l - 3), (l - 3) % 2
                n4, r4 = i * GRID + (l - 4), (l - 4) % 2
                if nrm:
                    wait(dve, sdev, n1 + 1)
                    wait(dve, xnd, n1 - 1)
                    dve.reciprocal(rstd[:, r1:r1 + 1], sd[:, r1:r1 + 1]).then_inc(rsd, 1)
                if fin:
                    wait(dve, sdev2, n4 + 1)
                    wait(dve, hnd, n4 - 1)
                    dve.reciprocal(rstd2[:, r4:r4 + 1], sd2[:, r4:r4 + 1]).then_inc(rsd2, 1)
                if nrm:
                    wait(dve, rsd, n1 + 1)
                    dve.tensor_scalar(nmu[:, r1:r1 + 1], mv[:, r1, 0:1], rstd[:, r1:r1 + 1], -1.0, ALU.mult,
                                      ALU.mult).then_inc(nmud, 1)
                if fin:
                    wait(dve, hnd, n4 - 1)
                    dve.scalar_tensor_tensor(out=t1[:, r4, :], in0=zs[:, r4, :], scalar=mv2[:, r4, 0:1],
                                             in1=g2_row[:, :], op0=ALU.subtract, op1=ALU.mult).then_inc(t1d, 1)
                if z:
                    wait(dve, z_ps, n3 + 1)
                    wait(dve, t1d, n3 - 1)
                    dve.tensor_tensor(zs[:, r3, :], z_bank(r3), zbias[:, :], ALU.add).then_inc(zsd, 1)
                if fin:
                    wait(dve, t1d, n4 + 1)
                    wait(dve, rsd2, n4 + 1)
                    if l % 2 == 0:
                        wait(dve, table_made, i * HP + (l - 4) // 2 + 1)
                    wait(dve, h_ps, n4 - 1)
                    wait(dve, hres, n4 - 1)
                    dve.scalar_tensor_tensor(out=hn[:, r4, :], in0=t1[:, r4, :], scalar=rstd2[:, r4:r4 + 1],
                                             in1=h[:, ds(n4 * D, D)], op0=ALU.mult, op1=ALU.add).then_inc(hnd, 1)
                if z:
                    wait(dve, zsd, n3 + 1)
                    wait(dve, aggr2, n3 - 1)
                    alone(dve, carried)
                    dve.bn_stats(stat2[:, r3, :], zs[:, r3, :]).then_inc(stat2d, 1)
                if z:
                    wait(dve, stat2d, n3 + 1)
                    alone(dve, carried)
                    dve.bn_aggr(mv2[:, r3, :], stat2[:, r3, :]).then_inc(aggr2, 1)
                if now:
                    if isinstance(i, int):
                        dve.wait_ge(in_x[i], 16 * 2 * CH)
                    elif l == 0:
                        for hp in range(1, HP):
                            dve.wait_ge(in_x[hp], 16 * 2 * CH)
                    wait(dve, aggr, n - 1)
                    alone(dve, carried)
                    src = xs[:, ds(i, 1), :, :].rearrange("p o c (y w q) -> p (o c) y w q", w=GRID, q=PATCH)
                    for c in range(CH):
                        dve.bn_stats(stat[:, r, 6 * c:6 * c + 6], src[:, c, :, l, :]).then_inc(statd, 1)
                if z:
                    wait(dve, aggr2, n3 + 1)
                    wait(dve, sdev2, n3 - 1)
                    dve.tensor_scalar(ve2[:, r3:r3 + 1], mv2[:, r3, 1:2], EPS, None, ALU.add).then_inc(var2, 1)
                if now:
                    wait(dve, statd, CH * n + CH)
                    wait(dve, nmud, n - 1)
                    alone(dve, carried)
                    dve.bn_aggr(mv[:, r, :], stat[:, r, :]).then_inc(aggr, 1)
                    wait(dve, aggr, n + 1)
                    wait(dve, sdev, n - 1)
                    dve.tensor_scalar(ve[:, r:r + 1], mv[:, r, 1:2], EPS, None, ALU.add).then_inc(vard, 1)

            rounds(dve, HP, GRID, 5, step)


def attention(nc, a, keep, first):
    hT_hi, hT_lo, ps = keep["hT_hi"], keep["hT_lo"], keep["ps"]
    wqkv_hi, wqkv_lo, ident, bias_col, attn = (keep[x] for x in ("wqkv_hi", "wqkv_lo", "ident", "bias_col", "attn"))
    tag = "a" if first else "b"
    bcol = 0 if first else 6
    PER = 2 * IG
    AHEAD = IG
    ROUNDS = UNITS // PER
    TAIL = AHEAD + 10
    FREE = 4
    CHUNKS = (2, 3, 0, 1, 4, 5)
    with phase(nc) as (ctx, taken):
        def sb(name, shape, dt=F32):
            return ctx.enter_context(nc.sbuf_tensor(name + tag, shape, dt))

        def sem(name):
            taken.append(nc.alloc_semaphore(name + tag))
            return taken[-1]

        qT = sb("qT", [P, 2, DC * GC + P])
        kT = sb("kT", [P, 2, DC * GC])
        vT = sb("vT", [P, 2, DC * 3 * GC])
        y = keep.get("y")
        ystat = sb("ystat", [P, 2, 6])
        yaggr = sb("yaggr", [P, 2, 2])
        kbd = sb("kbd", [P, 2, DC, HC, GC])
        PW = HC * NPOS + NPOS
        prob = sb("prob", [P, 4, PW])
        pT = sb("pT", [KEYROWS, 2, 3 * P])
        vbd = sb("vbd", [KEYROWS, 2, 2 * HEADS * VW])
        osb = sb("osb", [P, 2, D])
        mx = sb("mx", [P, 2, HC])
        rsum = sb("rsum", [P, 2, HEADS])
        kmask = sb("kmask", [P, HC])
        vmask3 = sb("vmask3", [KEYROWS, 3])
        vmask = sb("vmask", [KEYROWS, 2 * HEADS])
        raw = sb("raw", [P, 2, 2 * D]) if first else None

        kmask_steps, vmask_steps, vmask_made, zeros_made, ones_made = map(
            sem, ("kmask_steps", "vmask_steps", "vmask_made", "zeros_made", "ones_made"))
        qkv_ps, qkv_sb, kbd_made, s_ps, max_made, sub_made, exp_made = map(
            sem, ("qkv_ps", "qkv_sb", "kbd_made", "s_ps", "max_made", "sub_made", "exp_made"))
        pT_ps, pT_sb, v_ps, vbd_made, o_ps, rsum_made, o_made, oT_ps, oT_sb = map(
            sem, ("pT_ps", "pT_sb", "v_ps", "vbd_made", "o_ps", "rsum_made", "o_made", "oT_ps", "oT_sb"))
        y_zero, in_y, y_made, ystat_made, yaggr_made = map(sem, ("y_zero", "in_y", "y_made", "ystat_made", "yaggr_made"))
        carried, ymean_made = sem("carried_"), sem("ymean_made")
        in_exp = [sem(f"in_exp{r}") for r in range(2)]
        exp_hi, exp_lo = map(sem, ("exp_hi", "exp_lo"))

        def s_bank(r):
            return ps[:, 512 * r:512 * r + HC * NPOS]

        def pT_bank(r):
            return ps[0:KEYROWS, 1024 + 512 * r:1024 + 512 * r + 3 * P]

        def qkv_bank(i, l):
            b = 7 if isinstance(i, int) and i == 0 and l < IG and l % 2 else 4
            return ps[:, 512 * b:512 * b + GC].rearrange("p (k b) -> p k b", b=IG)

        def by_vector(i, l, c):
            return isinstance(i, int) and i == 0 and l < IG and c == 1

        v_bank = ps[0:KEYROWS, 2560:3072]
        o_bank = ps[:, 3072:3072 + HEADS * VW]
        oT_bank = ps[:, 3584:3584 + DC * P]

        block = ctx.enter_context(nc.Block())

        @block.gpsimd
        def _(pool):
            pool.memset(kmask[:, :], 1.0).then_inc(kmask_steps, 1)
            pool.wait_ge(kmask_steps, 1)
            pool.affine_select(out=kmask[:, :], in_=kmask[:, :], compare_op=ALU.is_ge, fill=0.0,
                               base=0, pattern=[[-HD, HC]], channel_multiplier=1).then_inc(kmask_steps, 1)
            pool.wait_ge(kmask_steps, 2)
            pool.affine_select(out=kmask[:, :], in_=kmask[:, :], compare_op=ALU.is_ge, fill=0.0,
                               base=HD - 1, pattern=[[HD, HC]], channel_multiplier=-1).then_inc(kmask_steps, 1)
            pool.memset(vmask3[:, :], 1.0).then_inc(vmask_steps, 1)
            pool.wait_ge(vmask_steps, 1)
            pool.affine_select(out=vmask3[:, :], in_=vmask3[:, :], compare_op=ALU.is_ge, fill=0.0,
                               base=0, pattern=[[-NPOS, 3]], channel_multiplier=1).then_inc(vmask_steps, 1)
            pool.wait_ge(vmask_steps, 2)
            pool.affine_select(out=vmask3[:, :], in_=vmask3[:, :], compare_op=ALU.is_ge, fill=0.0,
                               base=NPOS - 1, pattern=[[NPOS, 3]], channel_multiplier=-1).then_inc(vmask_steps, 1)
            pool.wait_ge(kmask_steps, 3)

            def step(i, l):
                for c in range(DC):
                    if l % IG == 1 + 2 * c and live(i, 2, l // IG, IG) and not by_vector(i, l, c):
                        g, r = 2 * i + l // IG, l // IG
                        wait(pool, qkv_sb, 6 * g + 1 + c)
                        wait(pool, s_ps, IG * (g - 1))
                        alone(pool, carried)
                        for hh in range(HC):
                            pool.tensor_scalar(kbd[:, r, c, hh, :], kT[:, r, c * GC:(c + 1) * GC],
                                               kmask[:, hh:hh + 1], 1.0, ALU.mult, ALU.mult).then_inc(kbd_made, 1)
                if not first and isinstance(i, int) and i == 0 and l == 2:
                    pool.memset(y[:, :], 0.0).then_inc(y_zero, 1)
                if first and isinstance(i, int) and i == 0 and AHEAD <= l < AHEAD + E:
                    e = l - AHEAD
                    pool.wait_ge(exp_hi, e + 1)
                    pool.tensor_tensor(keep["we_lo"][:, :, e * D:(e + 1) * D],
                                       raw[:, e % 2, :].rearrange("p (c n) -> p c n", c=DC),
                                       keep["we_hi"][:, :, e * D:(e + 1) * D].bitcast(F32), ALU.subtract
                                       ).then_inc(exp_lo, 1)

                if not first and l % 2 == 0 and live(i, PER // 2, (l - AHEAD - 6) // 2, B // 2):
                    p, r = i * (PER // 2) + (l - AHEAD - 6) // 2, ((l - AHEAD - 6) // 2) % 2
                    if isinstance(i, int) and p == 0:
                        pool.wait_ge(in_y, 64)
                    wait(pool, o_made, p + 1)
                    yp = y[:, ds(p * D, D)]
                    pool.tensor_tensor(yp, osb[:, r, :], yp, ALU.add).then_inc(y_made, 1)

            rounds(pool, ROUNDS, PER, TAIL, step)

        @block.sync
        def _(sp):
            if first:
                for e in range(E):
                    if e >= 2:
                        sp.wait_ge(exp_lo, e - 1)
                    sp.dma_start(raw[:, e % 2, :].rearrange("p (c n) -> p c n", c=DC),
                                 a["w_exp"][e].rearrange("(c p) n -> p c n", p=P)).then_inc(in_exp[e % 2], 16)
            else:
                sp.wait_ge(y_zero, 1)
                rows = y[:, :].rearrange("r (p d) -> r p d", d=D)
                left = a["left"].rearrange("(p m) s d -> m s p d", m=2)
                for im in range(2):
                    for s0, s1 in ((0, 1), (1, NPOS)):
                        sp.dma_start(rows[QPAD * im + s0:QPAD * im + s1, :, :], left[im, s0:s1, :, :]).then_inc(in_y, 16)

        @block.scalar
        def _(act):
            def step(i, l):
                if live(i, PER, l - AHEAD - 3, UNITS):
                    n, r = i * PER + (l - AHEAD - 3), (l - 3) % 2
                    wait(act, pT_ps, n + 1)
                    wait(act, o_ps, n - 1)
                    act.activation(pT[:, r, :], pT_bank(r), ACT.Copy).then_inc(pT_sb, 1)
                if l % IG < 6 and live(i, 2, l // IG, IG):
                    g, r, m, j = 2 * i + l // IG, l // IG, l % IG, CHUNKS[l % IG]
                    src = qkv_bank(i, l).rearrange("p k b -> p b k")
                    if j < 2 * DC:
                        dst = (qT, kT)[j // DC][:, r, (j % DC) * GC:(j % DC + 1) * GC].rearrange("p (b k) -> p b k", k=NPOS)
                    else:
                        dst = vT[:, r, (j % DC) * 3 * GC:(j % DC + 1) * 3 * GC].rearrange(
                            "p (b t k) -> p b t k", t=3, k=NPOS)
                        src = src.unsqueeze(2).to_broadcast([P, IG, 3, NPOS])
                    wait(act, qkv_ps, 6 * g + m + 1)
                    if j == 0:
                        wait(act, s_ps, IG * (g - 1))
                    if j == DC:
                        wait(act, kbd_made, 2 * HC * (g - 1))
                    if j == 2 * DC:
                        wait(act, v_ps, 4 * (g - 1))
                    act.activation(dst, src, ACT.Identity,
                                   bias=bias_col[:, bcol + j:bcol + j + 1]).then_inc(qkv_sb, 1)
                if first and isinstance(i, int) and i == 0 and AHEAD <= l < AHEAD + E:
                    e = l - AHEAD
                    act.wait_ge(in_exp[e % 2], 16 * (e // 2 + 1))
                    act.activation(keep["we_hi"][:, :, e * D:(e + 1) * D],
                                   raw[:, e % 2, :].rearrange("p (c n) -> p c n", c=DC), ACT.Copy).then_inc(exp_hi, 1)
                if live(i, PER, l - AHEAD, UNITS):
                    n, r = i * PER + (l - AHEAD), l % 4
                    wait(act, sub_made, n + 1)
                    p8 = prob[:, r, 0:HC * NPOS]
                    act.activation(p8, p8, ACT.Exp, scale=float(HD) ** -0.5).then_inc(exp_made, 1)
                if first and l % 2 == 0 and live(i, PER // 2, (l - AHEAD - 6) // 2, B // 2):
                    p = i * (PER // 2) + (l - AHEAD - 6) // 2
                    wait(act, oT_ps, p + 1)
                    src = oT_bank.rearrange("p (c m s) -> p c m s", c=DC, m=2)
                    dst = attn[:, 0:DC * NTOK].rearrange("p (c s b) -> p c s b", c=DC, b=B)
                    for im in range(2):
                        act.activation(dst[:, :, :, ds(2 * p + im, 1)].rearrange("p c s o -> p c (s o)"),
                                       src[:, :, im, 0:NPOS], ACT.Copy).then_inc(oT_sb, 1)

            rounds(act, ROUNDS, PER, TAIL, step)

        @block.tensor
        def _(pe):
            def step(i, l):
                if live(i, PER, l - AHEAD, UNITS):
                    n, r = i * PER + (l - AHEAD), l % 2
                    g, st, c = 2 * i + (l - AHEAD) // IG, ((l - AHEAD) // IG) % 2, l % 2
                    if isinstance(g, int) and g == 0:
                        if l % IG == 0:
                            pe.wait_ge(kbd_made, 2 * HC)
                            pe.wait_ge(zeros_made, 6)
                    elif l % IG < 2:
                        wait(pe, kbd_made, 2 * HC * g + HC * (c + 1))
                    wait(pe, sub_made, n - 1)
                    for im in range(2):
                        b = ((l % IG) // 2) * 2 + im
                        q0 = c * GC + b * NPOS
                        last = pe.matmul(s_bank(r)[QPAD * im:QPAD * im + QPAD, :], qT[:, st, q0:q0 + QPAD],
                                         kbd[:, st, c, :, b * NPOS:(b + 1) * NPOS], start=True, stop=True)
                    last.then_inc(s_ps, 1)
                if l % IG < 6 and live(i, 2, l // IG, IG):
                    g, m, j = 2 * i + l // IG, l % IG, CHUNKS[l % IG]
                    wait(pe, qkv_sb, 6 * g + m - (isinstance(i, int) and g == 0))
                    terms = [(w, x, c) for w, x in ((wqkv_hi, hT_hi), (wqkv_lo, hT_hi), (wqkv_hi, hT_lo)) for c in range(DC)]
                    for m, (w, x, c) in enumerate(terms):
                        rhs = x[:, c * NTOK:(c + 1) * NTOK].rearrange("p (s b) -> p s b", b=B)[:, :, ds(IG * g, IG)]
                        last = pe.matmul(qkv_bank(i, l), w[:, c, j * P:(j + 1) * P], rhs,
                                         start=(m == 0), stop=(m == len(terms) - 1))
                    last.then_inc(qkv_ps, 1)
                if l % 2 == 0 and live(i, PER // 2, (l - AHEAD) // 2, B // 2):
                    p, st = i * (PER // 2) + (l - AHEAD) // 2, ((l - AHEAD) // IG) % 2
                    wait(pe, vbd_made, p)
                    if l % IG == 0:
                        wait(pe, qkv_sb, 6 * (2 * i + (l - AHEAD) // IG) + 6)
                    for im in range(2):
                        b = ((l % IG) // 2) * 2 + im
                        for c in range(DC):
                            v0 = (c * IG + b) * KEYROWS
                            last = pe.transpose(v_bank[:, im * D + c * P:im * D + (c + 1) * P],
                                                vT[:, st, v0:v0 + KEYROWS], ident[:, :])
                    last.then_inc(v_ps, 1)
                if live(i, PER, l - AHEAD - 2, UNITS):
                    n, r = i * PER + (l - AHEAD - 2), (l - 2) % 2
                    wait(pe, exp_made, n + 1)
                    wait(pe, pT_sb, n - 1)
                    for t in range(3):
                        last = pe.transpose(pT_bank(r)[:, t * P:(t + 1) * P],
                                            prob[:, (l - 2) % 4, t * KEYROWS:(t + 1) * KEYROWS], ident[:, :])
                    last.then_inc(pT_ps, 1)
                if live(i, PER, l - AHEAD - 3, UNITS):
                    n, r, c = i * PER + (l - AHEAD - 3), (l - 3) % 2, (l - 3) % 2
                    p, pr = i * (PER // 2) + (l - AHEAD - 3 - c) // 2, ((l - AHEAD - 3) // 2) % 2
                    wait(pe, pT_sb, n + 1)
                    wait(pe, vbd_made, p + 1)
                    if c == 0:
                        wait(pe, o_made, p)
                    for t in range(3):
                        heads = min(3, HC - 3 * t)
                        h0 = HC * c + 3 * t
                        for im in range(2):
                            v0 = (HEADS * im + h0) * VW
                            last = pe.matmul(o_bank[QPAD * im:QPAD * im + QPAD, h0 * VW:(h0 + heads) * VW],
                                             pT[:, r, t * P + QPAD * im:t * P + QPAD * im + QPAD],
                                             vbd[:, pr, v0:v0 + heads * VW], start=True, stop=True)
                    last.then_inc(o_ps, 1)
                if first and l % 2 == 1 and live(i, PER // 2, (l - AHEAD - 5) // 2, B // 2):
                    p, r = i * (PER // 2) + (l - AHEAD - 5) // 2, ((l - AHEAD - 5) // 2) % 2
                    wait(pe, o_made, p + 1)
                    wait(pe, oT_sb, 2 * p)
                    for c in range(DC):
                        last = pe.transpose(oT_bank[:, c * P:(c + 1) * P], osb[:, r, c * P:(c + 1) * P], ident[:, :])
                    last.then_inc(oT_ps, 1)

            rounds(pe, ROUNDS, PER, TAIL, step)

        @block.vector
        def _(dve):
            for r in range(2):
                dve.memset(qT[:, r, DC * GC:DC * GC + P], 0.0).then_inc(zeros_made, 1)
            for r in range(4):
                dve.memset(prob[:, r, HC * NPOS:PW], 0.0).then_inc(zeros_made, 1)
            dve.wait_ge(kmask_steps, 3)
            dve.wait_ge(vmask_steps, 3)
            v8 = vmask[:, :].rearrange("p (g h) -> p g h", h=HC)
            for h0 in range(0, HC, 3):
                heads = min(3, HC - h0)
                dve.tensor_copy(v8[:, :, h0:h0 + heads], vmask3[:, 0:heads].unsqueeze(1).to_broadcast(
                    [KEYROWS, 2 * DC, heads])).then_inc(vmask_made, 1)
            dve.wait_ge(vmask_made, 3)
            for r in range(2):
                ones = vbd[:, r, :].rearrange("p (h v) -> p h v", v=VW)[:, :, HD:VW]
                dve.tensor_copy(ones, vmask[:, :].unsqueeze(2)).then_inc(ones_made, 1)
            dve.wait_ge(ones_made, 2)
            dve.sem_inc(yaggr_made, FREE)
            dve.sem_inc(ymean_made, FREE)

            def step(i, l):
                if l % 2 == 1 and live(i, PER // 2, (l - AHEAD - 5) // 2, B // 2):
                    p, r = i * (PER // 2) + (l - AHEAD - 5) // 2, ((l - AHEAD - 5) // 2) % 2
                    wait(dve, o_ps, 2 * p + 2)
                    wait(dve, o_made, p - 1)
                    o16 = o_bank.rearrange("p (h v) -> p h v", v=VW)
                    dve.reciprocal(rsum[:, r, :].unsqueeze(2), o16[:, :, HD:VW]).then_inc(rsum_made, 1)
                    wait(dve, rsum_made, p + 1)
                    wait(dve, oT_ps if first else y_made, p - 1)
                    dve.tensor_tensor(osb[:, r, :].rearrange("p (h v) -> p h v", v=HD), o16[:, :, 0:HD],
                                      rsum[:, r, :].unsqueeze(2).to_broadcast([P, HEADS, HD]), ALU.mult
                                      ).then_inc(o_made, 1)
                if l % 2 == 1 and live(i, PER // 2, (l - AHEAD - 1) // 2, B // 2):
                    p, r = i * (PER // 2) + (l - AHEAD - 1) // 2, ((l - AHEAD - 1) // 2) % 2
                    wait(dve, v_ps, p + 1)
                    wait(dve, o_ps, 2 * (p - 1))
                    dve.tensor_tensor(vbd[:, r, :].rearrange("p (h v) -> p h v", v=VW)[:, :, 0:HD],
                                      v_bank.rearrange("p (h v) -> p h v", v=HD),
                                      vmask[:, :].unsqueeze(2).to_broadcast([KEYROWS, 2 * HEADS, HD]), ALU.mult
                                      ).then_inc(vbd_made, 1)
                if l == 3 and by_vector(i, l, 1):
                    dve.wait_ge(qkv_sb, 2)
                    for hh in range(HC):
                        dve.tensor_scalar(kbd[:, 0, 1, hh, :], kT[:, 0, GC:2 * GC], kmask[:, hh:hh + 1], None,
                                          ALU.mult).then_inc(kbd_made, 1)
                if live(i, PER, l - AHEAD, UNITS):
                    n, r = i * PER + (l - AHEAD), l % 2
                    wait(dve, s_ps, n + 1)
                    wait(dve, sub_made, n - 1)
                    s8 = s_bank(r).rearrange("p (h k) -> p h k", k=NPOS)
                    dve.tensor_reduce(mx[:, r, :], s8, AX.X, ALU.max).then_inc(max_made, 1)
                    wait(dve, max_made, n + 1)
                    wait(dve, pT_ps, n - 3)
                    dve.tensor_tensor(prob[:, l % 4, 0:HC * NPOS].rearrange("p (h k) -> p h k", k=NPOS), s8,
                                      mx[:, r, :].unsqueeze(2).to_broadcast([P, HC, NPOS]), ALU.subtract
                                      ).then_inc(sub_made, 1)
                if not first and l % 2 == 0 and live(i, PER // 2, (l - AHEAD - 8) // 2, B // 2):
                    p, r = i * (PER // 2) + (l - AHEAD - 8) // 2, ((l - AHEAD - 8) // 2) % 2
                    wait(dve, y_made, p + 1)
                    wait(dve, yaggr_made, FREE + p - 1)
                    alone(dve, carried)
                    dve.bn_stats(ystat[:, r, :], y[:, ds(p * D, D)]).then_inc(ystat_made, 1)
                if not first and l % 2 == 1 and live(i, PER // 2, (l - AHEAD - 9) // 2, B // 2):
                    p, r = i * (PER // 2) + (l - AHEAD - 9) // 2, ((l - AHEAD - 9) // 2) % 2
                    wait(dve, ystat_made, p + 1)
                    wait(dve, ymean_made, FREE + 2 * (p - 1))
                    alone(dve, carried)
                    dve.bn_aggr(yaggr[:, r, :], ystat[:, r, :]).then_inc(yaggr_made, 1)
                    wait(dve, yaggr_made, FREE + p + 1)
                    dve.tensor_copy(keep["ymean"][:, ds(p, 1)], yaggr[:, r, 0:1]).then_inc(ymean_made, 1)
                    dve.tensor_scalar(keep["yvar"][:, ds(p, 1)], yaggr[:, r, 1:2], EPS, None, ALU.add).then_inc(ymean_made, 1)

            rounds(dve, ROUNDS, PER, TAIL, step)


def rsqrt_steps(dve, y, t, v, sem, at):
    I32 = mybir.dt.int32

    def run(k, op):
        def go():
            wait(dve, sem, at + k)
            op().then_inc(sem, 1)
        return go

    steps = [
        lambda: dve.tensor_scalar(t.bitcast(I32), v.bitcast(I32), 1, None, ALU.logical_shift_right),
        lambda: dve.tensor_scalar(y.bitcast(I32), t.bitcast(I32), -1, 0x5F3759DF, ALU.mult, ALU.add),
    ]
    for _ in range(3):
        steps += [
            lambda: dve.tensor_tensor(t, y, y, ALU.mult),
            lambda: dve.tensor_tensor(t, t, v, ALU.mult),
            lambda: dve.tensor_scalar(t, t, -0.5, 1.5, ALU.mult, ALU.add),
            lambda: dve.tensor_tensor(y, y, t, ALU.mult),
        ]
    assert len(steps) == RSQRT
    return [run(k, op) for k, op in enumerate(steps)]


RSQRT = 14


def norm_and_experts(nc, a, keep):
    h, hT_hi, hT_lo, ps, attn = (keep[x] for x in ("h", "hT_hi", "hT_lo", "ps", "attn"))
    wqkv_hi, wqkv_lo, wo_hi, wo_lo = (keep[x] for x in ("wqkv_hi", "wqkv_lo", "wo_hi", "wo_lo"))
    we_hi, we_lo, ident = keep["we_hi"], keep["we_lo"], keep["ident"]
    with phase(nc) as (ctx, taken):
        def sb(name, shape, dt=F32):
            return ctx.enter_context(nc.sbuf_tensor(name, shape, dt))

        def sem(name):
            taken.append(nc.alloc_semaphore(name))
            return taken[-1]

        w2_raw = sb("w2_raw", [P, DC, 3 * D])
        aT_hi = sb("aT_hi", [P, 2, DC * P], F32R)
        aT_lo = sb("aT_lo", [P, 2, DC * P], F32R)
        z = sb("z3", [P, 2, D])
        stat = sb("stat3", [P, 2, 6])
        mv = sb("mv3", [P, 2, 2])
        ve = sb("ve3", [P, 2])
        newt = sb("newt", [P, 2])
        rstd = sb("rstd3", [P, 2])
        nmr = sb("nmr3", [P, 2])
        hn = sb("hn3", [P, 3, D])
        tT_hi = sb("tT_hi", [P, 2, DC * P], F32R)
        tT_lo = sb("tT_lo", [P, 2, DC * P], F32R)
        wg_raw = sb("wg_raw", [P, DC, E])
        wg_hi = sb("wg_hi", [P, DC, E], F32R)
        wg_lo = sb("wg_lo", [P, DC, E], F32R)
        bg_row = sb("bg_row", [P, E])
        be = sb("be", [E, D])
        iota8 = sb("iota8", [P, E])
        lg = sb("lg", [P, 2, E])
        lmax = sb("lmax", [P, 2])
        lsub = sb("lsub", [P, 2, E])
        ge = sb("ge", [P, 2, E])
        gsum = sb("gsum", [P, 2])
        grs = sb("grs", [P, 2])
        gate = sb("gate", [P, 2, E])
        top = sb("top", [P, 2, E])
        topi = sb("topi", [P, 2, E], U32)
        topf = sb("topf", [P, 2, 2])
        pick = sb("pick", [P, 2, 2, E])
        comb = sb("comb", [P, 2, E])
        combT = sb("combT", [E, 2, P])
        scaled = sb("scaled", [P, 4, D])
        summed = sb("summed", [P, 2, D])
        direct = sb("direct", [P, 2, D])
        total = sb("total", [P, 2, D])

        carried = sem("carried3")
        in_w2, in_g, in_be, w2_hi, w2_lo, wg_h, wg_l, iota_made = map(
            sem, ("in_w2", "in_g", "in_be", "w2_hi", "w2_lo", "wg_h", "wg_l", "iota_made"))
        ahi, alo, wo_ps, zadd, statd, aggrd, vard, rsqd, nmrd = map(
            sem, ("ahi", "alo", "wo_ps", "zadd", "statd3", "aggrd", "vard3", "rsqd", "nmrd"))
        hnd, t_ps, thi, tlo, tcopy_hi, tcopy_lo, g_ps, lgd, lmaxd, lsubd, ged, grsd, gated, topd, topid, topfd, pickd, combd = map(
            sem, ("hnd3", "t_ps", "thi", "tlo", "tcopy_hi", "tcopy_lo", "g_ps", "lgd", "lmaxd", "lsubd", "ged", "grsd",
                  "gated", "topd", "topid", "topfd", "pickd", "combd"))
        cT_ps, cT_sb, be_ps, ex_ps, directd, scaledd, sumd, totald = map(
            sem, ("cT_ps", "cT_sb", "be_ps", "ex_ps", "directd", "scaledd", "sumd", "totald"))
        stored = [sem(f"stored3_{r}") for r in range(2)]

        DIRECT, SCALED = (0, 1, 4, 5), (2, 3, 6, 7)
        wo_bank = ps[:, 3584:3584 + D]
        t_bank = ps[:, 2048:2048 + D]
        g_bank = ps[:, 2560:2560 + E]
        cT_bank = ps[0:E, 2560 + 64:2560 + 64 + P]
        be_bank = ps[:, 3072:3072 + D]

        def tile(i, l, lag):
            return live(i, GRID, l - lag, NT), i * GRID + (l - lag), rows_of(i, l - lag), l - lag

        SPLIT, WO, GATE, EXPERTS, TOTAL = 0, 1, 2, 3, 4

        def cols(ap, m):
            return ap.rearrange("p (c h b) -> p c h b", c=DC, b=B)[:, :, 0:m // B, :]

        block = ctx.enter_context(nc.Block())

        @block.sync
        def _(sp):
            sp.dma_start(wg_raw[:, :, :], a["w_gate"].rearrange("(c p) e -> p c e", p=P)).then_inc(in_g, 16)
            sp.dma_start(bg_row[:, :], a["b_gate"].partition_broadcast(P)).then_inc(in_g, 16)
            sp.dma_start(be[:, :], a["b_exp"]).then_inc(in_be, 16)
            sp.dma_start(w2_raw[:, :, :], a["w_qkv"].rearrange("(c p) n -> p c n", p=P)).then_inc(in_w2, 16)

            def store(i, l):
                if live(i, GRID, l, NT):
                    r, n = l % 2, i * GRID + l
                    wait(sp, totald, n + 1)
                    if isinstance(i, int) and n == NPT:
                        sp.dma_start(a["left"][:, 0, :], total[0:B, r, :]).then_inc(stored[r], 16)
                        return
                    for h2 in range(2):
                        s = 2 * GRID * i + (1 + GRID * h2 + l)
                        sp.dma_start(a["left"][:, ds(s, 1), :].rearrange("b o d -> b (o d)"),
                                     total[B * h2:B * h2 + B, r, :]).then_inc(stored[r], 16)

            rounds(sp, HP, GRID, 1, store)
            sp.wait_ge(stored[0], 16 * (NPT + 1))
            sp.wait_ge(stored[1], 16 * NPT)

        @block.gpsimd
        def _(pool):
            pool.iota(iota8[:, :], pattern=[[1, E]], base=0, channel_multiplier=0,
                      allow_small_or_imprecise_dtypes=True).then_inc(iota_made, 1)

            def step(i, l):
                on, n, m, k = tile(i, l, SPLIT)
                if isinstance(i, int) and i == 0:
                    pool.wait_ge(w2_hi, l + 1)
                    c, cut = l % DC, slice(l // DC * D, (l // DC + 1) * D)
                    pool.tensor_tensor(wqkv_lo[:, c, cut], w2_raw[:, c, cut], wqkv_hi[:, c, cut].bitcast(F32),
                                       ALU.subtract).then_inc(w2_lo, 1)
                if on:
                    r = k % 2
                    wait(pool, ahi, n + 1)
                    wait(pool, wo_ps, n - 1)
                    pool.tensor_tensor(cols(aT_lo[:, r, :], m), tile_cols(attn, i, k),
                                       cols(aT_hi[:, r, :], m).bitcast(F32), ALU.subtract).then_inc(alo, 1)
                on2, n2, m2, k2 = tile(i, l, EXPERTS)
                on1, n1, m1, k1 = tile(i, l, GATE)

                def add_scaled(q):
                    r = k2 % 2
                    wait(pool, scaledd, 4 * n2 + q + 1)
                    if q == 0:
                        wait(pool, totald, n2 - 1)
                    else:
                        wait(pool, sumd, 4 * n2 + q)
                    src = hn[0:m2, k2 % 3, :] if q == 0 else summed[0:m2, r, :]
                    pool.tensor_tensor(summed[0:m2, r, :], src, scaled[0:m2, q, :], ALU.add).then_inc(sumd, 1)

                if on2:
                    add_scaled(0)
                    add_scaled(1)
                if on1:
                    wait(pool, thi, n1 + 1)
                    pool.tensor_copy(tile_cols(hT_hi, i, k1), cols(tT_hi[:, k1 % 2, :], m1)).then_inc(tcopy_hi, 1)
                if on2:
                    add_scaled(2)
                if on1:
                    wait(pool, tlo, n1 + 1)
                    pool.tensor_copy(tile_cols(hT_lo, i, k1), cols(tT_lo[:, k1 % 2, :], m1)).then_inc(tcopy_lo, 1)
                if on2:
                    add_scaled(3)

            rounds(pool, HP, GRID, EXPERTS + 1, step)

        @block.scalar
        def _(act):
            def step(i, l):
                on, n, m, k = tile(i, l, SPLIT)
                on1, n1, m1, k1 = tile(i, l, GATE)
                on2, n2, m2, k2 = tile(i, l, EXPERTS)
                if isinstance(i, int) and i == 0:
                    act.wait_ge(in_w2, 16)
                    c, cut = l % DC, slice(l // DC * D, (l // DC + 1) * D)
                    act.activation(wqkv_hi[:, c, cut], w2_raw[:, c, cut], ACT.Copy).then_inc(w2_hi, 1)
                if on:
                    wait(act, alo, n - 1)
                    wait(act, wo_ps, n - 1)
                    act.activation(cols(aT_hi[:, k % 2, :], m), tile_cols(attn, i, k), ACT.Copy).then_inc(ahi, 1)
                if on1:
                    wait(act, t_ps, n1 + 1)
                    wait(act, ex_ps, 4 * (n1 - 1))
                    wait(act, tcopy_hi, n1 - 1)
                    act.activation(cols(tT_hi[:, k1 % 2, :], m1), cols(t_bank, m1), ACT.Copy).then_inc(thi, 1)

                def scale(q):
                    e = SCALED[q]
                    wait(act, ex_ps, 4 * n2 + e // 2 + 1)
                    wait(act, sumd, 4 * (n2 - 1) + q + 1)
                    act.activation(scaled[0:m2, q, :], ps[0:m2, D * e:D * (e + 1)], ACT.Copy,
                                   scale=comb[0:m2, k2 % 2, e:e + 1]).then_inc(scaledd, 1)

                if on2:
                    wait(act, cT_ps, n2 + 1)
                    wait(act, be_ps, n2 - 1)
                    act.activation(combT[:, k2 % 2, 0:m2], cT_bank[:, 0:m2], ACT.Copy).then_inc(cT_sb, 1)
                if on1:
                    wait(act, lsubd, n1 + 1)
                    wait(act, gated, n1 - 1)
                    act.activation(ge[0:m1, k1 % 2, :], lsub[0:m1, k1 % 2, :], ACT.Exp,
                                   accum_out=gsum[0:m1, k1 % 2:k1 % 2 + 1]).then_inc(ged, 1)
                if on2:
                    wait(act, combd, n2 + 1)
                    scale(0)
                    scale(1)
                on, n, m, k = tile(i, l, WO)
                if on:
                    r = k % 2
                    wait(act, nmrd, n + 1)
                    wait(act, sumd, 4 * (n - 3) + 1)
                    act.activation(hn[0:m, k % 3, :], z[0:m, r, :], ACT.Identity, bias=nmr[0:m, r:r + 1],
                                   scale=rstd[0:m, r:r + 1]).then_inc(hnd, 1)
                if on2:
                    scale(2)
                    scale(3)

            act.wait_ge(in_g, 32)
            act.activation(wg_hi[:, :, :], wg_raw[:, :, :], ACT.Copy).then_inc(wg_h, 1)
            rounds(act, HP, GRID, EXPERTS + 1, step)

        @block.tensor
        def _(pe):
            pe.wait_ge(wg_l, 1)
            pe.wait_ge(in_be, 16)

            def product(out, x, r, m, pair, w0, w1, sem):
                hi, lo = x
                whi, wlo = pair
                terms = [(xx, ww, c) for xx, ww in ((hi, whi), (hi, wlo), (lo, whi)) for c in range(DC)]
                for j, (xx, ww, c) in enumerate(terms):
                    last = pe.matmul(out, xx[:, r, c * P:c * P + m], ww[:, c, w0:w1], start=(j == 0),
                                     stop=(j == len(terms) - 1))
                last.then_inc(sem, 1)

            def step(i, l):
                on, n, m, k = tile(i, l, WO)
                on1, n1, m1, k1 = tile(i, l, GATE)
                on2, n2, m2, k2 = tile(i, l, EXPERTS)

                def experts(q):
                    if q % 2 == 0:
                        wait(pe, directd, 5 * (n2 - 1) + q + 2)
                    else:
                        wait(pe, scaledd, 4 * (n2 - 1) + q + 1)
                    product(ps[0:m2, 512 * q:512 * (q + 1)], (tT_hi, tT_lo), k2 % 2, m2, (we_hi, we_lo),
                            2 * D * q, 2 * D * (q + 1), ex_ps)

                if on:
                    wait(pe, alo, n + 1)
                    wait(pe, zadd, n)
                    product(wo_bank[0:m, :], (aT_hi, aT_lo), k % 2, m, (wo_hi, wo_lo), 0, D, wo_ps)
                if on1:
                    wait(pe, hnd, n1 + 1)
                    wait(pe, thi, n1)
                    wait(pe, tlo, n1)
                    for c in range(DC):
                        last = pe.transpose(t_bank[:, c * P:c * P + m1], hn[0:m1, k1 % 3, c * P:(c + 1) * P],
                                            ident[0:m1, 0:m1])
                    last.then_inc(t_ps, 1)
                if on2:
                    wait(pe, combd, n2 + 1)
                    wait(pe, lgd, n2 + 1)
                    pe.transpose(cT_bank[:, 0:m2], comb[0:m2, k2 % 2, :], ident[0:m2, 0:m2]).then_inc(cT_ps, 1)
                    experts(0)
                if on1:
                    wait(pe, thi, n1 + 1)
                    wait(pe, tlo, n1 + 1)
                    wait(pe, cT_sb, n1)
                    product(g_bank[0:m1, :], (tT_hi, tT_lo), k1 % 2, m1, (wg_hi, wg_lo), 0, E, g_ps)
                if on2:
                    experts(1)
                    wait(pe, cT_sb, n2 + 1)
                    wait(pe, directd, 5 * n2)
                    pe.matmul(be_bank[0:m2, :], combT[:, k2 % 2, 0:m2], be[:, :], start=True, stop=True).then_inc(be_ps, 1)
                    experts(2)
                    experts(3)

            rounds(pe, HP, GRID, EXPERTS + 1, step)

        @block.vector
        def _(dve):
            dve.wait_ge(wg_h, 1)
            dve.tensor_tensor(wg_lo[:, :, :], wg_raw[:, :, :], wg_hi[:, :, :].bitcast(F32), ALU.subtract).then_inc(wg_l, 1)
            dve.wait_ge(iota_made, 1)

            def step(i, l):
                on, n, m, k = tile(i, l, WO)
                on1, n1, m1, k1 = tile(i, l, GATE)
                on2, n2, m2, k2 = tile(i, l, EXPERTS)
                r, r1, r2 = k % 2, k1 % 2, k2 % 2

                def add_direct(q):
                    acc = direct[0:m2, r2, :]
                    if q == 0:
                        wait(dve, combd, n2 + 1)
                        wait(dve, totald, n2 - 1)
                    else:
                        wait(dve, directd, 5 * n2 + q)
                    if q == 4:
                        wait(dve, be_ps, n2 + 1)
                        dve.tensor_tensor(acc, be_bank[0:m2, :], acc, ALU.add).then_inc(directd, 1)
                        return
                    e = DIRECT[q]
                    wait(dve, ex_ps, 4 * n2 + e // 2 + 1)
                    src, w = ps[0:m2, D * e:D * (e + 1)], comb[0:m2, r2, e:e + 1]
                    if q == 0:
                        dve.tensor_scalar(acc, src, w, None, ALU.mult).then_inc(directd, 1)
                    else:
                        dve.scalar_tensor_tensor(out=acc, in0=src, scalar=w, in1=acc, op0=ALU.mult,
                                                 op1=ALU.add).then_inc(directd, 1)

                if on1:
                    wait(dve, thi, n1 + 1)
                    wait(dve, ex_ps, 4 * (n1 - 1))
                    wait(dve, tcopy_lo, n1 - 1)
                    dve.tensor_tensor(cols(tT_lo[:, r1, :], m1), cols(t_bank, m1), cols(tT_hi[:, r1, :], m1).bitcast(F32),
                                      ALU.subtract).then_inc(tlo, 1)
                if on:
                    wait(dve, wo_ps, n + 1)
                    wait(dve, hnd, n - 1)
                    dve.tensor_tensor(z[0:m, r, :], wo_bank[0:m, :], h[0:m, ds(n * D, D)], ALU.add).then_inc(zadd, 1)
                    wait(dve, zadd, n + 1)
                    wait(dve, aggrd, n - 1)
                    alone(dve, carried)
                    dve.bn_stats(stat[0:m, r, :], z[0:m, r, :]).then_inc(statd, 1)
                if on:
                    wait(dve, statd, n + 1)
                    wait(dve, nmrd, n - 1)
                    alone(dve, carried)
                    dve.bn_aggr(mv[0:m, r, :], stat[0:m, r, :]).then_inc(aggrd, 1)
                    wait(dve, aggrd, n + 1)
                    dve.tensor_scalar(ve[0:m, r:r + 1], mv[0:m, r, 1:2], EPS, None, ALU.add).then_inc(vard, 1)
                    wait(dve, vard, n + 1)
                    wait(dve, hnd, n - 1)
                    root = rsqrt_steps(dve, rstd[0:m, r:r + 1], newt[0:m, r:r + 1], ve[0:m, r:r + 1], rsqd, RSQRT * n)
                else:
                    root = []

                def newton(count):
                    for _ in range(count if root else 0):
                        root.pop(0)()

                newton(1)
                if on2:
                    add_direct(0)
                newton(1)
                if on2:
                    add_direct(1)
                newton(1)
                if on1:
                    wait(dve, g_ps, n1 + 1)
                    wait(dve, lsubd, n1 - 1)
                    dve.tensor_tensor(lg[0:m1, r1, :], g_bank[0:m1, :], bg_row[0:m1, :], ALU.add).then_inc(lgd, 1)
                newton(1)
                if on1:
                    wait(dve, lgd, n1 + 1)
                    dve.tensor_reduce(lmax[0:m1, r1:r1 + 1], lg[0:m1, r1, :], AX.X, ALU.max).then_inc(lmaxd, 1)
                newton(1)
                if on1:
                    wait(dve, lmaxd, n1 + 1)
                    wait(dve, ged, n1 - 1)
                    dve.tensor_scalar(lsub[0:m1, r1, :], lg[0:m1, r1, :], lmax[0:m1, r1:r1 + 1], None,
                                      ALU.subtract).then_inc(lsubd, 1)
                newton(2)
                if on1:
                    wait(dve, ged, n1 + 1)
                    dve.reciprocal(grs[0:m1, r1:r1 + 1], gsum[0:m1, r1:r1 + 1]).then_inc(grsd, 1)
                newton(1)
                if on1:
                    wait(dve, grsd, n1 + 1)
                    dve.tensor_scalar(gate[0:m1, r1, :], ge[0:m1, r1, :], grs[0:m1, r1:r1 + 1], None,
                                      ALU.mult).then_inc(gated, 1)
                newton(1)
                if on1:
                    wait(dve, gated, n1 + 1)
                    alone(dve, carried)
                    dve.max(top[0:m1, r1, :], gate[0:m1, r1, :]).then_inc(topd, 1)
                newton(1)
                if on1:
                    wait(dve, topd, n1 + 1)
                    alone(dve, carried)
                    dve.max_index(topi[0:m1, r1, :], top[0:m1, r1, :], gate[0:m1, r1, :]).then_inc(topid, 1)
                newton(1)
                if on1:
                    wait(dve, topid, n1 + 1)
                    dve.tensor_copy(topf[0:m1, r1, :], topi[0:m1, r1, 0:2]).then_inc(topfd, 1)
                newton(2)
                on4, n4, m4, k4 = tile(i, l, TOTAL)
                if on4:
                    r4 = k4 % 2
                    wait(dve, directd, 5 * n4 + 5)
                    wait(dve, sumd, 4 * n4 + 4)
                    wait(dve, stored[r4], 32 * (i * HP + k4 // 2))
                    dve.tensor_tensor(total[0:m4, r4, :], direct[0:m4, r4, :], summed[0:m4, r4, :], ALU.add).then_inc(totald, 1)
                newton(1)
                if on1:
                    wait(dve, topfd, n1 + 1)
                    for t in range(2):
                        dve.tensor_scalar(pick[0:m1, r1, t, :], iota8[0:m1, :], topf[0:m1, r1, t:t + 1],
                                          top[0:m1, r1, t:t + 1], ALU.is_equal, ALU.mult).then_inc(pickd, 1)
                if on:
                    wait(dve, rsqd, RSQRT * n + RSQRT)
                    dve.tensor_scalar(nmr[0:m, r:r + 1], mv[0:m, r, 0:1], rstd[0:m, r:r + 1], -1.0, ALU.mult,
                                      ALU.mult).then_inc(nmrd, 1)
                if on1:
                    wait(dve, pickd, 2 * n1 + 2)
                    wait(dve, cT_ps, n1 - 1)
                    wait(dve, scaledd, 4 * (n1 - 1))
                    dve.tensor_tensor(comb[0:m1, r1, :], pick[0:m1, r1, 0, :], pick[0:m1, r1, 1, :], ALU.add).then_inc(combd, 1)
                if on2:
                    add_direct(2)
                    add_direct(3)
                    add_direct(4)

            rounds(dve, HP, GRID, TOTAL + 1, step)


def last_norm(nc, a, keep):
    y, mean, var = keep["y"], keep["ymean"], keep["yvar"]
    NP, PARTS = B // 2, 4
    with phase(nc) as (ctx, taken):
        def sb(name, shape, dt=F32):
            return ctx.enter_context(nc.sbuf_tensor(name, shape, dt))

        def sem(name):
            taken.append(nc.alloc_semaphore(name))
            return taken[-1]

        sd = sb("sd4", [P, NP])
        rstd = sb("rstd4", [P, NP])
        nmr = sb("nmr4", [P, NP])
        sdev, rsd, nmrd, stored = map(sem, ("sdev4", "rsd4", "nmrd4", "stored"))
        yd = [sem(f"yd{k}") for k in range(2)]
        block = ctx.enter_context(nc.Block())

        @block.vector
        def _(dve):
            dve.wait_ge(sdev, 1)
            dve.reciprocal(rstd[:, :], sd[:, :]).then_inc(rsd, 1)
            dve.wait_ge(rsd, 1)
            dve.scalar_tensor_tensor(out=nmr[:, :], in0=mean[:, :], scalar=-1.0, in1=rstd[:, :],
                                     op0=ALU.mult, op1=ALU.mult).then_inc(nmrd, 1)
            dve.wait_ge(nmrd, 1)
            for p in range(NP):
                if p % 2 == 0:
                    yp = y[:, p * D:(p + 1) * D]
                    dve.tensor_scalar(yp, yp, rstd[:, p:p + 1], nmr[:, p:p + 1], ALU.mult, ALU.add).then_inc(yd[0], 1)

        @block.scalar
        def _(act):
            act.activation(sd[:, :], var[:, :], ACT.Sqrt).then_inc(sdev, 1)
            act.wait_ge(nmrd, 1)
            for p in range(NP):
                if p % 2 == 1:
                    yp = y[:, p * D:(p + 1) * D]
                    act.activation(yp, yp, ACT.Identity, bias=nmr[:, p:p + 1], scale=rstd[:, p:p + 1]).then_inc(yd[1], 1)

        @block.sync
        def _(sp):
            rows = y[:, :].rearrange("r (p d) -> r p d", d=D)
            out = a["out"].rearrange("(p m) s d -> m s p d", m=2)
            for part in range(PARTS):
                p0, p1 = part * NP // PARTS, (part + 1) * NP // PARTS
                for k in range(2):
                    sp.wait_ge(yd[k], p1 // 2)
                for im in range(2):
                    sp.dma_start(out[im, 1:NPOS, p0:p1, :], rows[QPAD * im + 1:QPAD * im + NPOS, p0:p1, :]).then_inc(stored, 16)
            for im in range(2):
                sp.dma_start(out[im, 0:1, :, :], rows[QPAD * im:QPAD * im + 1, :, :]).then_inc(stored, 16)
            sp.wait_ge(stored, 16 * (2 * PARTS + 2))


def vit_layer(nc, a):
    with ExitStack() as ctx:
        def sb(name, shape, dt=F32):
            return ctx.enter_context(nc.sbuf_tensor(name, shape, dt))

        keep = {
            "h": sb("h", [P, NT * D]),
            "hT_hi": sb("hT_hi", [P, DC * NTOK], F32R),
            "hT_lo": sb("hT_lo", [P, DC * NTOK], F32R),
            "wqkv_hi": sb("wqkv_hi", [P, DC, 3 * D], F32R),
            "wqkv_lo": sb("wqkv_lo", [P, DC, 3 * D], F32R),
            "wo_hi": sb("wo_hi", [P, DC, D], F32R),
            "wo_lo": sb("wo_lo", [P, DC, D], F32R),
            "ident": sb("ident", [P, P]),
            "bias_col": sb("bias_col", [P, 12]),
            "ps": ctx.enter_context(nc.psum_tensor("ps", [P, 8 * 512], F32)),
        }
        patch_tokens(nc, a, keep)
        with ExitStack() as inner:
            keep["attn"] = inner.enter_context(nc.sbuf_tensor("attn", [P, DC * NTOK], F32))
            keep["we_hi"] = inner.enter_context(nc.sbuf_tensor("we_hi", [P, DC, E * D], F32R))
            keep["we_lo"] = inner.enter_context(nc.sbuf_tensor("we_lo", [P, DC, E * D], F32R))
            attention(nc, a, keep, True)
            norm_and_experts(nc, a, keep)
        keep["y"] = sb("y", [P, B // 2 * D])
        keep["ymean"] = sb("ymean", [P, B // 2])
        keep["yvar"] = sb("yvar", [P, B // 2])
        attention(nc, a, keep, False)
        last_norm(nc, a, keep)


_INS = {"x": "x", "L0_tok_ln1_g": "ln1_g", "L0_tok_ln1_b": "ln1_b", "L0_tok_W_proj": "w_proj",
        "L0_tok_b_proj": "b_proj", "L0_tok_ln2_g": "ln2_g", "L0_tok_ln2_b": "ln2_b", "L0_tok_cls_token": "cls",
        "L0_tok_pos_emb": "pos", "L0_attn_Wq": "wq", "L0_attn_bq": "bq", "L0_attn_Wk": "wk", "L0_attn_bk": "bk",
        "L0_attn_Wv": "wv", "L0_attn_bv": "bv", "L0_attn_Wo": "wo", "L0_attn_bo": "bo", "L0_ffn_W_qkv": "w_qkv",
        "L0_ffn_b_qkv": "b_qkv", "L0_ffn_W_gate": "w_gate", "L0_ffn_b_gate": "b_gate",
        "L0_ffn_W_experts": "w_exp", "L0_ffn_b_experts": "b_exp"}


def kernel(**inputs):
    import numpy as _np
    import concourse.bacc as _bacc
    from concourse import mybir as _mybir
    from concourse.bass_utils import run_bass_kernel_spmd as _run

    nc = _bacc.Bacc("TRN2", target_bir_lowering=False, num_devices=1)
    arrays, args = {}, {}
    for name, short in _INS.items():
        arr = _np.ascontiguousarray(inputs[name])
        arrays[f"in_{name}_dram"] = arr
        args[short] = nc.dram_tensor(f"in_{name}_dram", arr.shape, _mybir.dt.from_np(arr.dtype),
                                     kind="ExternalInput").ap()
    args["out"] = nc.dram_tensor("out_0_dram", (B, NPOS, D), _mybir.dt.float32, kind="ExternalOutput").ap()
    args["left"] = nc.dram_tensor("left", (B, NPOS, D), _mybir.dt.float32, kind="Internal").ap()
    vit_layer(nc, args)
    r = _run(nc, [arrays], core_ids=[0])
    return r.results[0]["out_0_dram"]
```

```python
from contextlib import ExitStack, contextmanager

import concourse.bass as bass
from concourse import mybir

F32 = mybir.dt.float32
F32R = mybir.dt.float32r
U32 = mybir.dt.uint32
ALU = mybir.AluOpType
ACT = mybir.ActivationFunctionType
AX = mybir.AxisListType

P = 128
B, CH, IMG = 64, 3, 96
PATCH = 16
GRID = IMG // PATCH
D = 256
DC = D // P
HEADS, HD = 16, 16
E = 8
EPS = 1e-5
NPOS = GRID * GRID + 1
NPT = GRID * GRID // 2
NT = NPT + 1
NTOK = NPOS * B
HP = GRID // 2
ROWPIX = PATCH * IMG
FC = CH * PATCH * PATCH // P

IG = 8
GC = IG * NPOS
HC = HEADS // DC
UNITS = B // 2 * DC
KEYROWS = 3 * NPOS
VW = HD + 1
QPAD = 64


@contextmanager
def phase(nc):
    taken = []
    with ExitStack() as ctx:
        yield ctx, taken
    nc.clear_and_free_semaphores(taken)
    nc.all_engine_barrier()


def ds(start, size):
    return bass.ds(start, size)


def wait(eng, sem, value):
    if not isinstance(value, int):
        assert bass.sinput_min_value(value) > 0
    if not isinstance(value, int) or value > 0:
        eng.wait_ge(sem, value)


def alone(eng, sem):
    eng.sem_inc(sem, 1)


def live(i, per, l, total):
    return 0 <= i * per + l < total if isinstance(i, int) else True


def rounds(eng, trips, per, tail, step):
    for l in range(per):
        step(0, l)
    with eng.Fori(1, trips) as i:
        for l in range(per):
            step(i, l)
    for l in range(tail):
        step(trips, l)


def tile_cols(buf, i, l):
    v = buf[:, 0:DC * NTOK].rearrange("p (c s b) -> p c s b", c=DC, b=B)
    if isinstance(i, int) and i * GRID + l == NPT:
        return v[:, :, 0:1, :]
    v = v[:, :, 1:NPOS, :].rearrange("p c (y h w) b -> p c y h w b", h=2, w=GRID)
    return v[:, :, ds(i + l // GRID, 1), :, l % GRID, :].rearrange("p c y h b -> p c (y h) b")


def by_tile(ap):
    return ap.rearrange("p (c h b) -> p c h b", c=DC, b=B)


STORED_FREE = 32


def rows_of(i, l, per=GRID):
    return B if isinstance(i, int) and i * per + l == NT - 1 else P


def patch_tokens(nc, a, keep):
    h, hT_hi, hT_lo, ps = keep["h"], keep["hT_hi"], keep["hT_lo"], keep["ps"]
    wqkv_hi, wqkv_lo, wo_hi, wo_lo = keep["wqkv_hi"], keep["wqkv_lo"], keep["wo_hi"], keep["wo_lo"]
    ident, bias_col = keep["ident"], keep["bias_col"]
    with phase(nc) as (ctx, taken):
        def sb(name, shape, dt=F32):
            return ctx.enter_context(nc.sbuf_tensor(name, shape, dt))

        def sem(name):
            taken.append(nc.alloc_semaphore(name))
            return taken[-1]

        xs = sb("xs", [P, HP, CH, ROWPIX])
        xn = sb("xn", [P, 2, CH * PATCH * PATCH])
        xT = sb("xT", [P, 2, FC * P])
        zs = sb("zs", [P, 2, D])
        t1 = sb("t1", [P, 2, D])
        hn = sb("hn", [P, 2, D])
        hraw = sb("hraw", [P, 2, D])
        hcls = sb("hcls", [B, 2, D])
        hcls_sum = sb("hcls_sum", [B, D])
        w_raw = sb("w_raw", [P, 4, DC, D])
        wp = sb("wp", [P, 2, CH, D])
        wpg = sb("wpg", [P, 2, CH, D])
        rows12 = sb("rows12", [12, P])
        rows4 = sb("rows4", [4, FC * P // 2])
        gcol = sb("gcol", [P, CH, 4])
        bmat = sb("bmat", [P, FC, P])
        bp_row = sb("bp_row", [P, D])
        zbias = sb("zbias", [P, D])
        g2_row = sb("g2_row", [P, D])
        b2_row = sb("b2_row", [P, D])
        bo_row = sb("bo_row", [P, D])
        stat = sb("stat", [P, 2, CH * 6])
        mv = sb("mv", [P, 2, 2])
        ve = sb("ve", [P, 2])
        sd = sb("sd", [P, 2])
        rstd = sb("rstd", [P, 2])
        nmu = sb("nmu", [P, 2])
        stat2 = sb("stat2", [P, 2, 6])
        mv2 = sb("mv2", [P, 2, 2])
        ve2 = sb("ve2", [P, 2])
        sd2 = sb("sd2", [P, 2])
        rstd2 = sb("rstd2", [P, 2])

        in_x = [sem(f"in_x{r}") for r in range(HP)]
        in_pos = [sem(f"in_pos{r}") for r in range(HP)]
        in_cls, in_rows, in_b, in_w, in_wp = map(sem, ("in_cls", "in_rows", "in_b", "in_w", "in_wp"))
        ident_zero, ident_made, cols_ps, cols_sb = map(sem, ("ident_zero", "ident_made", "cols_ps", "cols_sb"))
        wT_ps, wT_hi, wT_lo, bmat_made, zb_ps, zb_made, gain_made = map(
            sem, ("wT_ps", "wT_hi", "wT_lo", "bmat_made", "zb_ps", "zb_made", "gain_made"))
        table_made, cls_made, cls_ps, cls_raw, cls_hi, cls_out = map(
            sem, ("table_made", "cls_made", "cls_ps", "cls_raw", "cls_hi", "cls_out"))
        carried, carried_pool = sem("carried"), sem("carried_pool")
        statd, aggr, vard, sdev, rsd, nmud, xnd, xT_ps, xTd = map(
            sem, ("statd", "aggr", "vard", "sdev", "rsd", "nmud", "xnd", "xT_ps", "xTd"))
        z_ps, zsd, stat2d, aggr2, var2, sdev2, rsd2, t1d, hnd, h_ps, hrawd, hhi, hlo, hres = map(
            sem, ("z_ps", "zsd", "stat2d", "aggr2", "var2", "sdev2", "rsd2", "t1d", "hnd", "h_ps", "hrawd",
                  "hhi", "hlo", "hres"))

        def xT_bank(r):
            return ps[:, 1024 * r:1024 * r + FC * P]

        def z_bank(r):
            return ps[:, 2048 + 512 * r:2048 + 512 * r + D]

        def h_bank(r):
            return ps[:, 3072 + 512 * r:3072 + 512 * r + D]

        def w_bank(n):
            return ps[:, 3072 + 512 * (n % 2):3072 + 512 * (n % 2) + D]

        def turned(n):
            j, ic = n // DC, n % DC
            if j == 3:
                return wo_hi[:, ic, :], wo_lo[:, ic, :]
            return wqkv_hi[:, ic, j * D:(j + 1) * D], wqkv_lo[:, ic, j * D:(j + 1) * D]

        def weights_of(l):
            return range(2 * l, 2 * l + 2) if l < 4 else ()

        block = ctx.enter_context(nc.Block())

        @block.sync
        def _(sp):
            sp.dma_start(rows12[0:2, :], a["bq"].rearrange("(c p) -> c p", p=P)).then_inc(in_b, 16)
            sp.dma_start(rows12[2:4, :], a["bk"].rearrange("(c p) -> c p", p=P)).then_inc(in_b, 16)
            sp.dma_start(rows12[4:6, :], a["bv"].rearrange("(c p) -> c p", p=P)).then_inc(in_b, 16)
            sp.dma_start(rows12[6:12, :], a["b_qkv"].rearrange("(c p) -> c p", p=P)).then_inc(in_b, 16)
            sp.dma_start(rows4[0:2, :], a["ln1_g"].rearrange("(h f) -> h f", h=2)).then_inc(in_b, 16)
            sp.dma_start(rows4[2:4, :], a["ln1_b"].rearrange("(h f) -> h f", h=2)).then_inc(in_b, 16)
            for hp in range(HP):
                for c in range(CH):
                    for h2 in range(2):
                        r0 = PATCH * (2 * hp + h2)
                        sp.dma_start(xs[B * h2:B * h2 + B, hp, c, :],
                                     a["x"][:, c, r0:r0 + PATCH, :].rearrange("b r q -> b (r q)")).then_inc(in_x[hp], 16)
                if hp == 0:
                    for j, name in enumerate(("wq", "wk", "wv", "wo")):
                        sp.dma_start(w_raw[:, j, :, :], a[name].rearrange("(c p) n -> p c n", p=P)).then_inc(in_w, 16)
                for h2 in range(2):
                    s = 1 + 2 * GRID * hp + GRID * h2
                    sp.dma_start(h[B * h2:B * h2 + B, hp * GRID * D:(hp + 1) * GRID * D],
                                  a["pos"][0, s:s + GRID, :].rearrange("s d -> (s d)").partition_broadcast(B)
                                  ).then_inc(in_pos[hp], 16)
        @block.gpsimd
        def _(pool):
            pool.memset(ident[:, :], 0.0).then_inc(ident_zero, 1)
            pool.wait_ge(ident_zero, 1)
            pool.affine_select(out=ident[:, :], in_=ident[:, :], compare_op=ALU.not_equal, fill=1.0,
                               base=0, pattern=[[-1, P]], channel_multiplier=1).then_inc(ident_made, 1)
            pool.wait_ge(cols_sb, 2)
            pool.wait_ge(in_wp, 16)
            for half in range(2):
                for c in range(CH):
                    pool.tensor_scalar(wpg[:, half, c, :], wp[:, half, c, :], gcol[:, c, half:half + 1], 1.0,
                                       ALU.mult, ALU.mult).then_inc(gain_made, 1)
            pool.wait_ge(in_rows, 64)

            def step(i, l):
                if l < HP and live(i, GRID, 2 * l, NPT):
                    for hp in (range(i, i + 1) if isinstance(i, int) else range(1, HP)):
                        pool.wait_ge(in_pos[hp], 32)
                    part = h[:, ds((i * GRID + 2 * l) * D, 2 * D)].rearrange("p (w d) -> p w d", d=D)
                    pool.tensor_tensor(part, part, b2_row[:, :].unsqueeze(1).to_broadcast([P, 2, D]),
                                       ALU.add).then_inc(table_made, 1)
                if isinstance(i, int) and i == 0 and l == 4:
                    pool.wait_ge(cls_made, 1)
                    pool.tensor_tensor(h[0:B, NPT * D:NT * D], hcls_sum[:, :], bo_row[0:B, :], ALU.add).then_inc(cls_out, 1)
                    pool.wait_ge(cls_raw, 1)
                    pool.wait_ge(cls_hi, 1)
                    pool.tensor_tensor(tile_cols(hT_lo, HP, 0), by_tile(hraw[:, 0, 0:DC * B]),
                                       tile_cols(hT_hi, HP, 0).bitcast(F32), ALU.subtract).then_inc(cls_out, 1)
                if live(i, GRID, l - 4, NPT):
                    r, n = (l - 4) % 2, i * GRID + (l - 4)
                    wait(pool, hnd, n + 1)
                    alone(pool, carried_pool)
                    pool.tensor_tensor(h[:, ds(n * D, D)], hn[:, r, :], bo_row[:, :], ALU.add).then_inc(hres, 1)
                if live(i, GRID, l - 5, NPT):
                    r, n = (l - 5) % 2, i * GRID + (l - 5)
                    wait(pool, hrawd, n + 1)
                    wait(pool, hhi, n + 1)
                    pool.tensor_tensor(tile_cols(hT_lo, i, l - 5), by_tile(hraw[:, r, :]),
                                       tile_cols(hT_hi, i, l - 5).bitcast(F32), ALU.subtract).then_inc(hlo, 1)

            rounds(pool, HP, GRID, 5, step)

        @block.scalar
        def _(act):
            act.dma_start(wp[:, :, :, :],
                          a["w_proj"].rearrange("(h p c) n -> p h (c n)", h=2, c=CH).rearrange(
                              "p h (c n) -> p h c n", c=CH)).then_inc(in_wp, 16)
            for row, name in ((bp_row, "b_proj"), (g2_row, "ln2_g"), (b2_row, "ln2_b"), (bo_row, "bo")):
                act.dma_start(row[:, :], a[name].partition_broadcast(P)).then_inc(in_rows, 16)
            act.dma_start(hcls[:, 0, :], a["pos"][0, 0, :].partition_broadcast(B)).then_inc(in_cls, 16)
            act.dma_start(hcls[:, 1, :], a["cls"][0, 0, :].partition_broadcast(B)).then_inc(in_cls, 16)

            def step(i, l):
                if live(i, GRID, l - 1, NPT):
                    r, n = (l - 1) % 2, i * GRID + (l - 1)
                    hp, w = i + (l - 1) // GRID, (l - 1) % GRID
                    wait(act, nmud, n + 1)
                    wait(act, xT_ps, n - 1)
                    src = xs[:, ds(hp, 1), :, :].rearrange("p o c (y w q) -> p (o c) y w q", w=GRID, q=PATCH)
                    act.activation(xn[:, r, :].rearrange("p (c y q) -> p c y q", c=CH, q=PATCH), src[:, :, :, w, :],
                                   ACT.Identity, bias=nmu[:, r:r + 1], scale=rstd[:, r:r + 1]).then_inc(xnd, 1)
                if live(i, GRID, l - 2, NPT):
                    r, n = (l - 2) % 2, i * GRID + (l - 2)
                    wait(act, xT_ps, n + 1)
                    wait(act, z_ps, n - 1)
                    act.activation(xT[:, r, :], xT_bank(r), ACT.Copy).then_inc(xTd, 1)
                if live(i, GRID, l, NPT):
                    r, n = l % 2, i * GRID + l
                    wait(act, vard, n + 1)
                    wait(act, rsd, n - 1)
                    act.activation(sd[:, r:r + 1], ve[:, r:r + 1], ACT.Sqrt).then_inc(sdev, 1)
                if live(i, GRID, l - 5, NPT):
                    r, n = (l - 5) % 2, i * GRID + (l - 5)
                    wait(act, h_ps, n + 1)
                    wait(act, hlo, n)
                    wait(act, cls_out, 2)
                    act.activation(hraw[:, r, :], h_bank(r), ACT.Copy).then_inc(hrawd, 1)
                    act.activation(tile_cols(hT_hi, i, l - 5), by_tile(h_bank(r)), ACT.Copy).then_inc(hhi, 1)
                if live(i, GRID, l - 3, NPT):
                    r, n = (l - 3) % 2, i * GRID + (l - 3)
                    wait(act, var2, n + 1)
                    wait(act, rsd2, n - 1)
                    act.activation(sd2[:, r:r + 1], ve2[:, r:r + 1], ACT.Sqrt).then_inc(sdev2, 1)
                if isinstance(i, int) and i == 0:
                    for n in weights_of(l):
                        act.wait_ge(wT_ps, n + 1)
                        act.activation(turned(n)[0], w_bank(n), ACT.Copy).then_inc(wT_hi, 1)
                    if l == 3:
                        act.wait_ge(cls_ps, 1)
                        act.activation(hraw[:, 0, 0:DC * B], h_bank(0)[:, 0:DC * B], ACT.Copy).then_inc(cls_raw, 1)
                        act.activation(tile_cols(hT_hi, HP, 0), by_tile(h_bank(0)[:, 0:DC * B]), ACT.Copy).then_inc(cls_hi, 1)

            rounds(act, HP, GRID, 5, step)

        @block.tensor
        def _(pe):
            pe.wait_ge(ident_made, 1)
            pe.wait_ge(in_b, 96)
            pe.transpose(ps[:, 3584:3596], rows12[:, :], ident[0:12, 0:12])
            for c in range(CH):
                last = pe.transpose(ps[:, 3600 + 4 * c:3604 + 4 * c], rows4[:, c:FC * P // 2:CH], ident[0:4, 0:4])
            last.then_inc(cols_ps, 1)
            pe.wait_ge(bmat_made, FC)
            pe.wait_ge(in_wp, 16)
            for f in range(FC):
                last = pe.matmul(z_bank(1), bmat[:, f, :], wp[:, f // CH, f % CH, :], start=(f == 0),
                                 stop=(f == FC - 1))
            last.then_inc(zb_ps, 1)

            def step(i, l):
                if isinstance(i, int) and i == 0:
                    for n in weights_of(l):
                        j, ic = n // DC, n % DC
                        pe.wait_ge(in_w, 64)
                        if n == 1:
                            pe.wait_ge(cols_sb, 2)
                        wait(pe, wT_hi, n - 1)
                        wait(pe, wT_lo, n - 1)
                        for oc in range(DC):
                            last = pe.transpose(w_bank(n)[:, P * oc:P * (oc + 1)], w_raw[:, j, oc, ic * P:(ic + 1) * P],
                                                ident[:, :])
                        last.then_inc(wT_ps, 1)
                if live(i, GRID, l - 1, NPT):
                    r, n = (l - 1) % 2, i * GRID + (l - 1)
                    wait(pe, xnd, n + 1)
                    wait(pe, xTd, n - 1)
                    for f in range(FC):
                        last = pe.transpose(xT_bank(r)[:, f * P:(f + 1) * P], xn[:, r, f * P:(f + 1) * P], ident[:, :])
                    last.then_inc(xT_ps, 1)
                if live(i, GRID, l - 2, NPT):
                    r, n = (l - 2) % 2, i * GRID + (l - 2)
                    wait(pe, xTd, n + 1)
                    wait(pe, zsd, n - 1)
                    if isinstance(i, int) and i == 0:
                        pe.wait_ge(gain_made, FC)
                        if l == 3:
                            pe.wait_ge(zb_made, 1)
                    for f in range(FC):
                        last = pe.matmul(z_bank(r), xT[:, r, f * P:(f + 1) * P], wpg[:, f % 2, f // 2, :],
                                         start=(f == 0), stop=(f == FC - 1))
                    last.then_inc(z_ps, 1)
                if isinstance(i, int) and i == 0:
                    if l == 3:
                        pe.wait_ge(cls_made, 1)
                        pe.wait_ge(wT_lo, 7)
                        pe.wait_ge(wT_hi, 7)
                        for c in range(DC):
                            last = pe.transpose(h_bank(0)[:, c * B:(c + 1) * B], hcls_sum[:, c * P:(c + 1) * P],
                                                ident[0:B, 0:B])
                        last.then_inc(cls_ps, 1)
                if live(i, GRID, l - 4, NPT):
                    r, n = (l - 4) % 2, i * GRID + (l - 4)
                    wait(pe, hnd, n + 1)
                    wait(pe, hhi, n - 1)
                    wait(pe, cls_hi, 1)
                    wait(pe, wT_lo, 8)
                    for c in range(DC):
                        last = pe.transpose(h_bank(r)[:, c * P:(c + 1) * P], hn[:, r, c * P:(c + 1) * P], ident[:, :])
                    last.then_inc(h_ps, 1)

            rounds(pe, HP, GRID, 5, step)

        @block.vector
        def _(dve):
            dve.wait_ge(cols_ps, 1)
            dve.tensor_copy(bias_col[:, :], ps[:, 3584:3596]).then_inc(cols_sb, 1)
            dve.tensor_copy(gcol[:, :, :], ps[:, 3600:3612].rearrange("p (c f) -> p c f", f=4)).then_inc(cols_sb, 1)
            dve.wait_ge(cols_sb, 2)
            for f in range(FC):
                dve.tensor_copy(bmat[:, f, :], gcol[:, f % CH, 2 + f // CH:3 + f // CH].to_broadcast([P, P])
                                ).then_inc(bmat_made, 1)
            def step(i, l):
                now, nrm, z, fin = (live(i, GRID, l - lag, NPT) for lag in (0, 1, 3, 4))
                n, r = i * GRID + l, l % 2
                n1, r1 = i * GRID + (l - 1), (l - 1) % 2
                n3, r3 = i * GRID + (l - 3), (l - 3) % 2
                n4, r4 = i * GRID + (l - 4), (l - 4) % 2
                if nrm:
                    wait(dve, sdev, n1 + 1)
                    wait(dve, xnd, n1 - 1)
                    dve.reciprocal(rstd[:, r1:r1 + 1], sd[:, r1:r1 + 1]).then_inc(rsd, 1)
                if fin:
                    wait(dve, sdev2, n4 + 1)
                    wait(dve, hnd, n4 - 1)
                    dve.reciprocal(rstd2[:, r4:r4 + 1], sd2[:, r4:r4 + 1]).then_inc(rsd2, 1)
                if nrm:
                    wait(dve, rsd, n1 + 1)
                    dve.tensor_scalar(nmu[:, r1:r1 + 1], mv[:, r1, 0:1], rstd[:, r1:r1 + 1], -1.0, ALU.mult,
                                      ALU.mult).then_inc(nmud, 1)
                if now:
                    if isinstance(i, int):
                        dve.wait_ge(in_x[i], 16 * 2 * CH)
                    elif l == 0:
                        for hp in range(1, HP):
                            dve.wait_ge(in_x[hp], 16 * 2 * CH)
                    wait(dve, aggr, n - 1)
                    alone(dve, carried)
                    src = xs[:, ds(i, 1), :, :].rearrange("p o c (y w q) -> p (o c) y w q", w=GRID, q=PATCH)
                    for c in range(CH):
                        dve.bn_stats(stat[:, r, 6 * c:6 * c + 6], src[:, c, :, l, :]).then_inc(statd, 1)
                if z:
                    wait(dve, z_ps, n3 + 1)
                    wait(dve, t1d, n3 - 1)
                    dve.tensor_tensor(zs[:, r3, :], z_bank(r3), zbias[:, :], ALU.add).then_inc(zsd, 1)
                if now:
                    wait(dve, statd, CH * n + CH)
                    wait(dve, nmud, n - 1)
                    alone(dve, carried)
                    dve.bn_aggr(mv[:, r, :], stat[:, r, :]).then_inc(aggr, 1)
                if fin:
                    wait(dve, hnd, n4 - 1)
                    dve.scalar_tensor_tensor(out=t1[:, r4, :], in0=zs[:, r4, :], scalar=mv2[:, r4, 0:1],
                                             in1=g2_row[:, :], op0=ALU.subtract, op1=ALU.mult).then_inc(t1d, 1)
                if now:
                    wait(dve, aggr, n + 1)
                    wait(dve, sdev, n - 1)
                    dve.tensor_scalar(ve[:, r:r + 1], mv[:, r, 1:2], EPS, None, ALU.add).then_inc(vard, 1)
                if fin:
                    wait(dve, t1d, n4 + 1)
                    wait(dve, rsd2, n4 + 1)
                    if l % 2 == 0:
                        wait(dve, table_made, i * HP + (l - 4) // 2 + 1)
                    wait(dve, h_ps, n4 - 1)
                    wait(dve, hres, n4 - 1)
                    dve.scalar_tensor_tensor(out=hn[:, r4, :], in0=t1[:, r4, :], scalar=rstd2[:, r4:r4 + 1],
                                             in1=h[:, ds(n4 * D, D)], op0=ALU.mult, op1=ALU.add).then_inc(hnd, 1)
                if z:
                    wait(dve, zsd, n3 + 1)
                    wait(dve, aggr2, n3 - 1)
                    alone(dve, carried)
                    dve.bn_stats(stat2[:, r3, :], zs[:, r3, :]).then_inc(stat2d, 1)
                if z:
                    wait(dve, stat2d, n3 + 1)
                    alone(dve, carried)
                    dve.bn_aggr(mv2[:, r3, :], stat2[:, r3, :]).then_inc(aggr2, 1)
                if z:
                    wait(dve, aggr2, n3 + 1)
                    wait(dve, sdev2, n3 - 1)
                    dve.tensor_scalar(ve2[:, r3:r3 + 1], mv2[:, r3, 1:2], EPS, None, ALU.add).then_inc(var2, 1)
                if isinstance(i, int) and i == 0:
                    if l == 1:
                        dve.wait_ge(in_cls, 32)
                        dve.tensor_tensor(hcls_sum[:, :], hcls[:, 0, :], hcls[:, 1, :], ALU.add).then_inc(cls_made, 1)
                    if l == 2:
                        dve.wait_ge(zb_ps, 1)
                        dve.wait_ge(in_rows, 64)
                        dve.tensor_tensor(zbias[:, :], z_bank(1), bp_row[:, :], ALU.add).then_inc(zb_made, 1)
                        dve.wait_ge(zb_made, 1)
                    for n in weights_of(l):
                        hi, lo = turned(n)
                        dve.wait_ge(wT_hi, n + 1)
                        dve.tensor_tensor(lo, w_bank(n), hi.bitcast(F32), ALU.subtract).then_inc(wT_lo, 1)

            rounds(dve, HP, GRID, 5, step)


def attention(nc, a, keep, first):
    hT_hi, hT_lo, ps = keep["hT_hi"], keep["hT_lo"], keep["ps"]
    wqkv_hi, wqkv_lo, ident, bias_col, attn = (keep[x] for x in ("wqkv_hi", "wqkv_lo", "ident", "bias_col", "attn"))
    tag = "a" if first else "b"
    bcol = 0 if first else 6
    PER = 2 * IG
    AHEAD = IG
    ROUNDS = UNITS // PER
    TAIL = AHEAD + 10
    FREE = 4
    CHUNKS = (2, 3, 0, 1, 4, 5)
    with phase(nc) as (ctx, taken):
        def sb(name, shape, dt=F32):
            return ctx.enter_context(nc.sbuf_tensor(name + tag, shape, dt))

        def sem(name):
            taken.append(nc.alloc_semaphore(name + tag))
            return taken[-1]

        qT = sb("qT", [P, 2, DC * GC + P])
        kT = sb("kT", [P, 2, DC * GC])
        vT = sb("vT", [P, 2, DC * 3 * GC])
        y = keep.get("y")
        ystat = sb("ystat", [P, 2, 6])
        yaggr = sb("yaggr", [P, 2, 2])
        kbd = sb("kbd", [P, 2, DC, HC, GC])
        PW = HC * NPOS + NPOS
        prob = sb("prob", [P, 4, PW])
        pT = sb("pT", [KEYROWS, 2, 3 * P])
        vbd = sb("vbd", [KEYROWS, 2, 2 * HEADS * VW])
        osb = sb("osb", [P, 2, D])
        mx = sb("mx", [P, 2, HC])
        rsum = sb("rsum", [P, 2, HEADS])
        kmask = sb("kmask", [P, HC])
        vmask3 = sb("vmask3", [KEYROWS, 3])
        vmask = sb("vmask", [KEYROWS, 2 * HEADS])
        raw = sb("raw", [P, 2, 2 * D]) if first else None
        warm = sb("warm", [P, 1])

        kmask_steps, vmask_steps, vmask_made, zeros_made, ones_made = map(
            sem, ("kmask_steps", "vmask_steps", "vmask_made", "zeros_made", "ones_made"))
        qkv_ps, qkv_sb, kbd_made, s_ps, max_made, sub_made, exp_made = map(
            sem, ("qkv_ps", "qkv_sb", "kbd_made", "s_ps", "max_made", "sub_made", "exp_made"))
        pT_ps, pT_sb, v_ps, vbd_made, o_ps, rsum_made, o_made, oT_ps, oT_sb = map(
            sem, ("pT_ps", "pT_sb", "v_ps", "vbd_made", "o_ps", "rsum_made", "o_made", "oT_ps", "oT_sb"))
        y_zero, in_y, y_made, ystat_made, yaggr_made = map(sem, ("y_zero", "in_y", "y_made", "ystat_made", "yaggr_made"))
        carried, ymean_made = sem("carried_"), sem("ymean_made")
        in_exp = [sem(f"in_exp{r}") for r in range(2)]
        exp_hi, exp_lo, in_next, warmed = map(sem, ("exp_hi", "exp_lo", "in_next", "warmed"))

        def s_bank(r):
            return ps[:, 512 * r:512 * r + HC * NPOS]

        def pT_bank(r):
            return ps[0:KEYROWS, 1024 + 512 * r:1024 + 512 * r + 3 * P]

        def qkv_bank(i, l):
            b = 7 if isinstance(i, int) and i == 0 and l < IG and l % 2 else 4
            return ps[:, 512 * b:512 * b + GC].rearrange("p (k b) -> p k b", b=IG)

        def expert_of(i, l):
            if first and isinstance(i, int) and i == 0 and l >= 6 and l % 2 == 0:
                return (l - 6) // 2
            return E - 3 + l // 2 if first and isinstance(i, int) and i == ROUNDS and l in (0, 2, 4) else None

        def by_vector(i, l, c):
            return isinstance(i, int) and i == 0 and l < IG and c == 1

        v_bank = ps[0:KEYROWS, 2560:3072]
        o_bank = ps[:, 3072:3072 + HEADS * VW]
        oT_bank = ps[:, 3584:3584 + DC * P]

        block = ctx.enter_context(nc.Block())

        @block.gpsimd
        def _(pool):
            pool.memset(kmask[:, :], 1.0).then_inc(kmask_steps, 1)
            pool.wait_ge(kmask_steps, 1)
            pool.affine_select(out=kmask[:, :], in_=kmask[:, :], compare_op=ALU.is_ge, fill=0.0,
                               base=0, pattern=[[-HD, HC]], channel_multiplier=1).then_inc(kmask_steps, 1)
            pool.wait_ge(kmask_steps, 2)
            pool.affine_select(out=kmask[:, :], in_=kmask[:, :], compare_op=ALU.is_ge, fill=0.0,
                               base=HD - 1, pattern=[[HD, HC]], channel_multiplier=-1).then_inc(kmask_steps, 1)
            pool.memset(vmask3[:, :], 1.0).then_inc(vmask_steps, 1)
            pool.wait_ge(vmask_steps, 1)
            pool.affine_select(out=vmask3[:, :], in_=vmask3[:, :], compare_op=ALU.is_ge, fill=0.0,
                               base=0, pattern=[[-NPOS, 3]], channel_multiplier=1).then_inc(vmask_steps, 1)
            pool.wait_ge(vmask_steps, 2)
            pool.affine_select(out=vmask3[:, :], in_=vmask3[:, :], compare_op=ALU.is_ge, fill=0.0,
                               base=NPOS - 1, pattern=[[NPOS, 3]], channel_multiplier=-1).then_inc(vmask_steps, 1)
            pool.wait_ge(kmask_steps, 3)

            def step(i, l):
                for c in range(DC):
                    if l % IG == 1 + 2 * c and live(i, 2, l // IG, IG) and not by_vector(i, l, c):
                        g, r = 2 * i + l // IG, l // IG
                        wait(pool, qkv_sb, 6 * g + 1 + c)
                        wait(pool, s_ps, IG * (g - 1))
                        alone(pool, carried)
                        for hh in range(HC):
                            pool.tensor_scalar(kbd[:, r, c, hh, :], kT[:, r, c * GC:(c + 1) * GC],
                                               kmask[:, hh:hh + 1], 1.0, ALU.mult, ALU.mult).then_inc(kbd_made, 1)
                if not first and isinstance(i, int) and i == 0 and l == 2:
                    pool.memset(y[:, :], 0.0).then_inc(y_zero, 1)
                e = expert_of(i, l)
                if e is not None:
                    pool.wait_ge(exp_hi, e + 1)
                    pool.tensor_tensor(keep["we_lo"][:, :, e * D:(e + 1) * D],
                                       raw[:, e % 2, :].rearrange("p (c n) -> p c n", c=DC),
                                       keep["we_hi"][:, :, e * D:(e + 1) * D].bitcast(F32), ALU.subtract
                                       ).then_inc(exp_lo, 1)

                if not first and l % 2 == 0 and live(i, PER // 2, (l - AHEAD - 6) // 2, B // 2):
                    p, r = i * (PER // 2) + (l - AHEAD - 6) // 2, ((l - AHEAD - 6) // 2) % 2
                    if isinstance(i, int) and p == 0:
                        pool.wait_ge(in_y, 64)
                    wait(pool, o_made, p + 1)
                    yp = y[:, ds(p * D, D)]
                    pool.tensor_tensor(yp, osb[:, r, :], yp, ALU.add).then_inc(y_made, 1)

            rounds(pool, ROUNDS, PER, TAIL, step)

        @block.sync
        def _(sp):
            if first:
                for e in range(E):
                    if e >= 2:
                        sp.wait_ge(exp_lo, e - 1)
                    sp.dma_start(raw[:, e % 2, :].rearrange("p (c n) -> p c n", c=DC),
                                 a["w_exp"][e].rearrange("(c p) n -> p c n", p=P)).then_inc(in_exp[e % 2], 16)
                sp.dma_start(keep["wg_raw"][:, :, :], a["w_gate"].rearrange("(c p) e -> p c e", p=P)).then_inc(in_next, 16)
                sp.dma_start(keep["bg_row"][:, :], a["b_gate"].partition_broadcast(P)).then_inc(in_next, 16)
                sp.dma_start(keep["be"][:, :], a["b_exp"]).then_inc(in_next, 16)
                sp.wait_ge(in_next, 48)
            else:
                sp.wait_ge(y_zero, 1)
                sp.wait_ge(keep["stored"][0], STORED_FREE + 16 * (NPT + 1))
                sp.wait_ge(keep["stored"][1], STORED_FREE + 16 * NPT)
                rows = y[:, :].rearrange("r (p d) -> r p d", d=D)
                left = a["left"].rearrange("(p m) s d -> m s p d", m=2)
                for im in range(2):
                    for s0, s1 in ((0, 1), (1, NPOS)):
                        sp.dma_start(rows[QPAD * im + s0:QPAD * im + s1, :, :], left[im, s0:s1, :, :]).then_inc(in_y, 16)

        @block.scalar
        def _(act):
            def step(i, l):
                if live(i, PER, l - AHEAD - 3, UNITS):
                    n, r = i * PER + (l - AHEAD - 3), (l - 3) % 2
                    wait(act, pT_ps, n + 1)
                    wait(act, o_ps, n - 1)
                    act.activation(pT[:, r, :], pT_bank(r), ACT.Copy).then_inc(pT_sb, 1)
                if l % IG < 6 and live(i, 2, l // IG, IG):
                    g, r, m, j = 2 * i + l // IG, l // IG, l % IG, CHUNKS[l % IG]
                    src = qkv_bank(i, l).rearrange("p k b -> p b k")
                    if j < 2 * DC:
                        dst = (qT, kT)[j // DC][:, r, (j % DC) * GC:(j % DC + 1) * GC].rearrange("p (b k) -> p b k", k=NPOS)
                    else:
                        dst = vT[:, r, (j % DC) * 3 * GC:(j % DC + 1) * 3 * GC].rearrange(
                            "p (b t k) -> p b t k", t=3, k=NPOS)
                        src = src.unsqueeze(2).to_broadcast([P, IG, 3, NPOS])
                    wait(act, qkv_ps, 6 * g + m + 1)
                    if j == 0:
                        wait(act, s_ps, IG * (g - 1))
                    if j == DC:
                        wait(act, kbd_made, 2 * HC * (g - 1))
                    if j == 2 * DC:
                        wait(act, v_ps, 4 * (g - 1))
                    act.activation(dst, src, ACT.Identity,
                                   bias=bias_col[:, bcol + j:bcol + j + 1]).then_inc(qkv_sb, 1)
                e = expert_of(i, l)
                if e is not None:
                    act.wait_ge(in_exp[e % 2], 16 * (e // 2 + 1))
                    act.activation(keep["we_hi"][:, :, e * D:(e + 1) * D],
                                   raw[:, e % 2, :].rearrange("p (c n) -> p c n", c=DC), ACT.Copy).then_inc(exp_hi, 1)
                if live(i, PER, l - AHEAD, UNITS):
                    n, r = i * PER + (l - AHEAD), l % 4
                    wait(act, sub_made, n + 1)
                    p8 = prob[:, r, 0:HC * NPOS]
                    act.activation(p8, p8, ACT.Exp, scale=float(HD) ** -0.5).then_inc(exp_made, 1)
                if first and l % 2 == 0 and live(i, PER // 2, (l - AHEAD - 6) // 2, B // 2):
                    p = i * (PER // 2) + (l - AHEAD - 6) // 2
                    wait(act, oT_ps, p + 1)
                    src = oT_bank.rearrange("p (c m s) -> p c m s", c=DC, m=2)
                    dst = attn[:, 0:DC * NTOK].rearrange("p (c s b) -> p c s b", c=DC, b=B)
                    for im in range(2):
                        act.activation(dst[:, :, :, ds(2 * p + im, 1)].rearrange("p c s o -> p c (s o)"),
                                       src[:, :, im, 0:NPOS], ACT.Copy).then_inc(oT_sb, 1)

            rounds(act, ROUNDS, PER, TAIL, step)
            if not first:
                act.wait_ge(kmask_steps, 3)
                act.activation(warm[:, :], kmask[:, 0:1], ACT.Sqrt).then_inc(warmed, 1)

        @block.tensor
        def _(pe):
            def step(i, l):
                if live(i, PER, l - AHEAD, UNITS):
                    n, r = i * PER + (l - AHEAD), l % 2
                    g, st, c = 2 * i + (l - AHEAD) // IG, ((l - AHEAD) // IG) % 2, l % 2
                    if isinstance(g, int) and g == 0:
                        if l % IG == 0:
                            pe.wait_ge(kbd_made, 2 * HC)
                            pe.wait_ge(zeros_made, 6)
                    elif l % IG < 2:
                        wait(pe, kbd_made, 2 * HC * g + HC * (c + 1))
                    wait(pe, sub_made, n - 1)
                    for im in range(2):
                        b = ((l % IG) // 2) * 2 + im
                        q0 = c * GC + b * NPOS
                        last = pe.matmul(s_bank(r)[QPAD * im:QPAD * im + QPAD, :], qT[:, st, q0:q0 + QPAD],
                                         kbd[:, st, c, :, b * NPOS:(b + 1) * NPOS], start=True, stop=True)
                    last.then_inc(s_ps, 1)
                if live(i, PER, l - AHEAD - 2, UNITS):
                    n, r = i * PER + (l - AHEAD - 2), (l - 2) % 2
                    wait(pe, exp_made, n + 1)
                    wait(pe, pT_sb, n - 1)
                    for t in range(3):
                        last = pe.transpose(pT_bank(r)[:, t * P:(t + 1) * P],
                                            prob[:, (l - 2) % 4, t * KEYROWS:(t + 1) * KEYROWS], ident[:, :])
                    last.then_inc(pT_ps, 1)
                if l % IG < 6 and live(i, 2, l // IG, IG):
                    g, m, j = 2 * i + l // IG, l % IG, CHUNKS[l % IG]
                    wait(pe, qkv_sb, 6 * g + m - (isinstance(i, int) and g == 0))
                    terms = [(w, x, c) for w, x in ((wqkv_hi, hT_hi), (wqkv_lo, hT_hi), (wqkv_hi, hT_lo)) for c in range(DC)]
                    for m, (w, x, c) in enumerate(terms):
                        rhs = x[:, c * NTOK:(c + 1) * NTOK].rearrange("p (s b) -> p s b", b=B)[:, :, ds(IG * g, IG)]
                        last = pe.matmul(qkv_bank(i, l), w[:, c, j * P:(j + 1) * P], rhs,
                                         start=(m == 0), stop=(m == len(terms) - 1))
                    last.then_inc(qkv_ps, 1)
                if l % 2 == 0 and live(i, PER // 2, (l - AHEAD) // 2, B // 2):
                    p, st = i * (PER // 2) + (l - AHEAD) // 2, ((l - AHEAD) // IG) % 2
                    wait(pe, vbd_made, p)
                    if l % IG == 0:
                        wait(pe, qkv_sb, 6 * (2 * i + (l - AHEAD) // IG) + 6)
                    for im in range(2):
                        b = ((l % IG) // 2) * 2 + im
                        for c in range(DC):
                            v0 = (c * IG + b) * KEYROWS
                            last = pe.transpose(v_bank[:, im * D + c * P:im * D + (c + 1) * P],
                                                vT[:, st, v0:v0 + KEYROWS], ident[:, :])
                    last.then_inc(v_ps, 1)
                if first and l % 2 == 1 and live(i, PER // 2, (l - AHEAD - 5) // 2, B // 2):
                    p, r = i * (PER // 2) + (l - AHEAD - 5) // 2, ((l - AHEAD - 5) // 2) % 2
                    wait(pe, o_made, p + 1)
                    wait(pe, oT_sb, 2 * p)
                    for c in range(DC):
                        last = pe.transpose(oT_bank[:, c * P:(c + 1) * P], osb[:, r, c * P:(c + 1) * P], ident[:, :])
                    last.then_inc(oT_ps, 1)
                if live(i, PER, l - AHEAD - 3, UNITS):
                    n, r, c = i * PER + (l - AHEAD - 3), (l - 3) % 2, (l - 3) % 2
                    p, pr = i * (PER // 2) + (l - AHEAD - 3 - c) // 2, ((l - AHEAD - 3) // 2) % 2
                    wait(pe, pT_sb, n + 1)
                    wait(pe, vbd_made, p + 1)
                    if c == 0:
                        wait(pe, o_made, p)
                    for t in range(3):
                        heads = min(3, HC - 3 * t)
                        h0 = HC * c + 3 * t
                        for im in range(2):
                            v0 = (HEADS * im + h0) * VW
                            last = pe.matmul(o_bank[QPAD * im:QPAD * im + QPAD, h0 * VW:(h0 + heads) * VW],
                                             pT[:, r, t * P + QPAD * im:t * P + QPAD * im + QPAD],
                                             vbd[:, pr, v0:v0 + heads * VW], start=True, stop=True)
                    last.then_inc(o_ps, 1)

            rounds(pe, ROUNDS, PER, TAIL, step)

        @block.vector
        def _(dve):
            for r in range(2):
                dve.memset(qT[:, r, DC * GC:DC * GC + P], 0.0).then_inc(zeros_made, 1)
            for r in range(4):
                dve.memset(prob[:, r, HC * NPOS:PW], 0.0).then_inc(zeros_made, 1)
            dve.wait_ge(kmask_steps, 3)
            dve.wait_ge(vmask_steps, 3)
            v8 = vmask[:, :].rearrange("p (g h) -> p g h", h=HC)
            for h0 in range(0, HC, 3):
                heads = min(3, HC - h0)
                dve.tensor_copy(v8[:, :, h0:h0 + heads], vmask3[:, 0:heads].unsqueeze(1).to_broadcast(
                    [KEYROWS, 2 * DC, heads])).then_inc(vmask_made, 1)
            dve.wait_ge(vmask_made, 3)
            for r in range(2):
                ones = vbd[:, r, :].rearrange("p (h v) -> p h v", v=VW)[:, :, HD:VW]
                dve.tensor_copy(ones, vmask[:, :].unsqueeze(2)).then_inc(ones_made, 1)
            dve.wait_ge(ones_made, 2)
            dve.sem_inc(yaggr_made, FREE)
            dve.sem_inc(ymean_made, FREE)

            def step(i, l):
                if l % 2 == 1 and live(i, PER // 2, (l - AHEAD - 5) // 2, B // 2):
                    p, r = i * (PER // 2) + (l - AHEAD - 5) // 2, ((l - AHEAD - 5) // 2) % 2
                    wait(dve, o_ps, 2 * p + 2)
                    wait(dve, o_made, p - 1)
                    o16 = o_bank.rearrange("p (h v) -> p h v", v=VW)
                    dve.reciprocal(rsum[:, r, :].unsqueeze(2), o16[:, :, HD:VW]).then_inc(rsum_made, 1)
                    wait(dve, rsum_made, p + 1)
                    wait(dve, oT_ps if first else y_made, p - 1)
                    dve.tensor_tensor(osb[:, r, :].rearrange("p (h v) -> p h v", v=HD), o16[:, :, 0:HD],
                                      rsum[:, r, :].unsqueeze(2).to_broadcast([P, HEADS, HD]), ALU.mult
                                      ).then_inc(o_made, 1)
                if l == 3 and by_vector(i, l, 1):
                    dve.wait_ge(qkv_sb, 2)
                    for hh in range(HC):
                        dve.tensor_scalar(kbd[:, 0, 1, hh, :], kT[:, 0, GC:2 * GC], kmask[:, hh:hh + 1], None,
                                          ALU.mult).then_inc(kbd_made, 1)
                if live(i, PER, l - AHEAD, UNITS):
                    n, r = i * PER + (l - AHEAD), l % 2
                    wait(dve, s_ps, n + 1)
                    wait(dve, sub_made, n - 1)
                    s8 = s_bank(r).rearrange("p (h k) -> p h k", k=NPOS)
                    dve.tensor_reduce(mx[:, r, :], s8, AX.X, ALU.max).then_inc(max_made, 1)
                    wait(dve, max_made, n + 1)
                    wait(dve, pT_ps, n - 3)
                    dve.tensor_tensor(prob[:, l % 4, 0:HC * NPOS].rearrange("p (h k) -> p h k", k=NPOS), s8,
                                      mx[:, r, :].unsqueeze(2).to_broadcast([P, HC, NPOS]), ALU.subtract
                                      ).then_inc(sub_made, 1)
                if l % 2 == 1 and live(i, PER // 2, (l - AHEAD - 1) // 2, B // 2):
                    p, r = i * (PER // 2) + (l - AHEAD - 1) // 2, ((l - AHEAD - 1) // 2) % 2
                    wait(dve, v_ps, p + 1)
                    wait(dve, o_ps, 2 * (p - 1))
                    dve.tensor_tensor(vbd[:, r, :].rearrange("p (h v) -> p h v", v=VW)[:, :, 0:HD],
                                      v_bank.rearrange("p (h v) -> p h v", v=HD),
                                      vmask[:, :].unsqueeze(2).to_broadcast([KEYROWS, 2 * HEADS, HD]), ALU.mult
                                      ).then_inc(vbd_made, 1)
                if not first and l % 2 == 0 and live(i, PER // 2, (l - AHEAD - 8) // 2, B // 2):
                    p, r = i * (PER // 2) + (l - AHEAD - 8) // 2, ((l - AHEAD - 8) // 2) % 2
                    wait(dve, y_made, p + 1)
                    wait(dve, yaggr_made, FREE + p - 1)
                    alone(dve, carried)
                    dve.bn_stats(ystat[:, r, :], y[:, ds(p * D, D)]).then_inc(ystat_made, 1)
                if not first and l % 2 == 1 and live(i, PER // 2, (l - AHEAD - 9) // 2, B // 2):
                    p, r = i * (PER // 2) + (l - AHEAD - 9) // 2, ((l - AHEAD - 9) // 2) % 2
                    wait(dve, ystat_made, p + 1)
                    wait(dve, ymean_made, FREE + 2 * (p - 1))
                    alone(dve, carried)
                    dve.bn_aggr(yaggr[:, r, :], ystat[:, r, :]).then_inc(yaggr_made, 1)
                    wait(dve, yaggr_made, FREE + p + 1)
                    dve.tensor_copy(keep["ymean"][:, ds(p, 1)], yaggr[:, r, 0:1]).then_inc(ymean_made, 1)
                    dve.tensor_scalar(keep["yvar"][:, ds(p, 1)], yaggr[:, r, 1:2], EPS, None, ALU.add).then_inc(ymean_made, 1)

            rounds(dve, ROUNDS, PER, TAIL, step)


def rsqrt_steps(dve, y, t, v, sem, at):
    I32 = mybir.dt.int32

    def run(k, op):
        def go():
            wait(dve, sem, at + k)
            op().then_inc(sem, 1)
        return go

    steps = [
        lambda: dve.tensor_scalar(t.bitcast(I32), v.bitcast(I32), 1, None, ALU.logical_shift_right),
        lambda: dve.tensor_scalar(y.bitcast(I32), t.bitcast(I32), -1, 0x5F3759DF, ALU.mult, ALU.add),
    ]
    for _ in range(3):
        steps += [
            lambda: dve.tensor_scalar(t, y, y, v, ALU.mult, ALU.mult),
            lambda: dve.tensor_scalar(t, t, -0.5, 1.5, ALU.mult, ALU.add),
            lambda: dve.tensor_tensor(y, y, t, ALU.mult),
        ]
    assert len(steps) == RSQRT
    return [run(k, op) for k, op in enumerate(steps)]


RSQRT = 11


def norm_and_experts(nc, a, keep):
    h, hT_hi, hT_lo, ps, attn = (keep[x] for x in ("h", "hT_hi", "hT_lo", "ps", "attn"))
    wqkv_hi, wqkv_lo, wo_hi, wo_lo = (keep[x] for x in ("wqkv_hi", "wqkv_lo", "wo_hi", "wo_lo"))
    we_hi, we_lo, ident = keep["we_hi"], keep["we_lo"], keep["ident"]
    with phase(nc) as (ctx, taken):
        def sb(name, shape, dt=F32):
            return ctx.enter_context(nc.sbuf_tensor(name, shape, dt))

        def sem(name):
            taken.append(nc.alloc_semaphore(name))
            return taken[-1]

        wg_raw, bg_row, be = (keep[x] for x in ("wg_raw", "bg_row", "be"))
        w2_raw = sb("w2_raw", [P, DC, 3 * D])
        aT_hi = sb("aT_hi", [P, 2, DC * P], F32R)
        aT_lo = sb("aT_lo", [P, 2, DC * P], F32R)
        z = sb("z3", [P, 2, D])
        stat = sb("stat3", [P, 2, 6])
        mv = sb("mv3", [P, 2, 2])
        ve = sb("ve3", [P, 2])
        newt = sb("newt", [P, 2])
        rstd = sb("rstd3", [P, 2])
        nmr = sb("nmr3", [P, 2])
        hn = sb("hn3", [P, 3, D])
        tT_hi = sb("tT_hi", [P, 3, DC * P], F32R)
        tT_lo = sb("tT_lo", [P, 3, DC * P], F32R)
        wg_hi = sb("wg_hi", [P, DC, E], F32R)
        wg_lo = sb("wg_lo", [P, DC, E], F32R)
        iota8 = sb("iota8", [P, E])
        lg = sb("lg", [P, 2, E])
        lmax = sb("lmax", [P, 2])
        lsub = sb("lsub", [P, 2, E])
        ge = sb("ge", [P, 2, E])
        gsum = sb("gsum", [P, 2])
        grs = sb("grs", [P, 2])
        gate = sb("gate", [P, 2, E])
        top = sb("top", [P, 2, E])
        topi = sb("topi", [P, 2, E], U32)
        topf = sb("topf", [P, 2, 2])
        pick = sb("pick", [P, 2, 2, E])
        comb = sb("comb", [P, 2, E])
        combT = sb("combT", [E, 2, P])
        scaled = sb("scaled", [P, 4, D])
        summed = sb("summed", [P, 2, D])
        direct = sb("direct", [P, 2, D])
        total, stored = keep["total"], keep["stored"]

        carried = sem("carried3")
        in_w2, w2_hi, w2_lo, wg_h, wg_l, iota_made = map(
            sem, ("in_w2", "w2_hi", "w2_lo", "wg_h", "wg_l", "iota_made"))
        ahi, alo, wo_ps, zadd, statd, aggrd, vard, rsqd, nmrd = map(
            sem, ("ahi", "alo", "wo_ps", "zadd", "statd3", "aggrd", "vard3", "rsqd", "nmrd"))
        (hnd, t_ps, thi, tlo, tcopy_hi, tcopy_lo, g_ps, lgd, lmaxd, lsubd, ged, grsd, gated, topd, topid, topfd, pickd,
         combd) = map(
            sem, ("hnd3", "t_ps", "thi", "tlo", "tcopy_hi", "tcopy_lo", "g_ps", "lgd", "lmaxd", "lsubd", "ged", "grsd",
                  "gated", "topd", "topid", "topfd", "pickd", "combd"))
        cT_ps, cT_sb, be_ps, ex_ps, directd, scaledd, sumd, totald = map(
            sem, ("cT_ps", "cT_sb", "be_ps", "ex_ps", "directd", "scaledd", "sumd", "totald"))

        DIRECT, SCALED = (0, 1, None, 4, 5), (2, 3, 6, 7)
        wo_bank = ps[:, 3584:3584 + D]
        t_bank = ps[:, 2048:2048 + D]
        g_bank = ps[:, 2048 + D:2048 + D + E]
        cT_bank = ps[0:E, 2560:2560 + P]
        be_bank = ps[:, 3072:3072 + D]

        def tile(i, l, lag):
            return live(i, GRID, l - lag, NT), i * GRID + (l - lag), rows_of(i, l - lag), l - lag

        SPLIT, WO, TURN, GATE, EXPERTS, TOTAL = 0, 1, 2, 3, 4, 5

        def cols(ap, m):
            return ap.rearrange("p (c h b) -> p c h b", c=DC, b=B)[:, :, 0:m // B, :]

        FREE = STORED_FREE
        block = ctx.enter_context(nc.Block())

        @block.sync
        def _(sp):
            sp.dma_start(w2_raw[:, :, :], a["w_qkv"].rearrange("(c p) n -> p c n", p=P)).then_inc(in_w2, 16)
            for r in range(2):
                sp.sem_inc(stored[r], FREE)

            def store(i, l):
                if live(i, GRID, l, NT):
                    r, n = l % 2, i * GRID + l
                    wait(sp, totald, n + 1)
                    if isinstance(i, int) and n == NPT:
                        sp.dma_start(a["left"][:, 0, :], total[0:B, r, :]).then_inc(stored[r], 16)
                        return
                    for h2 in range(2):
                        s = 2 * GRID * i + (1 + GRID * h2 + l)
                        sp.dma_start(a["left"][:, ds(s, 1), :].rearrange("b o d -> b (o d)"),
                                     total[B * h2:B * h2 + B, r, :]).then_inc(stored[r], 16)

            rounds(sp, HP, GRID, 1, store)

        @block.gpsimd
        def _(pool):
            pool.iota(iota8[:, :], pattern=[[1, E]], base=0, channel_multiplier=0,
                      allow_small_or_imprecise_dtypes=True).then_inc(iota_made, 1)

            def step(i, l):
                on, n, m, k = tile(i, l, SPLIT)
                if isinstance(i, int) and i == 0 and DC <= l < DC + 3:
                    for c in range(DC):
                        cut = slice((l - DC) * D, (l - DC + 1) * D)
                        pool.wait_ge(w2_hi, DC * (l - DC) + c + 1)
                        pool.tensor_tensor(wqkv_lo[:, c, cut], w2_raw[:, c, cut], wqkv_hi[:, c, cut].bitcast(F32),
                                           ALU.subtract).then_inc(w2_lo, 1)
                if on:
                    r = k % 2
                    wait(pool, ahi, n + 1)
                    wait(pool, wo_ps, n - 1)
                    pool.tensor_tensor(cols(aT_lo[:, r, :], m), tile_cols(attn, i, k),
                                       cols(aT_hi[:, r, :], m).bitcast(F32), ALU.subtract).then_inc(alo, 1)
                on2, n2, m2, k2 = tile(i, l, EXPERTS)
                on1, n1, m1, k1 = tile(i, l, GATE)

                def add_scaled(q):
                    r = k2 % 2
                    wait(pool, scaledd, 4 * n2 + q + 1)
                    if q == 0:
                        wait(pool, totald, n2 - 1)
                    else:
                        wait(pool, sumd, 4 * n2 + q)
                    src = hn[0:m2, k2 % 3, :] if q == 0 else summed[0:m2, r, :]
                    pool.tensor_tensor(summed[0:m2, r, :], src, scaled[0:m2, q, :], ALU.add).then_inc(sumd, 1)

                if on2:
                    add_scaled(0)
                    add_scaled(1)
                if on1:
                    wait(pool, thi, n1 + 1)
                    pool.tensor_copy(tile_cols(hT_hi, i, k1), cols(tT_hi[:, k1 % 3, :], m1)).then_inc(tcopy_hi, 1)
                if on2:
                    add_scaled(2)
                if on1:
                    wait(pool, tlo, n1 + 1)
                    pool.tensor_copy(tile_cols(hT_lo, i, k1), cols(tT_lo[:, k1 % 3, :], m1)).then_inc(tcopy_lo, 1)
                if on2:
                    add_scaled(3)

            rounds(pool, HP, GRID, EXPERTS + 1, step)

        @block.scalar
        def _(act):
            def step(i, l):
                on, n, m, k = tile(i, l, SPLIT)
                on1, n1, m1, k1 = tile(i, l, GATE)
                on2, n2, m2, k2 = tile(i, l, EXPERTS)
                if isinstance(i, int) and i == 0 and DC <= l < DC + 3:
                    act.wait_ge(in_w2, 16)
                    for c in range(DC):
                        cut = slice((l - DC) * D, (l - DC + 1) * D)
                        act.activation(wqkv_hi[:, c, cut], w2_raw[:, c, cut], ACT.Copy).then_inc(w2_hi, 1)
                if on:
                    wait(act, alo, n - 1)
                    wait(act, wo_ps, n - 1)
                    act.activation(cols(aT_hi[:, k % 2, :], m), tile_cols(attn, i, k), ACT.Copy).then_inc(ahi, 1)
                def scale(q):
                    e = SCALED[q]
                    wait(act, ex_ps, 4 * n2 + e // 2 + 1)
                    wait(act, sumd, 4 * (n2 - 1) + q + 1)
                    act.activation(scaled[0:m2, q, :], ps[0:m2, D * e:D * (e + 1)], ACT.Copy,
                                   scale=comb[0:m2, k2 % 2, e:e + 1]).then_inc(scaledd, 1)

                if on2:
                    wait(act, cT_ps, n2 + 1)
                    wait(act, be_ps, n2 - 1)
                    act.activation(combT[:, k2 % 2, 0:m2], cT_bank[:, 0:m2], ACT.Copy).then_inc(cT_sb, 1)
                if on1:
                    wait(act, lsubd, n1 + 1)
                    wait(act, gated, n1 - 1)
                    act.activation(ge[0:m1, k1 % 2, :], lsub[0:m1, k1 % 2, :], ACT.Exp,
                                   accum_out=gsum[0:m1, k1 % 2:k1 % 2 + 1]).then_inc(ged, 1)
                ont, nt, mt, kt = tile(i, l, TURN)
                if ont:
                    wait(act, t_ps, nt + 1)
                    wait(act, ex_ps, 4 * (nt - 2))
                    wait(act, tcopy_hi, nt - 2)
                    act.activation(cols(tT_hi[:, kt % 3, :], mt), cols(t_bank, mt), ACT.Copy).then_inc(thi, 1)
                if on2:
                    wait(act, combd, n2 + 1)
                    scale(0)
                    scale(1)
                on, n, m, k = tile(i, l, WO)
                if on:
                    r = k % 2
                    wait(act, nmrd, n + 1)
                    wait(act, sumd, 4 * (n - 3) + 1)
                    act.activation(hn[0:m, k % 3, :], z[0:m, r, :], ACT.Identity, bias=nmr[0:m, r:r + 1],
                                   scale=rstd[0:m, r:r + 1]).then_inc(hnd, 1)
                if on2:
                    scale(2)
                    scale(3)

            act.activation(wg_hi[:, :, :], wg_raw[:, :, :], ACT.Copy).then_inc(wg_h, 1)
            rounds(act, HP, GRID, EXPERTS + 1, step)

        @block.tensor
        def _(pe):
            pe.wait_ge(wg_l, 1)

            def product(out, x, r, m, pair, w0, w1, sem):
                hi, lo = x
                whi, wlo = pair
                terms = [(xx, ww, c) for xx, ww in ((hi, whi), (hi, wlo), (lo, whi)) for c in range(DC)]
                for j, (xx, ww, c) in enumerate(terms):
                    last = pe.matmul(out, xx[:, r, c * P:c * P + m], ww[:, c, w0:w1], start=(j == 0),
                                     stop=(j == len(terms) - 1))
                last.then_inc(sem, 1)

            def step(i, l):
                on, n, m, k = tile(i, l, WO)
                on1, n1, m1, k1 = tile(i, l, GATE)
                on2, n2, m2, k2 = tile(i, l, EXPERTS)

                def experts(q):
                    if q % 2 == 0:
                        wait(pe, directd, 5 * (n2 - 1) + (2 if q == 0 else 5))
                    else:
                        wait(pe, scaledd, 4 * (n2 - 1) + q + 1)
                    product(ps[0:m2, 512 * q:512 * (q + 1)], (tT_hi, tT_lo), k2 % 3, m2, (we_hi, we_lo),
                            2 * D * q, 2 * D * (q + 1), ex_ps)

                if on:
                    wait(pe, alo, n + 1)
                    wait(pe, zadd, n)
                    product(wo_bank[0:m, :], (aT_hi, aT_lo), k % 2, m, (wo_hi, wo_lo), 0, D, wo_ps)
                if on1:
                    wait(pe, thi, n1 + 1)
                    wait(pe, tlo, n1 + 1)
                    wait(pe, lgd, n1)
                    product(g_bank[0:m1, :], (tT_hi, tT_lo), k1 % 3, m1, (wg_hi, wg_lo), 0, E, g_ps)
                if on2:
                    wait(pe, combd, n2 + 1)
                    wait(pe, cT_sb, n2)
                    pe.transpose(cT_bank[:, 0:m2], comb[0:m2, k2 % 2, :], ident[0:m2, 0:m2]).then_inc(cT_ps, 1)
                    experts(0)
                ont, nt, mt, kt = tile(i, l, TURN)
                if ont:
                    wait(pe, hnd, nt + 1)
                    if on1:
                        wait(pe, lgd, n1 + 1)
                    wait(pe, thi, nt)
                    wait(pe, tlo, nt)
                    for c in range(DC):
                        last = pe.transpose(t_bank[:, c * P:c * P + mt], hn[0:mt, kt % 3, c * P:(c + 1) * P],
                                            ident[0:mt, 0:mt])
                    last.then_inc(t_ps, 1)
                if on2:
                    experts(1)
                    wait(pe, cT_sb, n2 + 1)
                    wait(pe, directd, 5 * (n2 - 1) + 3)
                    pe.matmul(be_bank[0:m2, :], combT[:, k2 % 2, 0:m2], be[:, :], start=True, stop=True).then_inc(be_ps, 1)
                    experts(2)
                    experts(3)

            rounds(pe, HP, GRID, EXPERTS + 1, step)

        @block.vector
        def _(dve):
            dve.wait_ge(wg_h, 1)
            dve.tensor_tensor(wg_lo[:, :, :], wg_raw[:, :, :], wg_hi[:, :, :].bitcast(F32), ALU.subtract).then_inc(wg_l, 1)
            dve.wait_ge(iota_made, 1)

            def step(i, l):
                on, n, m, k = tile(i, l, WO)
                on1, n1, m1, k1 = tile(i, l, GATE)
                on2, n2, m2, k2 = tile(i, l, EXPERTS)
                r, r1, r2 = k % 2, k1 % 2, k2 % 2

                def add_direct(q):
                    acc = direct[0:m2, r2, :]
                    if q == 0:
                        wait(dve, combd, n2 + 1)
                        wait(dve, totald, n2 - 1)
                    else:
                        wait(dve, directd, 5 * n2 + q)
                    if q == 2:
                        wait(dve, be_ps, n2 + 1)
                        dve.tensor_tensor(acc, be_bank[0:m2, :], acc, ALU.add).then_inc(directd, 1)
                        return
                    e = DIRECT[q]
                    wait(dve, ex_ps, 4 * n2 + e // 2 + 1)
                    src, w = ps[0:m2, D * e:D * (e + 1)], comb[0:m2, r2, e:e + 1]
                    if q == 0:
                        dve.tensor_scalar(acc, src, w, None, ALU.mult).then_inc(directd, 1)
                    else:
                        dve.scalar_tensor_tensor(out=acc, in0=src, scalar=w, in1=acc, op0=ALU.mult,
                                                 op1=ALU.add).then_inc(directd, 1)

                if on:
                    wait(dve, wo_ps, n + 1)
                    wait(dve, hnd, n - 1)
                    dve.tensor_tensor(z[0:m, r, :], wo_bank[0:m, :], h[0:m, ds(n * D, D)], ALU.add).then_inc(zadd, 1)
                if on1:
                    wait(dve, g_ps, n1 + 1)
                    wait(dve, lsubd, n1 - 1)
                    dve.tensor_tensor(lg[0:m1, r1, :], g_bank[0:m1, :], bg_row[0:m1, :], ALU.add).then_inc(lgd, 1)
                if on:
                    wait(dve, zadd, n + 1)
                    wait(dve, aggrd, n - 1)
                    alone(dve, carried)
                    dve.bn_stats(stat[0:m, r, :], z[0:m, r, :]).then_inc(statd, 1)
                if on1:
                    wait(dve, lgd, n1 + 1)
                    dve.tensor_reduce(lmax[0:m1, r1:r1 + 1], lg[0:m1, r1, :], AX.X, ALU.max).then_inc(lmaxd, 1)
                if on:
                    wait(dve, statd, n + 1)
                    wait(dve, nmrd, n - 1)
                    alone(dve, carried)
                    dve.bn_aggr(mv[0:m, r, :], stat[0:m, r, :]).then_inc(aggrd, 1)
                if on1:
                    wait(dve, lmaxd, n1 + 1)
                    wait(dve, ged, n1 - 1)
                    dve.tensor_scalar(lsub[0:m1, r1, :], lg[0:m1, r1, :], lmax[0:m1, r1:r1 + 1], None,
                                      ALU.subtract).then_inc(lsubd, 1)
                if on:
                    wait(dve, aggrd, n + 1)
                    dve.tensor_scalar(ve[0:m, r:r + 1], mv[0:m, r, 1:2], EPS, None, ALU.add).then_inc(vard, 1)
                if on:
                    wait(dve, vard, n + 1)
                    wait(dve, hnd, n - 1)
                    root = rsqrt_steps(dve, rstd[0:m, r:r + 1], newt[0:m, r:r + 1], ve[0:m, r:r + 1], rsqd, RSQRT * n)
                else:
                    root = []

                def newton(count):
                    for _ in range(count if root else 0):
                        root.pop(0)()

                newton(1)
                if on1:
                    wait(dve, ged, n1 + 1)
                    dve.reciprocal(grs[0:m1, r1:r1 + 1], gsum[0:m1, r1:r1 + 1]).then_inc(grsd, 1)
                newton(1)
                if on1:
                    wait(dve, grsd, n1 + 1)
                    dve.tensor_scalar(gate[0:m1, r1, :], ge[0:m1, r1, :], grs[0:m1, r1:r1 + 1], None,
                                      ALU.mult).then_inc(gated, 1)
                newton(1)
                newton(1)
                if on1:
                    wait(dve, gated, n1 + 1)
                    alone(dve, carried)
                    dve.max(top[0:m1, r1, :], gate[0:m1, r1, :]).then_inc(topd, 1)
                newton(1)
                if on1:
                    wait(dve, topd, n1 + 1)
                    alone(dve, carried)
                    dve.max_index(topi[0:m1, r1, :], top[0:m1, r1, :], gate[0:m1, r1, :]).then_inc(topid, 1)
                newton(1)
                if on2:
                    add_direct(0)
                newton(1)
                ont, nt, mt, kt = tile(i, l, TURN)
                if ont:
                    wait(dve, thi, nt + 1)
                    wait(dve, ex_ps, 4 * (nt - 2))
                    wait(dve, tcopy_lo, nt - 2)
                    dve.tensor_tensor(cols(tT_lo[:, kt % 3, :], mt), cols(t_bank, mt), cols(tT_hi[:, kt % 3, :], mt).bitcast(F32),
                                      ALU.subtract).then_inc(tlo, 1)
                if on1:
                    wait(dve, topid, n1 + 1)
                    dve.tensor_copy(topf[0:m1, r1, :], topi[0:m1, r1, 0:2]).then_inc(topfd, 1)
                newton(1)
                if on2:
                    add_direct(1)
                newton(1)
                if on1:
                    wait(dve, topfd, n1 + 1)
                    for t in range(2):
                        dve.tensor_scalar(pick[0:m1, r1, t, :], iota8[0:m1, :], topf[0:m1, r1, t:t + 1],
                                          top[0:m1, r1, t:t + 1], ALU.is_equal, ALU.mult).then_inc(pickd, 1)
                newton(1)
                if on1:
                    wait(dve, pickd, 2 * n1 + 2)
                    wait(dve, cT_ps, n1 - 1)
                    wait(dve, scaledd, 4 * (n1 - 1))
                    dve.tensor_tensor(comb[0:m1, r1, :], pick[0:m1, r1, 0, :], pick[0:m1, r1, 1, :], ALU.add).then_inc(combd, 1)
                newton(1)
                if on2:
                    add_direct(2)
                newton(3)
                if on:
                    wait(dve, rsqd, RSQRT * n + RSQRT)
                    dve.tensor_scalar(nmr[0:m, r:r + 1], mv[0:m, r, 0:1], rstd[0:m, r:r + 1], -1.0, ALU.mult,
                                      ALU.mult).then_inc(nmrd, 1)
                if on2:
                    add_direct(3)
                    add_direct(4)
                on4, n4, m4, k4 = tile(i, l, TOTAL)
                if on4:
                    r4 = k4 % 2
                    wait(dve, directd, 5 * n4 + 5)
                    wait(dve, sumd, 4 * n4 + 4)
                    wait(dve, stored[r4], FREE + 32 * (i * HP + k4 // 2))
                    dve.tensor_tensor(total[0:m4, r4, :], direct[0:m4, r4, :], summed[0:m4, r4, :], ALU.add).then_inc(totald, 1)

            rounds(dve, HP, GRID, TOTAL + 1, step)


def last_norm(nc, a, keep):
    y, mean, var = keep["y"], keep["ymean"], keep["yvar"]
    NP, PARTS = B // 2, 4
    with phase(nc) as (ctx, taken):
        def sb(name, shape, dt=F32):
            return ctx.enter_context(nc.sbuf_tensor(name, shape, dt))

        def sem(name):
            taken.append(nc.alloc_semaphore(name))
            return taken[-1]

        sd = sb("sd4", [P, NP])
        rstd = sb("rstd4", [P, NP])
        nmr = sb("nmr4", [P, NP])
        sdev, rsd, nmrd, out_stored = map(sem, ("sdev4", "rsd4", "nmrd4", "out_stored"))
        yd = [sem(f"yd{k}") for k in range(3)]
        SHARE = (0, 1, 0, 2, 0, 1, 2, 0)
        block = ctx.enter_context(nc.Block())

        @block.vector
        def _(dve):
            dve.wait_ge(sdev, 1)
            dve.reciprocal(rstd[:, :], sd[:, :]).then_inc(rsd, 1)
            dve.wait_ge(rsd, 1)
            dve.scalar_tensor_tensor(out=nmr[:, :], in0=mean[:, :], scalar=-1.0, in1=rstd[:, :],
                                     op0=ALU.mult, op1=ALU.mult).then_inc(nmrd, 1)
            dve.wait_ge(nmrd, 1)
            for p in range(NP):
                if SHARE[p % 8] == 0:
                    yp = y[:, p * D:(p + 1) * D]
                    dve.tensor_scalar(yp, yp, rstd[:, p:p + 1], nmr[:, p:p + 1], ALU.mult, ALU.add).then_inc(yd[0], 1)

        @block.scalar
        def _(act):
            act.activation(sd[:, :], var[:, :], ACT.Sqrt).then_inc(sdev, 1)
            act.wait_ge(nmrd, 1)
            for p in range(NP):
                if SHARE[p % 8] == 1:
                    yp = y[:, p * D:(p + 1) * D]
                    act.activation(yp, yp, ACT.Identity, bias=nmr[:, p:p + 1], scale=rstd[:, p:p + 1]).then_inc(yd[1], 1)

        @block.gpsimd
        def _(pool):
            pool.wait_ge(nmrd, 1)
            for p in range(NP):
                if SHARE[p % 8] == 2:
                    yp = y[:, p * D:(p + 1) * D]
                    pool.tensor_scalar(yp, yp, rstd[:, p:p + 1], nmr[:, p:p + 1], ALU.mult, ALU.add).then_inc(yd[2], 1)

        @block.sync
        def _(sp):
            rows = y[:, :].rearrange("r (p d) -> r p d", d=D)
            out = a["out"].rearrange("(p m) s d -> m s p d", m=2)
            for part in range(PARTS):
                p0, p1 = part * NP // PARTS, (part + 1) * NP // PARTS
                for k in range(3):
                    sp.wait_ge(yd[k], p1 // 8 * SHARE.count(k))
                for im in range(2):
                    sp.dma_start(out[im, 1:NPOS, p0:p1, :], rows[QPAD * im + 1:QPAD * im + NPOS, p0:p1, :]).then_inc(out_stored, 16)
                if part >= PARTS - 2:
                    c0 = p0 if part == PARTS - 1 else 0
                    for im in range(2):
                        sp.dma_start(out[im, 0:1, c0:p1, :], rows[QPAD * im:QPAD * im + 1, c0:p1, :]).then_inc(out_stored, 16)
            sp.wait_ge(out_stored, 16 * (2 * PARTS + 4))


def vit_layer(nc, a):
    with ExitStack() as ctx:
        def sb(name, shape, dt=F32):
            return ctx.enter_context(nc.sbuf_tensor(name, shape, dt))

        keep = {
            "h": sb("h", [P, NT * D]),
            "hT_hi": sb("hT_hi", [P, DC * NTOK], F32R),
            "hT_lo": sb("hT_lo", [P, DC * NTOK], F32R),
            "wqkv_hi": sb("wqkv_hi", [P, DC, 3 * D], F32R),
            "wqkv_lo": sb("wqkv_lo", [P, DC, 3 * D], F32R),
            "wo_hi": sb("wo_hi", [P, DC, D], F32R),
            "wo_lo": sb("wo_lo", [P, DC, D], F32R),
            "ident": sb("ident", [P, P]),
            "bias_col": sb("bias_col", [P, 12]),
            "ps": ctx.enter_context(nc.psum_tensor("ps", [P, 8 * 512], F32)),
        }
        keep["total"] = sb("total", [P, 2, D])
        keep["stored"] = [ctx.enter_context(nc.semaphore(f"stored{r}")) for r in range(2)]
        patch_tokens(nc, a, keep)
        with ExitStack() as inner:
            keep["attn"] = inner.enter_context(nc.sbuf_tensor("attn", [P, DC * NTOK], F32))
            keep["we_hi"] = inner.enter_context(nc.sbuf_tensor("we_hi", [P, DC, E * D], F32R))
            keep["we_lo"] = inner.enter_context(nc.sbuf_tensor("we_lo", [P, DC, E * D], F32R))
            keep["wg_raw"] = inner.enter_context(nc.sbuf_tensor("wg_raw", [P, DC, E], F32))
            keep["bg_row"] = inner.enter_context(nc.sbuf_tensor("bg_row", [P, E], F32))
            keep["be"] = inner.enter_context(nc.sbuf_tensor("be", [E, D], F32))
            attention(nc, a, keep, True)
            norm_and_experts(nc, a, keep)
        keep["y"] = sb("y", [P, B // 2 * D])
        keep["ymean"] = sb("ymean", [P, B // 2])
        keep["yvar"] = sb("yvar", [P, B // 2])
        attention(nc, a, keep, False)
        last_norm(nc, a, keep)


_INS = {"x": "x", "L0_tok_ln1_g": "ln1_g", "L0_tok_ln1_b": "ln1_b", "L0_tok_W_proj": "w_proj",
        "L0_tok_b_proj": "b_proj", "L0_tok_ln2_g": "ln2_g", "L0_tok_ln2_b": "ln2_b", "L0_tok_cls_token": "cls",
        "L0_tok_pos_emb": "pos", "L0_attn_Wq": "wq", "L0_attn_bq": "bq", "L0_attn_Wk": "wk", "L0_attn_bk": "bk",
        "L0_attn_Wv": "wv", "L0_attn_bv": "bv", "L0_attn_Wo": "wo", "L0_attn_bo": "bo", "L0_ffn_W_qkv": "w_qkv",
        "L0_ffn_b_qkv": "b_qkv", "L0_ffn_W_gate": "w_gate", "L0_ffn_b_gate": "b_gate",
        "L0_ffn_W_experts": "w_exp", "L0_ffn_b_experts": "b_exp"}


def kernel(**inputs):
    import numpy as _np
    import concourse.bacc as _bacc
    from concourse import mybir as _mybir
    from concourse.bass_utils import run_bass_kernel_spmd as _run

    nc = _bacc.Bacc("TRN2", target_bir_lowering=False, num_devices=1)
    arrays, args = {}, {}
    for name, short in _INS.items():
        arr = _np.ascontiguousarray(inputs[name])
        arrays[f"in_{name}_dram"] = arr
        args[short] = nc.dram_tensor(f"in_{name}_dram", arr.shape, _mybir.dt.from_np(arr.dtype),
                                     kind="ExternalInput").ap()
    args["out"] = nc.dram_tensor("out_0_dram", (B, NPOS, D), _mybir.dt.float32, kind="ExternalOutput").ap()
    args["left"] = nc.dram_tensor("left", (B, NPOS, D), _mybir.dt.float32, kind="Internal").ap()
    vit_layer(nc, args)
    r = _run(nc, [arrays], core_ids=[0])
    return r.results[0]["out_0_dram"]
```
